# Optimizing a Trainium2 kernel written in Bass

```python
import numpy as np
import jax
import jax.numpy as jnp

def _softmax(x, axis=-1):
    return jax.nn.softmax(x, axis=axis)

def _gelu(x):
    return jax.nn.gelu(x, approximate=True)

def _silu(x):
    return jax.nn.silu(x)

def _sigmoid(x):
    return jax.nn.sigmoid(x)

def _layernorm(x, axis=-1, eps=1e-05):
    m = jnp.mean(x, axis=axis, keepdims=True)
    v = jnp.var(x, axis=axis, keepdims=True)
    return (x - m) / jnp.sqrt(v + eps)

def _scatter_add(tgt, idx, src, axis=0):
    return tgt.at[idx].add(src)

def _segment_sum(src, seg, n):
    return jax.ops.segment_sum(src, seg, n)
kernel_name = 'mk_decoder_preln_d2_seqx_r8_809237'

def setup_inputs(seed: int=0):
    np.random.seed(seed)
    _w = jnp.asarray

    def _rec_inputs():
        import jax
        import jax.numpy as jnp
        _rk = jax.random.key(seed)
        x = 0.0003765 + 1 * jax.random.normal(jax.random.fold_in(_rk, 1), (16, 128, 256), jnp.float32)
        _lenS = 128 - jax.random.randint(jax.random.fold_in(_rk, 7), (16,), 0, max(1, 128 // 4) + 1, jnp.int32)
        _lenS2 = 128 - jax.random.randint(jax.random.fold_in(_rk, 8), (16,), 0, max(1, 128 // 4) + 1, jnp.int32)
        _ctx_2048P = jax.random.normal(jax.random.fold_in(_rk, 11), (16, 16, 256), jnp.float32)
        _ctx_2048c = jax.random.dirichlet(jax.random.fold_in(_rk, 511), 0.3 * jnp.ones((16,), jnp.float32), (16, 128))
        _ctx_2048t = jnp.einsum('bsk,bkd->bsd', _ctx_2048c, _ctx_2048P)
        _ctx_2048t = _ctx_2048t * jax.lax.rsqrt(jnp.mean(jnp.square(_ctx_2048t)) + 1e-12) * 0.953939
        ctx_2048 = -0.000292821 + 1.00034 * (_ctx_2048t + 0.3 * jax.random.normal(jax.random.fold_in(_rk, 611), (16, 128, 256), jnp.float32))
        _validS = jnp.arange(128)[None, :] < _lenS[:, None]
        _validS2 = jnp.arange(128)[None, :] < _lenS2[:, None]
        _causal = jnp.tril(jnp.ones((128, 128), dtype=bool))
        mask_BxS2_ff1 = jnp.where(jnp.ones((16, 128), dtype=bool), 1.0, 0.0).astype(jnp.float32)
        return (x, ctx_2048, mask_BxS2_ff1)
    x, ctx_2048, mask_BxS2_ff1 = _rec_inputs()

    def _L0_attn_setup():
        import jax, jax.numpy as jnp
        import numpy as np
        DIM = 256
        HEADS = 16
        HEAD_DIM = DIM // HEADS
        RANK = 16
        ALPHA = 8.0
        SCALING = ALPHA / RANK
        SCALE = HEAD_DIM ** (-0.5)

        def lora_linear(x, W, b, Bm, Am):
            out = jnp.einsum('bld,od->blo', x, W) + b
            upd = jnp.einsum('blr,or->blo', jnp.einsum('bld,rd->blr', x, Bm), Am)
            return out + SCALING * upd

        def _split(t):
            B, L, D = t.shape
            return t.reshape(B, L, HEADS, HEAD_DIM).transpose(0, 2, 1, 3)
        key = jax.random.key(seed)
        ks = jax.random.split(key, 20)
        B, L = (4, 256)
        x = jax.random.normal(ks[0], (B, L, DIM), dtype=jnp.float32)
        s = 0.02
        inp = {'x': x}
        for i, name in enumerate(['q', 'k', 'v', 'o']):
            inp[f'W{name}'] = jax.random.normal(ks[1 + 4 * i], (DIM, DIM), jnp.float32) * s
            inp[f'b{name}'] = jax.random.normal(ks[2 + 4 * i], (DIM,), jnp.float32) * s
            inp[f'B{name}'] = jax.random.normal(ks[3 + 4 * i], (RANK, DIM), jnp.float32) * s
            inp[f'A{name}'] = jax.random.uniform(ks[4 + 4 * i], (DIM, RANK), jnp.float32, -0.1, 0.1)
        return inp
    _L0_attn_all = _L0_attn_setup()
    _L0_attn_in = {k: v for k, v in _L0_attn_all.items() if k in ('Wq', 'bq', 'Bq', 'Aq', 'Wk', 'bk', 'Bk', 'Ak', 'Wv', 'bv', 'Bv', 'Av', 'Wo', 'bo', 'Bo', 'Ao')}
    del _L0_attn_all

    def _L0_xattn_setup():
        import jax, jax.numpy as jnp
        import numpy as np
        key = jax.random.key(seed)
        k1, k2, k3, k4, k5 = jax.random.split(key, 5)
        B, D_MODEL, L = (2, 128, 256)
        HEAD_DIM = 8
        H = D_MODEL // HEAD_DIM
        return {'k': jax.random.normal(k1, (B, D_MODEL, L), dtype=jnp.float32), 'v': jax.random.normal(k2, (B, D_MODEL, L), dtype=jnp.float32), 'q': jax.random.normal(k3, (B, D_MODEL, L), dtype=jnp.float32), 'ssm_kernel': jax.random.normal(k4, (H, L), dtype=jnp.float32), 'D': jax.random.normal(k5, (H,), dtype=jnp.float32), 'head_dim': HEAD_DIM}
    _L0_xattn_all = _L0_xattn_setup()
    _L0_xattn_in = {k: v for k, v in _L0_xattn_all.items() if k in ('ssm_kernel', 'D')}
    del _L0_xattn_all

    def _L0_ffn_setup():
        import jax, jax.numpy as jnp
        import numpy as np
        B_, S_, H_, O_ = (4, 256, 256, 256)
        E_, R_ = (8, 16)
        LORA_ALPHA = 16.0
        key = jax.random.key(seed)
        ks = jax.random.split(key, 5)
        x = jax.random.normal(ks[0], (B_, S_, H_), dtype=jnp.float32)
        W = jax.random.normal(ks[1], (O_, H_), dtype=jnp.float32) * 0.02
        gate_w = jax.random.normal(ks[2], (E_, H_), dtype=jnp.float32) * 0.02
        A = jax.random.normal(ks[3], (E_, R_, H_), dtype=jnp.float32) * 0.02
        B = jax.random.normal(ks[4], (E_, O_, R_), dtype=jnp.float32) * 0.02
        return {'x': x, 'W': W, 'gate_w': gate_w, 'A': A, 'B': B}
    _L0_ffn_all = _L0_ffn_setup()
    _L0_ffn_in = {k: v for k, v in _L0_ffn_all.items() if k in ('W', 'gate_w', 'A', 'B')}
    del _L0_ffn_all

    def _L1_attn_setup():
        import jax, jax.numpy as jnp
        import numpy as np
        key = jax.random.key(seed)
        ks = jax.random.split(key, 5)
        B, S, D = (1, 512, 256)
        H, Dh = (16, 128)
        scale = 1.0 / np.sqrt(D).astype(np.float32)
        return {'x': jax.random.normal(ks[0], (B, S, D), dtype=jnp.float32), 'W_K': jax.random.normal(ks[1], (H, Dh, D), dtype=jnp.float32) * scale, 'W_Q': jax.random.normal(ks[2], (H, Dh, D), dtype=jnp.float32) * scale, 'W_V': jax.random.normal(ks[3], (H, Dh, D), dtype=jnp.float32) * scale, 'W_O': jax.random.normal(ks[4], (D, H * Dh), dtype=jnp.float32) * scale}
    _L1_attn_all = _L1_attn_setup()
    _L1_attn_in = {k: v for k, v in _L1_attn_all.items() if k in ('W_K', 'W_Q', 'W_V', 'W_O')}
    del _L1_attn_all

    def _L1_xattn_setup():
        import jax, jax.numpy as jnp
        import numpy as np
        H = 256
        NH = 16
        HD = H // NH
        FD = 64
        key = jax.random.key(seed)
        ks = jax.random.split(key, 12)
        B, S = (4, 512)
        s = 1.0 / np.sqrt(H)
        sf = 1.0 / np.sqrt(HD)
        return {'query': jax.random.normal(ks[0], (B, S, H), jnp.float32), 'key': jax.random.normal(ks[1], (B, S, H), jnp.float32), 'value': jax.random.normal(ks[2], (B, S, H), jnp.float32), 'attention_mask': jnp.ones((B, S), jnp.float32), 'Wq': jax.random.normal(ks[3], (H, H), jnp.float32) * s, 'bq': jnp.zeros((H,), jnp.float32), 'Wk': jax.random.normal(ks[4], (H, H), jnp.float32) * s, 'bk': jnp.zeros((H,), jnp.float32), 'Wv': jax.random.normal(ks[5], (H, H), jnp.float32) * s, 'bv': jnp.zeros((H,), jnp.float32), 'Wqf': jax.random.normal(ks[6], (FD, HD), jnp.float32) * sf, 'Wkf': jax.random.normal(ks[7], (FD, HD), jnp.float32) * sf, 'Wo': jax.random.normal(ks[8], (H, H), jnp.float32) * s, 'bo': jnp.zeros((H,), jnp.float32)}
    _L1_xattn_all = _L1_xattn_setup()
    _L1_xattn_in = {k: v for k, v in _L1_xattn_all.items() if k in ('Wq', 'bq', 'Wk', 'bk', 'Wv', 'bv', 'Wqf', 'Wkf', 'Wo', 'bo')}
    del _L1_xattn_all

    def _L1_ffn_setup():
        import jax, jax.numpy as jnp
        import numpy as np
        B, T, C = (8, 256, 256)
        E, H = (32, 64)

        def _gating(hidden_states, sim_matrix, gates):
            seq_rep = jnp.mean(hidden_states, axis=1)
            sr_n = seq_rep / jnp.linalg.norm(seq_rep, axis=-1, keepdims=True)
            sm_n = sim_matrix / jnp.linalg.norm(sim_matrix, axis=0, keepdims=True)
            affinity = sr_n @ sm_n
            logits = affinity - jax.nn.sigmoid(gates)
            gated = jax.nn.relu(logits)
            mask = (gated > 0).astype(hidden_states.dtype)
            inactive = jnp.sum(mask, axis=1) == 0
            k_fb = E // 2
            _, fb_idx = jax.lax.top_k(logits, k_fb)
            fb_mask = jnp.sum(jax.nn.one_hot(fb_idx, E, dtype=mask.dtype), axis=1)
            mask = jnp.where(inactive[:, None], jnp.maximum(mask, fb_mask), mask)
            fallback_count = jnp.sum(inactive).astype(jnp.float32)
            neg = -jnp.finfo(hidden_states.dtype).max
            routing = jax.nn.softmax(jnp.where(mask > 0, gated, neg), axis=-1)
            return (routing, mask, fallback_count)
        key = jax.random.key(seed)
        ks = jax.random.split(key, 7)
        scale = 1.0 / np.sqrt(C)
        return {'hidden_states': jax.random.normal(ks[0], (B, T, C), dtype=jnp.float32), 'sim_matrix': jax.random.normal(ks[1], (C, E), dtype=jnp.float32), 'gates': jnp.zeros((E,), dtype=jnp.float32), 'w_q': jax.random.normal(ks[2], (E, H, C), dtype=jnp.float32) * scale, 'w_k': jax.random.normal(ks[3], (E, H, C), dtype=jnp.float32) * scale, 'w_v': jax.random.normal(ks[4], (E, H, C), dtype=jnp.float32) * scale, 'o_weights': jax.random.normal(ks[5], (E, H, C), dtype=jnp.float32)}
    _L1_ffn_all = _L1_ffn_setup()
    _L1_ffn_in = {k: v for k, v in _L1_ffn_all.items() if k in ('sim_matrix', 'gates', 'w_q', 'w_k', 'w_v', 'o_weights')}
    del _L1_ffn_all
    return {'x': x, 'ctx_2048': ctx_2048, 'mask_BxS2_ff1': mask_BxS2_ff1, 'L0_attn_Wq': _L0_attn_in['Wq'], 'L0_attn_bq': _L0_attn_in['bq'], 'L0_attn_Bq': _L0_attn_in['Bq'], 'L0_attn_Aq': _L0_attn_in['Aq'], 'L0_attn_Wk': _L0_attn_in['Wk'], 'L0_attn_bk': _L0_attn_in['bk'], 'L0_attn_Bk': _L0_attn_in['Bk'], 'L0_attn_Ak': _L0_attn_in['Ak'], 'L0_attn_Wv': _L0_attn_in['Wv'], 'L0_attn_bv': _L0_attn_in['bv'], 'L0_attn_Bv': _L0_attn_in['Bv'], 'L0_attn_Av': _L0_attn_in['Av'], 'L0_attn_Wo': _L0_attn_in['Wo'], 'L0_attn_bo': _L0_attn_in['bo'], 'L0_attn_Bo': _L0_attn_in['Bo'], 'L0_attn_Ao': _L0_attn_in['Ao'], 'L0_xattn_ssm_kernel': _L0_xattn_in['ssm_kernel'], 'L0_xattn_D': _L0_xattn_in['D'], 'L0_ffn_W': _L0_ffn_in['W'], 'L0_ffn_gate_w': _L0_ffn_in['gate_w'], 'L0_ffn_A': _L0_ffn_in['A'], 'L0_ffn_B': _L0_ffn_in['B'], 'L1_attn_W_K': _L1_attn_in['W_K'], 'L1_attn_W_Q': _L1_attn_in['W_Q'], 'L1_attn_W_V': _L1_attn_in['W_V'], 'L1_attn_W_O': _L1_attn_in['W_O'], 'L1_xattn_Wq': _L1_xattn_in['Wq'], 'L1_xattn_bq': _L1_xattn_in['bq'], 'L1_xattn_Wk': _L1_xattn_in['Wk'], 'L1_xattn_bk': _L1_xattn_in['bk'], 'L1_xattn_Wv': _L1_xattn_in['Wv'], 'L1_xattn_bv': _L1_xattn_in['bv'], 'L1_xattn_Wqf': _L1_xattn_in['Wqf'], 'L1_xattn_Wkf': _L1_xattn_in['Wkf'], 'L1_xattn_Wo': _L1_xattn_in['Wo'], 'L1_xattn_bo': _L1_xattn_in['bo'], 'L1_ffn_sim_matrix': _L1_ffn_in['sim_matrix'], 'L1_ffn_gates': _L1_ffn_in['gates'], 'L1_ffn_w_q': _L1_ffn_in['w_q'], 'L1_ffn_w_k': _L1_ffn_in['w_k'], 'L1_ffn_w_v': _L1_ffn_in['w_v'], 'L1_ffn_o_weights': _L1_ffn_in['o_weights']}

def reference(x, ctx_2048, mask_BxS2_ff1, L0_attn_Wq, L0_attn_bq, L0_attn_Bq, L0_attn_Aq, L0_attn_Wk, L0_attn_bk, L0_attn_Bk, L0_attn_Ak, L0_attn_Wv, L0_attn_bv, L0_attn_Bv, L0_attn_Av, L0_attn_Wo, L0_attn_bo, L0_attn_Bo, L0_attn_Ao, L0_xattn_ssm_kernel, L0_xattn_D, L0_ffn_W, L0_ffn_gate_w, L0_ffn_A, L0_ffn_B, L1_attn_W_K, L1_attn_W_Q, L1_attn_W_V, L1_attn_W_O, L1_xattn_Wq, L1_xattn_bq, L1_xattn_Wk, L1_xattn_bk, L1_xattn_Wv, L1_xattn_bv, L1_xattn_Wqf, L1_xattn_Wkf, L1_xattn_Wo, L1_xattn_bo, L1_ffn_sim_matrix, L1_ffn_gates, L1_ffn_w_q, L1_ffn_w_k, L1_ffn_w_v, L1_ffn_o_weights):
    import jax
    import jax.numpy as jnp

    def _L0_attn_ref(x, Wq, bq, Bq, Aq, Wk, bk, Bk, Ak, Wv, bv, Bv, Av, Wo, bo, Bo, Ao):
        import jax, jax.numpy as jnp
        import numpy as np
        DIM = 256
        HEADS = 16
        HEAD_DIM = DIM // HEADS
        RANK = 16
        ALPHA = 8.0
        SCALING = ALPHA / RANK
        SCALE = HEAD_DIM ** (-0.5)

        def lora_linear(x, W, b, Bm, Am):
            out = jnp.einsum('bld,od->blo', x, W) + b
            upd = jnp.einsum('blr,or->blo', jnp.einsum('bld,rd->blr', x, Bm), Am)
            return out + SCALING * upd

        def _split(t):
            B, L, D = t.shape
            return t.reshape(B, L, HEADS, HEAD_DIM).transpose(0, 2, 1, 3)
        q = _split(lora_linear(x, Wq, bq, Bq, Aq))
        k = _split(lora_linear(x, Wk, bk, Bk, Ak))
        v = _split(lora_linear(x, Wv, bv, Bv, Av))
        scores = jnp.einsum('bhqd,bhkd->bhqk', q, k) * SCALE
        attn = jax.nn.softmax(scores, axis=-1)
        out = jnp.einsum('bhqk,bhkd->bhqd', attn, v)
        B, H, L, hd = out.shape
        out = out.transpose(0, 2, 1, 3).reshape(B, L, H * hd)
        return lora_linear(out, Wo, bo, Bo, Ao)

    def _L0_xattn_ref(k, v, q, ssm_kernel, D, head_dim):
        import jax, jax.numpy as jnp
        import numpy as np
        B, HD, L = k.shape
        H = HD // head_dim
        fft_size = 2 * L
        k_ = k.reshape(B, H, head_dim, L)
        v_ = v.reshape(B, H, head_dim, L)
        q_ = q.reshape(B, H, head_dim, L)
        kv = jnp.einsum('bhil,bhjl->bijhl', k_, v_)
        kv_f = jnp.fft.rfft(kv, n=fft_size)
        kernel_f = jnp.fft.rfft(ssm_kernel, n=fft_size)
        y = jnp.fft.irfft(kv_f * kernel_f, n=fft_size)[..., :L]
        out = y + kv * D[None, None, None, :, None]
        out = jnp.einsum('bijhl,bhil->bjhl', out, q_)
        out = jnp.transpose(out, (0, 2, 1, 3)).reshape(B, H * head_dim, L)
        return out.astype(k.dtype)

    def _L0_ffn_ref(x, W, gate_w, A, B):
        import jax, jax.numpy as jnp
        import numpy as np
        B_, S_, H_, O_ = (4, 256, 256, 256)
        E_, R_ = (8, 16)
        LORA_ALPHA = 16.0
        bsz, seq, hid = x.shape
        E = gate_w.shape[0]
        x_flat = x.reshape(-1, hid)
        out = x_flat @ W.T
        logits = x_flat @ gate_w.T
        probs = jax.nn.softmax(logits, axis=-1)
        topk_w, topk_idx = jax.lax.top_k(probs, 2)
        topk_w = topk_w / jnp.sum(topk_w, axis=-1, keepdims=True)
        onehot = jax.nn.one_hot(topk_idx, E, dtype=x.dtype)
        wmat = jnp.einsum('tk,tke->te', topk_w, onehot) * LORA_ALPHA
        h = jnp.einsum('th,erh->etr', x_flat, A)
        hw = h * wmat.T[:, :, None]
        lora = jnp.einsum('etr,eor->to', hw, B)
        return (out + lora).reshape(bsz, seq, -1)

    def _L1_attn_ref(x, W_K, W_Q, W_V, W_O):
        import jax, jax.numpy as jnp
        import numpy as np
        b, pos, d_model = x.shape
        d_head = W_K.shape[1]
        k = jnp.einsum('ihd,bpd->biph', W_K, x)
        q = jnp.einsum('ihd,bpd->biph', W_Q, x)
        v = jnp.einsum('ihd,bpd->biph', W_V, x)
        scores = jnp.einsum('biph,biqh->biqp', k, q)
        mask = jnp.tril(jnp.ones((pos, pos), dtype=x.dtype))
        masked = scores * mask - jnp.float32(10000000000.0) * (1.0 - mask)
        attn = jax.nn.softmax(masked / jnp.sqrt(jnp.float32(d_head)), axis=-1)
        z = jnp.einsum('biqp,biph->biqh', attn, v)
        z_flat = jnp.transpose(z, (0, 2, 1, 3)).reshape(b, pos, -1)
        out = jnp.einsum('df,bqf->bqd', W_O, z_flat)
        return out

    def _L1_xattn_ref(query, key, value, attention_mask, Wq, bq, Wk, bk, Wv, bv, Wqf, Wkf, Wo, bo):
        import jax, jax.numpy as jnp
        import numpy as np
        H = 256
        NH = 16
        HD = H // NH
        FD = 64
        B, Sq, _ = query.shape
        Sk = key.shape[1]

        def heads(x, W, b, S):
            return (x @ W.T + b).reshape(B, S, NH, HD).transpose(0, 2, 1, 3)
        q = heads(query, Wq, bq, Sq)
        k = heads(key, Wk, bk, Sk)
        v = heads(value, Wv, bv, Sk)
        q_prime = jax.nn.relu(jnp.einsum('bhnd,fd->bhnf', q, Wqf))
        k_prime = jax.nn.relu(jnp.einsum('bhnd,fd->bhnf', k, Wkf))
        k_prime = k_prime * attention_mask[:, None, :, None]
        kv = jnp.einsum('bhnf,bhne->bhfe', k_prime, v)
        qkv = jnp.einsum('bhmf,bhfe->bhme', q_prime, kv)
        k_sum = jnp.sum(k_prime, axis=2)
        qk_sum = jnp.einsum('bhmf,bhf->bhm', q_prime, k_sum)[..., None]
        out = qkv / (qk_sum + 1e-08)
        out = out.transpose(0, 2, 1, 3).reshape(B, Sq, H)
        return out @ Wo.T + bo

    def _L1_ffn_ref(hidden_states, sim_matrix, gates, w_q, w_k, w_v, o_weights):
        import jax, jax.numpy as jnp
        import numpy as np
        B, T, C = (8, 256, 256)
        E, H = (32, 64)

        def _gating(hidden_states, sim_matrix, gates):
            seq_rep = jnp.mean(hidden_states, axis=1)
            sr_n = seq_rep / jnp.linalg.norm(seq_rep, axis=-1, keepdims=True)
            sm_n = sim_matrix / jnp.linalg.norm(sim_matrix, axis=0, keepdims=True)
            affinity = sr_n @ sm_n
            logits = affinity - jax.nn.sigmoid(gates)
            gated = jax.nn.relu(logits)
            mask = (gated > 0).astype(hidden_states.dtype)
            inactive = jnp.sum(mask, axis=1) == 0
            k_fb = E // 2
            _, fb_idx = jax.lax.top_k(logits, k_fb)
            fb_mask = jnp.sum(jax.nn.one_hot(fb_idx, E, dtype=mask.dtype), axis=1)
            mask = jnp.where(inactive[:, None], jnp.maximum(mask, fb_mask), mask)
            fallback_count = jnp.sum(inactive).astype(jnp.float32)
            neg = -jnp.finfo(hidden_states.dtype).max
            routing = jax.nn.softmax(jnp.where(mask > 0, gated, neg), axis=-1)
            return (routing, mask, fallback_count)
        routing, mask, fallback_count = _gating(hidden_states, sim_matrix, gates)
        v_all = jnp.einsum('btc,ehc->bteh', hidden_states, w_v)
        full_expert_outputs = v_all * mask[:, None, :, None]
        combined = jnp.einsum('be,bteh->bth', routing, full_expert_outputs)
        w_o_dyn = jnp.einsum('be,ehd->bhd', routing, o_weights)
        final_output = jnp.einsum('bth,bhd->btd', combined, w_o_dyn)
        return final_output
    x = x + _L0_attn_ref(_layernorm(x, axis=-1), L0_attn_Wq, L0_attn_bq, L0_attn_Bq, L0_attn_Aq, L0_attn_Wk, L0_attn_bk, L0_attn_Bk, L0_attn_Ak, L0_attn_Wv, L0_attn_bv, L0_attn_Bv, L0_attn_Av, L0_attn_Wo, L0_attn_bo, L0_attn_Bo, L0_attn_Ao)
    x = x + _L0_xattn_ref(ctx_2048, ctx_2048, _layernorm(x, axis=-1), L0_xattn_ssm_kernel, L0_xattn_D, 8)
    x = x + _L0_ffn_ref(_layernorm(x, axis=-1), L0_ffn_W, L0_ffn_gate_w, L0_ffn_A, L0_ffn_B)
    x = x + _L1_attn_ref(_layernorm(x, axis=-1), L1_attn_W_K, L1_attn_W_Q, L1_attn_W_V, L1_attn_W_O)
    x = x + _L1_xattn_ref(_layernorm(x, axis=-1), ctx_2048, ctx_2048, mask_BxS2_ff1, L1_xattn_Wq, L1_xattn_bq, L1_xattn_Wk, L1_xattn_bk, L1_xattn_Wv, L1_xattn_bv, L1_xattn_Wqf, L1_xattn_Wkf, L1_xattn_Wo, L1_xattn_bo)
    x = x + _L1_ffn_ref(_layernorm(x, axis=-1), L1_ffn_sim_matrix, L1_ffn_gates, L1_ffn_w_q, L1_ffn_w_k, L1_ffn_w_v, L1_ffn_o_weights)
    return x

_drawn_inputs = setup_inputs


def setup_inputs(seed=0):
    import zlib

    import numpy as np

    out = dict(_drawn_inputs(seed))
    spreads = {'L1_xattn_bq': (0.0, 0.8),
     'L1_xattn_bk': (0.0, 0.8),
     'L1_xattn_bv': (0.0, 0.8),
     'L1_xattn_bo': (0.0, 0.8),
     'L1_ffn_gates': (0.0, 0.8)}
    factors = {'L0_attn_Wq': 8.0,
     'L0_attn_bq': 8.0,
     'L0_attn_Bq': 8.0,
     'L0_attn_Aq': 8.0,
     'L0_attn_Wk': 8.0,
     'L0_attn_bk': 8.0,
     'L0_attn_Bk': 8.0,
     'L0_attn_Ak': 8.0,
     'L0_attn_Wv': 3.375,
     'L0_attn_bv': 4.88,
     'L0_attn_Bv': 8.0,
     'L0_attn_Av': 8.0,
     'L0_attn_Wo': 2.856,
     'L0_attn_Bo': 8.0,
     'L0_attn_Ao': 8.0,
     'L0_ffn_W': 6.549,
     'L0_ffn_gate_w': 8.0,
     'L0_ffn_A': 7.24,
     'L0_ffn_B': 7.255,
     'L1_attn_W_K': 3.598,
     'L1_attn_W_Q': 3.597,
     'L1_xattn_Wq': 8.0,
     'L1_xattn_Wk': 8.0,
     'L1_xattn_Wv': 3.91,
     'L1_xattn_Wqf': 8.0,
     'L1_xattn_Wkf': 8.0,
     'L1_xattn_Wo': 3.886,
     'L1_ffn_sim_matrix': 5.104,
     'L1_ffn_w_v': 4.253,
     'L1_ffn_o_weights': 4.248}
    for name, (base, spread) in spreads.items():
        noise = np.random.default_rng([zlib.crc32(name.encode()), seed]).standard_normal(out[name].shape)
        drawn = base * np.exp(spread * noise) if base else spread * noise
        out[name] = jnp.asarray(drawn.astype(out[name].dtype))
    for name, factor in factors.items():
        out[name] = (out[name] * factor).astype(out[name].dtype)
    return out
```

```python
from contextlib import ExitStack

import concourse.bass as bass
from concourse import mybir

F32 = mybir.dt.float32
F32R = mybir.dt.float32r
BF16 = mybir.dt.bfloat16
ALU = mybir.AluOpType
ACT = mybir.ActivationFunctionType
AX = mybir.AxisListType.X

P = 128
NB = 16
G = 4
NG = NB // G
D = 256
DC = D // P
GT = G * P
EPS = 1e-5
ONE = 1


class Chain:

    def __init__(self, eng, sem, it, per):
        self.eng, self.sem, self.it, self.per, self.n = eng, sem, it, per, 0

    def done(self, ins):
        self.n += 1
        ins.then_inc(self.sem, 1)
        self.eng.wait_ge(self.sem, self.it * self.per + self.n)

    def close(self):
        assert self.n == self.per, (self.n, self.per)


def product(nc, out, a, b, start, stop):
    nc.tensor.matmul(out, a[0], b[0], start=start, stop=False, skip_group_check=True)
    nc.tensor.matmul(out, a[0], b[1], start=False, stop=False, skip_group_check=True)
    return nc.tensor.matmul(out, a[1], b[0], start=False, stop=stop, skip_group_check=True)


def pair(t, *index):
    return t[0][index], t[1][index]


class Program:
    def __init__(self, nc, io):
        self.nc, self.io = nc, io
        self.sems = []

    def sem(self, name):
        self.sems.append(self.nc.alloc_semaphore(name=name))
        return self.sems[-1]

    def release_semaphores(self):
        self.nc.clear_and_free_semaphores(self.sems)
        self.nc.all_engine_barrier()
        self.sems = []


class Norm:

    def __init__(self, pr, ctx, st, banks, name, split=True):
        nc = pr.nc
        self.nc, self.pr, self.banks, self.split = nc, pr, banks, split
        sb = lambda n, shape, dt: ctx.enter_context(nc.sbuf_tensor(f"{name}_{n}", shape, dt))
        self.stats = sb("stats", [P, G, 6], F32)
        self.meanvar = sb("meanvar", [P, G, 2], F32)
        self.rstd = sb("rstd", [P, G], F32)
        self.xn = sb("xn", [P, G, D], F32)
        if split:
            self.xT = (sb("xT_hi", [P, DC, GT], F32R), sb("xT_lo", [P, DC, GT], F32R))
        else:
            self.xT = sb("xT", [P, DC, GT], F32)
        self.s_chain = pr.sem(f"{name}_norm_chain")
        self.s_var = pr.sem(f"{name}_var_ready")
        self.s_pool = pr.sem(f"{name}_rstd_ready")
        self.s_xn = pr.sem(f"{name}_xn_ready")
        self.s_tr = pr.sem(f"{name}_xT_in_psum")
        self.s_hi = pr.sem(f"{name}_xT_hi_ready")
        self.s_lo = pr.sem(f"{name}_xT_ready")

    def vector_norm(self, dve, it):
        nc, x = self.nc, self.pr.x
        chain = Chain(dve, self.s_chain, it, 2)
        for j in range(G):
            last = nc.vector.bn_stats(self.stats[:, j, :], x[:, it * G + j, :])
        chain.done(last)
        nc.vector.memset(self.pr.wait_slot[:], 0.0)
        for j in range(G):
            last = nc.vector.bn_aggr(self.meanvar[:, j, :], self.stats[:, j, :])
        chain.done(last)
        chain.close()
        nc.vector.tensor_scalar(self.rstd[:], self.meanvar[:, :, 1], EPS, None, ALU.add).then_inc(self.s_var, 1)
        dve.wait_ge(self.s_pool, it + 1)
        for j in range(G):
            last = nc.vector.tensor_scalar(self.xn[:, j, :], x[:, it * G + j, :], self.meanvar[:, j, 0:1],
                                           self.rstd[:, j:j + 1], ALU.subtract, ALU.mult)
        last.then_inc(self.s_xn, 1)

    def pool_rstd(self, pool, it):
        pool.wait_ge(self.s_var, it + 1)
        self.nc.gpsimd.tensor_tensor(self.rstd[:], self.rstd[:], self.pr.minus_half[:], ALU.pow)\
            .then_inc(self.s_pool, 1)

    def tensor_transpose(self, pe, it):
        pe.wait_ge(self.s_xn, it + 1)
        for c in range(DC):
            for j in range(G):
                last = self.nc.tensor.transpose(self.banks[c][:, j * P:(j + 1) * P],
                                                self.xn[:, j, c * P:(c + 1) * P], self.pr.ident[:])
            last.then_inc(self.s_tr, 1)

    def scalar_hi(self, act, it):
        for c in range(DC):
            act.wait_ge(self.s_tr, it * DC + c + 1)
            out = self.xT[0] if self.split else self.xT
            self.nc.scalar.copy(out[:, c, :], self.banks[c][:, :]).then_inc(self.s_hi, 1)

    def vector_lo(self, dve, it):
        for c in range(DC):
            dve.wait_ge(self.s_hi, it * DC + c + 1)
            self.nc.vector.tensor_tensor(self.xT[1][:, c, :], self.banks[c][:, :],
                                         self.xT[0][:, c, :].bitcast(F32), ALU.subtract).then_inc(self.s_lo, 1)


def stage_lora_attention(pr):
    nc, io, x, banks = pr.nc, pr.io, pr.x, pr.banks
    H, HD, R = 16, 16, 16
    RG = 4
    U = G * RG
    LORA = 0.5
    SCALE = HD ** -0.5
    b_p, b_s, b_t, b_v = banks[0:2], banks[2:6], banks[6], banks[7]
    with ExitStack() as ctx:
        sb = lambda n, shape, dt=F32: ctx.enter_context(nc.sbuf_tensor(f"la_{n}", shape, dt))
        sem = lambda n: pr.sem(f"la_{n}")
        norm = Norm(pr, ctx, None, b_p, "la")
        w_raw = sb("w_raw", [P, 4, DC, D])
        lora_a = sb("lora_a", [R, 4, D])
        lora_b = sb("lora_b", [R, 4, D])
        w = (sb("w_hi", [P, 4, DC, D], F32R), sb("w_lo", [P, 4, DC, D], F32R))
        qk_bias = sb("qk_bias", [P, 2, DC])
        v_bias = sb("v_bias", [1, 2, D])
        row_bias = (sb("row_bias_hi", [1, 2, D], F32R), sb("row_bias_lo", [1, 2, D], F32R))
        parity = sb("parity", [P, 2])
        q = sb("q", [P, 2, DC, GT])
        k = sb("k", [P, DC, GT])
        DIAG = P + HD
        v_flat = sb("v", [P, G * H * P + P])
        v = v_flat[:, 0:G * H * P].rearrange("p (j h d) -> p j h d", j=G, h=H)
        negmax = sb("negmax", [P, 2, 4])
        sums = sb("sums", [P, 2, H])
        rsum = sb("rsum", [P, 2, H])
        prob = sb("prob", [P, 2, 4, P])
        probT = sb("probT", [P, 2, 4, P])
        o = sb("o", [P, 2, D])
        oT = (sb("oT_hi", [P, 2, DC, P], F32R), sb("oT_lo", [P, 2, DC, P], F32R))

        loaded = sem("weights_loaded")
        w_ps, w_f32, w_hi, w_lo = sem("w_in_psum"), sem("w_f32"), sem("w_hi"), sem("w_ready")
        q_ps, q_ok = sem("q_in_psum"), sem("q_ready")
        k_ps, k_ok = sem("k_in_psum"), sem("k_ready")
        v_ps, v_ok = sem("v_in_psum"), sem("v_ready")
        s_ps, max_ok, exp_ok = sem("scores_in_psum"), sem("negmax_ready"), sem("probs_ready")
        t_ps, t_ok = sem("probsT_in_psum"), sem("probsT_ready")
        av_ps, av_ok = sem("av_in_psum"), sem("o_ready")
        ot_ps, ot_hi, ot_lo = sem("oT_in_psum"), sem("oT_hi_ready"), sem("oT_ready")
        o_ps, x_ok = sem("out_in_psum"), sem("x_updated")
        chain_s = sem("vector_chain")
        v_zero = sem("v_cleared")
        NLOAD = 7
        block = ctx.enter_context(nc.Block())

        def head(r, s):
            return (s // 2) * 8 + 2 * r + s % 2

        @block.sync
        def _(sp):
            sp.dma_start(w_raw[:], io["l0_w"]).then_inc(loaded, 16)
            sp.dma_start(lora_a[:], io["l0_a"]).then_inc(loaded, 16)
            sp.dma_start(lora_b[:], io["l0_b"]).then_inc(loaded, 16)
            sp.dma_start(qk_bias[:], io["l0_qk_bias"]).then_inc(loaded, 16)
            sp.dma_start(v_bias[:], io["l0_vo_bias"]).then_inc(loaded, 16)
            sp.dma_start(parity[:], io["parity"]).then_inc(loaded, 16)
            sp.dma_start(pr.ident[:], io["ident"]).then_inc(loaded, 16)
            for t in range(NG):
                sp.dma_start(x[:, t * G:(t + 1) * G, :],
                             io["x"][t * G:(t + 1) * G].rearrange("b t d -> t b d")).then_inc(pr.x_loaded, 16)

        @block.gpsimd
        def _(pool):
            nc.gpsimd.memset(pr.minus_half[:], -0.5).then_inc(pr.const_ok, 1)
            nc.gpsimd.memset(pr.ones_row32[:], 1.0).then_inc(pr.const_ok, 1)
            nc.gpsimd.memset(v_flat[:], 0.0).then_inc(v_zero, 1)
            pool.wait_ge(pr.const_ok, 2)
            nc.gpsimd.tensor_copy(pr.ones_row[:], pr.ones_row32[:]).then_inc(pr.const_ok, 1)
            with pool.Fori(0, NG) as it:
                norm.pool_rstd(pool, it)

        @block.tensor
        def _(pe):
            pe.wait_ge(loaded, 16 * NLOAD)
            pe.wait_ge(pr.const_ok, 3)
            for n in range(4):
                if n >= 2:
                    pe.wait_ge(w_f32, n - 1)
                for c in range(DC):
                    last = nc.tensor.matmul(b_p[n % 2][:, c * D:(c + 1) * D], lora_b[:, n, c * P:(c + 1) * P],
                                            lora_a[:, n, :], start=True, stop=True)
                last.then_inc(w_ps, 1)
            pe.wait_ge(w_f32, 4)
            pe.wait_ge(w_lo, 2)
            with pe.Fori(0, NG) as it:
                pe.wait_ge(x_ok, ONE + it * G)
                norm.tensor_transpose(pe, it)
                pe.wait_ge(norm.s_lo, it * DC + DC)
                xT = norm.xT
                for n, (ps, free) in enumerate(((q_ps, None), (k_ps, q_ok))):
                    for m in range(DC):
                        if free is not None:
                            pe.wait_ge(free, it * DC + m + 1)
                        for c in range(DC):
                            last = product(nc, b_p[m][:, :], pair(w, slice(None), n, c, slice(m * P, m * P + P)),
                                           pair(xT, slice(None), c), c == 0, c == DC - 1)
                        last.then_inc(ps, 1)
                for half in range(2):
                    pe.wait_ge(k_ok, it * DC + half + 1)
                    for jj in range(2):
                        j = 2 * half + jj
                        out = b_p[half][:, jj * D:(jj + 1) * D]
                        nc.tensor.matmul(out, pr.ones_row[:], row_bias[0][:, 0, :], start=True, stop=False,
                                         skip_group_check=True)
                        nc.tensor.matmul(out, pr.ones_row[:], row_bias[1][:, 0, :], start=False, stop=False,
                                         skip_group_check=True)
                        for c in range(DC):
                            last = product(nc, out, pair(xT, slice(None), c, slice(j * P, j * P + P)),
                                           pair(w, slice(None), 2, c), False, c == DC - 1)
                    last.then_inc(v_ps, 1)

                def scores(u):
                    for s in range(4):
                        for d in range(2):
                            j, r = divmod(u + d, RG)
                            if s == 0:
                                pe.wait_ge(exp_ok, ONE + it * U + max(0, u + d - RG + 1))
                            rows = slice(32 * r, 32 * r + 32)
                            m, e = divmod(s, 2)
                            last = nc.tensor.matmul(b_s[r][:, s * P:(s + 1) * P],
                                                    q[rows, e, m, j * P:(j + 1) * P],
                                                    k[rows, m, j * P:(j + 1) * P], start=True, stop=True)
                            if s == 3:
                                last.then_inc(s_ps, 1)

                def turn(u):
                    pe.wait_ge(exp_ok, ONE + it * U + u + 1)
                    pe.wait_ge(t_ok, ONE + it * U + u)
                    for s in range(4):
                        last = nc.tensor.transpose(b_t[:, s * P:(s + 1) * P], prob[:, u % 2, s, :], pr.ident[:])
                    last.then_inc(t_ps, 1)

                def weigh(u):
                    j, r = divmod(u, RG)
                    pe.wait_ge(t_ok, ONE + it * U + u + 1)
                    if r == 0:
                        pe.wait_ge(av_ok, ONE + it * G + j)
                    for s in range(4):
                        last = nc.tensor.matmul(b_v[:, s // 2 * P:(s // 2 + 1) * P], probT[:, u % 2, s, :],
                                                v[:, j, head(r, s), :], start=(r == 0 and s == 0),
                                                stop=(r == RG - 1), skip_group_check=True)
                    last.then_inc(av_ps, 1)

                def turn_o(j):
                    pe.wait_ge(av_ok, ONE + it * G + j + 1)
                    if j >= 1:
                        pe.wait_ge(ot_lo, it * G + j)
                    for c in range(DC):
                        last = nc.tensor.transpose(b_p[0][:, c * P:(c + 1) * P], o[:, j % 2, c * P:(c + 1) * P],
                                                   pr.ident[:])
                    last.then_inc(ot_ps, 1)

                def project(j):
                    pe.wait_ge(ot_lo, it * G + j + 1)
                    if j >= 1:
                        pe.wait_ge(x_ok, ONE + it * G + j)
                    out = b_p[1][:, 0:D]
                    nc.tensor.matmul(out, pr.ones_row[:], row_bias[0][:, 1, :], start=True, stop=False,
                                     skip_group_check=True)
                    nc.tensor.matmul(out, pr.ones_row[:], row_bias[1][:, 1, :], start=False, stop=False,
                                     skip_group_check=True)
                    for c in range(DC):
                        last = product(nc, out, pair(oT, slice(None), j % 2, c), pair(w, slice(None), 3, c),
                                       False, c == DC - 1)
                    last.then_inc(o_ps, 1)

                pe.wait_ge(q_ok, it * DC + DC)
                pe.wait_ge(k_ok, it * DC + DC)
                pe.wait_ge(v_ok, it * 2 + 2)
                scores(0)
                for u in range(U + 3):
                    if u < U:
                        turn(u)
                    if 1 <= u <= U:
                        weigh(u - 1)
                    if u % 2 == 0 and u + 2 < U:
                        scores(u + 2)
                    if u >= 5 and (u - 5) % 4 == 0:
                        turn_o((u - 5) // 4)
                    if u >= 6 and (u - 6) % 4 == 0:
                        project((u - 6) // 4)

        @block.scalar
        def _(act):
            act.wait_ge(loaded, 16 * NLOAD)
            nc.scalar.copy(row_bias[0][:], v_bias[:]).then_inc(w_hi, 1)
            act.wait_ge(w_f32, 4)
            nc.scalar.copy(w[0][:], w_raw[:]).then_inc(w_hi, 1)
            act.sem_inc(exp_ok, ONE)
            act.wait_ge(v_zero, 1)
            with act.Fori(0, NG) as it:
                norm.scalar_hi(act, it)
                for m in range(DC):
                    act.wait_ge(k_ps, it * DC + m + 1)
                    nc.scalar.activation(k[:, m, :], b_p[m][:, :], ACT.Identity,
                                         bias=qk_bias[:, 1, m:m + 1]).then_inc(k_ok, 1)
                for half in range(2):
                    act.wait_ge(v_ps, it * 2 + half + 1)
                    for jj in range(2):
                        for m in range(DC):
                            at = ((2 * half + jj) * H + 8 * m) * P
                            src = b_p[half][:, jj * D + m * P:jj * D + m * P + P]
                            last = nc.scalar.copy(
                                v_flat[:, at:at + 8 * DIAG].rearrange("p (h s) -> p h s", s=DIAG)[:, :, 0:HD],
                                src.rearrange("p (h d) -> p h d", d=HD))
                    last.then_inc(v_ok, 1)

                def exps(u):
                    j, r = divmod(u, RG)
                    act.wait_ge(max_ok, it * U + u + 1)
                    if u >= 2:
                        act.wait_ge(t_ps, it * U + u - 1)
                    if r == 0 and j >= 2:
                        act.wait_ge(av_ok, ONE + it * G + j - 1)
                    for s in range(4):
                        h = head(r, s)
                        last = nc.scalar.activation(prob[:, u % 2, s, :], b_s[r][:, s * P:(s + 1) * P], ACT.Exp,
                                                    bias=negmax[:, u % 2, s:s + 1], scale=SCALE,
                                                    accum_out=sums[:, j % 2, h:h + 1])
                    last.then_inc(exp_ok, 1)

                for u in range(U + 3):
                    if u < U:
                        exps(u)
                    if u >= 5 and (u - 5) % 4 == 0:
                        j = (u - 5) // 4
                        act.wait_ge(ot_ps, it * G + j + 1)
                        nc.scalar.copy(oT[0][:, j % 2, :, :],
                                       b_p[0][:, 0:D].rearrange("p (c t) -> p c t", c=DC)).then_inc(ot_hi, 1)

        @block.vector
        def _(dve):
            dve.wait_ge(loaded, 16 * NLOAD)
            for n in range(4):
                dve.wait_ge(w_ps, n + 1)
                nc.vector.scalar_tensor_tensor(w_raw[:, n], b_p[n % 2][:, :].rearrange("p (c o) -> p c o", c=DC),
                                               LORA, w_raw[:, n], ALU.mult, ALU.add).then_inc(w_f32, 1)
            dve.wait_ge(w_hi, 1)
            nc.vector.tensor_tensor(row_bias[1][:], v_bias[:], row_bias[0][:].bitcast(F32), ALU.subtract)\
                .then_inc(w_lo, 1)
            dve.wait_ge(w_hi, 2)
            nc.vector.tensor_tensor(w[1][:], w_raw[:], w[0][:].bitcast(F32), ALU.subtract).then_inc(w_lo, 1)
            dve.wait_ge(pr.x_loaded, 16 * NG)
            for event in (t_ok, av_ok, x_ok):
                dve.sem_inc(event, ONE)
            with dve.Fori(0, NG) as it:
                norm.vector_norm(dve, it)
                norm.vector_lo(dve, it)
                chain = Chain(dve, chain_s, it, U + G)
                for m in range(DC):
                    dve.wait_ge(q_ps, it * DC + m + 1)
                    for e in range(2):
                        last = nc.vector.tensor_scalar(q[:, e, m, :], b_p[m][:, :], qk_bias[:, 0, m:m + 1],
                                                       parity[:, e:e + 1], ALU.add, ALU.mult)
                    last.then_inc(q_ok, 1)

                def row_max(u):
                    dve.wait_ge(s_ps, it * U + u + 1)
                    if u >= 2:
                        dve.wait_ge(exp_ok, ONE + it * U + u - 1)
                    chain.done(nc.vector.tensor_reduce(
                        negmax[:, u % 2, :], b_s[u % RG][:, :].rearrange("p (s k) -> p s k", s=4), AX, ALU.max))
                    nc.vector.tensor_scalar(negmax[:, u % 2, :], negmax[:, u % 2, :], -SCALE, None, ALU.mult)\
                        .then_inc(max_ok, 1)

                def keep_probT(u):
                    dve.wait_ge(t_ps, it * U + u + 1)
                    if u >= 2:
                        dve.wait_ge(av_ps, it * U + u - 1)
                    nc.vector.tensor_copy(probT[:, u % 2, :, :], b_t[:, :].rearrange("p (s k) -> p s k", s=4))\
                        .then_inc(t_ok, 1)

                def normalise(j):
                    dve.wait_ge(exp_ok, ONE + it * U + (j + 1) * RG)
                    chain.done(nc.vector.reciprocal(rsum[:, j % 2, :], sums[:, j % 2, :]))
                    dve.wait_ge(av_ps, it * U + (j + 1) * RG)
                    if j >= 2:
                        dve.wait_ge(ot_ps, it * G + j - 1)
                    nc.vector.tensor_tensor(o[:, j % 2, :].rearrange("p (h d) -> p h d", h=H),
                                            b_v[:, 0:D].rearrange("p (h d) -> p h d", h=H),
                                            rsum[:, j % 2, :].unsqueeze(2).to_broadcast([P, H, HD]), ALU.mult)\
                        .then_inc(av_ok, 1)

                row_max(0)
                for u in range(U + 3):
                    if u + 1 < U:
                        row_max(u + 1)
                    if u < U:
                        keep_probT(u)
                    if u >= 4 and (u - 4) % 4 == 0:
                        normalise((u - 4) // 4)
                    if u >= 5 and (u - 5) % 4 == 0:
                        j = (u - 5) // 4
                        dve.wait_ge(ot_hi, it * G + j + 1)
                        if j >= 2:
                            dve.wait_ge(o_ps, it * G + j - 1)
                        nc.vector.tensor_tensor(oT[1][:, j % 2, :, :],
                                                b_p[0][:, 0:D].rearrange("p (c t) -> p c t", c=DC),
                                                oT[0][:, j % 2, :, :].bitcast(F32), ALU.subtract).then_inc(ot_lo, 1)
                    if u >= 6 and (u - 6) % 4 == 0:
                        j = (u - 6) // 4
                        dve.wait_ge(o_ps, it * G + j + 1)
                        nc.vector.tensor_tensor(x[:, it * G + j, :], b_p[1][:, 0:D], x[:, it * G + j, :],
                                                ALU.add).then_inc(x_ok, 1)
                chain.close()


def stage_long_conv(pr):
    nc, io, x, banks = pr.nc, pr.io, pr.x, pr.banks
    H, C = 16, 8
    HALF = 2
    NPAIR = C * (C + 1) // 2
    OFF = [d * C - d * (d - 1) // 2 for d in range(C)]
    BH = HALF * G * H
    HS = 3
    N = G * NPAIR
    GROUPS = [range(h, min(h + HS, H)) for h in range(0, H, HS)]
    NGR = len(GROUPS)
    b_x, b_c = banks[0:2], banks[2:8]
    with ExitStack() as ctx:
        sb = lambda n, shape, dt=F32: ctx.enter_context(nc.sbuf_tensor(f"lc_{n}", shape, dt))
        sem = lambda n: pr.sem(f"lc_{n}")
        norm = Norm(pr, ctx, None, b_x, "lc", split=False)
        toep32 = sb("toep32", [P, H, HALF * P])
        toep = (sb("toep_hi", [P, H, HALF * P], F32R), sb("toep_lo", [P, H, HALF * P], F32R))
        skip = sb("skip", [P, H])
        anti = sb("anti", [P, P])
        kt = sb("kt", [P, HALF, NB * H, C])
        kk32 = sb("kk32", [P, HALF, G * H, NPAIR])
        kk = (sb("kk_hi", [P, HALF, G * H, NPAIR], F32R), sb("kk_lo", [P, HALF, G * H, NPAIR], F32R))
        y = sb("y", [P, HALF, G * H, NPAIR])
        yq = sb("yq", [P, C, BH, C])

        loaded, kt_loaded = sem("consts_loaded"), sem("kt_loaded")
        diag_ok, t_hi, t_lo = sem("toeplitz_diag"), sem("toeplitz_hi"), sem("toeplitz_ready")
        kk_ok, sq_ok, kk_hi, kk_lo = sem("kk_ready"), sem("kk_squares"), sem("kk_hi_ready"), sem("kk_split")
        c_ps, c_ok = sem("conv_in_psum"), sem("conv_ready")
        yq_ok, y_ps, x_ok = sem("yq_ready"), sem("y_in_psum"), sem("x_updated")
        block = ctx.enter_context(nc.Block())

        @block.sync
        def _(sp):
            sp.dma_start(toep32[:], io["toeplitz"]).then_inc(loaded, 16)
            sp.dma_start(skip[:], io["conv_d"]).then_inc(loaded, 16)
            sp.dma_start(anti[:], io["anti"]).then_inc(loaded, 16)
            sp.dma_start(kt[:], io["ctx_rev"].rearrange("p a b (h c) -> p a (b h) c", c=C)).then_inc(kt_loaded, 16)

        @block.gpsimd
        def _(pool):
            with pool.Fori(0, NG) as it:
                norm.pool_rstd(pool, it)

        @block.tensor
        def _(pe):
            pe.wait_ge(t_lo, 1)
            with pe.Fori(0, NG) as it:
                pe.wait_ge(x_ok, ONE + it * G)
                norm.tensor_transpose(pe, it)
                pe.wait_ge(kk_lo, it + 1)
                for g, heads in enumerate(GROUPS):
                    lo_bank, hi_bank = b_c[2 * (g % 3)], b_c[2 * (g % 3) + 1]
                    pe.wait_ge(c_ok, ONE + it * NGR + max(0, g - 2))
                    for n, h in enumerate(heads):
                        cols = slice(n * N, (n + 1) * N)
                        rhs = [[kk[part][:, half, :, :].rearrange("p (b h) n -> p b h n", h=H)[:, :, h, :]
                                for half in range(HALF)] for part in range(2)]
                        d_hi, d_lo = toep[0][:, h, 0:P], toep[1][:, h, 0:P]
                        f_hi, f_lo = toep[0][:, h, P:2 * P], toep[1][:, h, P:2 * P]
                        mm = lambda out, a, b, start, stop=False: nc.tensor.matmul(
                            out[:, cols], a, b, start=start, stop=stop, skip_group_check=True)
                        mm(lo_bank, d_hi, rhs[0][0], True)
                        mm(lo_bank, d_hi, rhs[1][0], False)
                        mm(hi_bank, d_hi, rhs[0][1], True)
                        mm(hi_bank, d_hi, rhs[1][1], False)
                        mm(lo_bank, d_lo, rhs[0][0], False, True)
                        mm(hi_bank, d_lo, rhs[0][1], False)
                        mm(hi_bank, f_hi, rhs[0][0], False)
                        mm(hi_bank, f_hi, rhs[1][0], False)
                        last = mm(hi_bank, f_lo, rhs[0][0], False, True)
                    last.then_inc(c_ps, 1)
                for s in range(C):
                    pe.wait_ge(yq_ok, it * C + s + 1)
                    for j in range(G):
                        for half in range(HALF):
                            first = (half * G + j) * H
                            last = nc.tensor.matmul(
                                b_x[j // 2][:, (j % 2) * D + half * P:(j % 2) * D + half * P + P],
                                yq[:, s, first:first + H, :], pr.ident[:], is_transpose=True,
                                start=(s == 0 and j % 2 == 0 and half == 0), stop=(s == C - 1),
                                skip_group_check=True)
                last.then_inc(y_ps, 1)

        @block.scalar
        def _(act):
            act.wait_ge(diag_ok, 1)
            nc.scalar.copy(toep[0][:], toep32[:]).then_inc(t_hi, 1)

            def squares(i):
                act.wait_ge(kk_lo, i) if not isinstance(i, int) or i > 0 else None
                nc.scalar.activation(kk32[:, :, :, 0:C], kt[:, :, bass.ds(i * (G * H), G * H), :],
                                     ACT.Square).then_inc(sq_ok, 1)

            def split_hi(i):
                act.wait_ge(kk_ok, i + 1)
                nc.scalar.copy(kk[0][:], kk32[:]).then_inc(kk_hi, 1)

            def group(i, last):
                norm.scalar_hi(act, i)
                if not last:
                    squares(i + 1)
                for g, heads in enumerate(GROUPS):
                    act.wait_ge(c_ps, i * NGR + g + 1)
                    if g == 0:
                        act.wait_ge(yq_ok, i * C) if not isinstance(i, int) or i > 0 else None
                    for half in range(HALF):
                        src = b_c[2 * (g % 3) + half][:, 0:len(heads) * N]
                        dst = y[:, half, :, :].rearrange("p (b h) n -> p h b n", h=H)[:, heads[0]:heads[-1] + 1]
                        ins = nc.scalar.copy(dst, src.rearrange("p (h b n) -> p h b n", b=G, n=NPAIR))
                    ins.then_inc(c_ok, 1)
                if not last:
                    split_hi(i + 1)

            act.sem_inc(c_ok, ONE)
            act.wait_ge(kt_loaded, 16)
            squares(0)
            split_hi(0)
            with act.Fori(0, NG - 1) as it:
                group(it, False)
            group(NG - 1, True)

        @block.vector
        def _(dve):
            dve.wait_ge(loaded, 16 * 3)
            for h in range(H):
                last = nc.vector.scalar_tensor_tensor(toep32[:, h, 0:P], anti[:], skip[:, h:h + 1],
                                                      toep32[:, h, 0:P], ALU.mult, ALU.add)
            last.then_inc(diag_ok, 1)
            dve.wait_ge(t_hi, 1)
            nc.vector.tensor_tensor(toep[1][:], toep32[:], toep[0][:].bitcast(F32), ALU.subtract)\
                .then_inc(t_lo, 1)

            def products(i):
                own = kt[:, :, bass.ds(i * (G * H), G * H), :]
                for d in range(1, C):
                    last = nc.vector.tensor_tensor(kk32[:, :, :, OFF[d]:OFF[d] + C - d], own[:, :, :, 0:C - d],
                                                   own[:, :, :, d:C], ALU.mult)
                dve.wait_ge(sq_ok, i + 1)
                nc.vector.memset(pr.wait_slot[:], 0.0).then_inc(kk_ok, 1)

            def split_lo(i):
                dve.wait_ge(kk_hi, i + 1)
                nc.vector.tensor_tensor(kk[1][:], kk32[:], kk[0][:].bitcast(F32), ALU.subtract).then_inc(kk_lo, 1)

            def group(i, last):
                norm.vector_norm(dve, i)
                if not last:
                    products(i + 1)
                dve.wait_ge(norm.s_hi, i * DC + DC)
                dve.wait_ge(c_ok, ONE + (i + 1) * NGR)
                yv = y[:].rearrange("p a bh n -> p (a bh) n")
                qv = norm.xT[:].rearrange("p a (bh c) -> p (a bh) c", c=C)
                for s in range(C):
                    ins = nc.vector.tensor_tensor(yq[:, s, :, s:C], yv[:, :, OFF[s]:OFF[s] + C - s],
                                                  qv[:, :, 0:C - s], ALU.mult)
                    if s > 0:
                        d = C - s
                        ins = nc.vector.tensor_tensor(yq[:, s, :, 0:s], yv[:, :, OFF[d]:OFF[d] + s],
                                                      qv[:, :, d:C], ALU.mult)
                    ins.then_inc(yq_ok, 1)
                if not last:
                    split_lo(i + 1)
                dve.wait_ge(y_ps, i + 1)
                for j in range(G):
                    nc.vector.tensor_tensor(x[:, i * G + j, :], b_x[j // 2][:, (j % 2) * D:(j % 2) * D + D],
                                            x[:, i * G + j, :], ALU.add).then_inc(x_ok, 1)

            dve.sem_inc(x_ok, ONE)
            dve.wait_ge(kt_loaded, 16)
            products(0)
            split_lo(0)
            with dve.Fori(0, NG - 1) as it:
                group(it, False)
            group(NG - 1, True)


def stage_lora_experts(pr):
    nc, io, x, banks = pr.nc, pr.io, pr.x, pr.banks
    E, R, TOP, ALPHA = 8, 16, 2, 16.0
    W = D + E * R + E
    b_p, b_o, b_h = banks[0:2], banks[2:6], banks[6]
    with ExitStack() as ctx:
        sb = lambda n, shape, dt=F32: ctx.enter_context(nc.sbuf_tensor(f"le_{n}", shape, dt))
        sem = lambda n: pr.sem(f"le_{n}")
        norm = Norm(pr, ctx, None, b_p, "le")
        w32 = sb("w32", [P, DC, W])
        w = (sb("w_hi", [P, DC, W], F32R), sb("w_lo", [P, DC, W], F32R))
        u32 = sb("u32", [P, D])
        up = (sb("u_hi", [P, D], F32R), sb("u_lo", [P, D], F32R))
        before = sb("before", [P, E, E])
        logit = sb("logit", [P, G, E])
        stat = sb("stat", [P, 4, G])
        prob = sb("prob", [P, G, E])
        more = sb("more", [P, G, E, E])
        tied = sb("tied", [P, G, E, E])
        rank = sb("rank", [P, G, E])
        hw = sb("hw", [P, G, E * R])
        hT = (sb("hT_hi", [P, G * P], F32R), sb("hT_lo", [P, G * P], F32R))
        raw = [sb(f"raw{n}", [P, WIDE_CHUNK]) for n in range(3)]

        loaded, w_hi, w_lo = sem("weights_loaded"), sem("w_hi"), sem("w_ready")
        p_ps, d_ok, e_ok, hw_ok = sem("proj_in_psum"), sem("logits_ready"), sem("exps_ready"), sem("hw_ready")
        h_ps, h_hi, h_lo = sem("hT_in_psum"), sem("hT_hi_ready"), sem("hT_ready")
        o_ps, x_ok = sem("out_in_psum"), sem("x_updated")
        chain_s = sem("vector_chain")
        wide_in = [sem(f"wide_loaded{n}") for n in range(3)]
        wide_hi, wide_lo = sem("wide_hi"), sem("wide_ready")
        block = ctx.enter_context(nc.Block())

        pieces = [(n, at) for n in range(4) for at in range(0, WIDE_COLS, WIDE_CHUNK)]

        @block.sync
        def _(sp):
            sp.dma_start(w32[:], io["le_w"]).then_inc(loaded, 16)
            sp.dma_start(u32[:], io["le_u"]).then_inc(loaded, 16)
            sp.dma_start(before[:], io["before8"]).then_inc(loaded, 16)
            for n, (m, at) in enumerate(pieces):
                if n >= 3:
                    sp.wait_ge(wide_lo, n - 2)
                sp.dma_start(raw[n % 3][:], io["wide_w"][m, :, at:at + WIDE_CHUNK]).then_inc(wide_in[n % 3], 16)

        @block.gpsimd
        def _(pool):
            with pool.Fori(0, NG) as it:
                norm.pool_rstd(pool, it)

        @block.tensor
        def _(pe):
            pe.wait_ge(w_lo, 2)
            with pe.Fori(0, NG) as it:
                pe.wait_ge(x_ok, ONE + it * G)
                norm.tensor_transpose(pe, it)
                pe.wait_ge(norm.s_lo, it * DC + DC)
                for j in range(G):
                    for c in range(DC):
                        last = product(nc, b_o[j][:, 0:W], pair(norm.xT, slice(None), c, slice(j * P, j * P + P)),
                                       pair(w, slice(None), c), c == 0, c == DC - 1)
                    last.then_inc(p_ps, 1)
                pe.wait_ge(hw_ok, it + 1)
                for j in range(G):
                    last = nc.tensor.transpose(b_h[:, j * P:(j + 1) * P], hw[:, j, :], pr.ident[:])
                last.then_inc(h_ps, 1)
                pe.wait_ge(h_lo, it + 1)
                for j in range(G):
                    product(nc, b_o[j][:, 0:D], pair(hT, slice(None), slice(j * P, j * P + P)),
                            (up[0][:], up[1][:]), False, True).then_inc(o_ps, 1)

        def split_piece(eng, n, hi):
            m, at = pieces[n]
            dst = pr.wide[m]
            if hi:
                eng.wait_ge(wide_in[n % 3], 16 * (n // 3 + 1))
                nc.scalar.copy(dst[0][:, at:at + WIDE_CHUNK], raw[n % 3][:]).then_inc(wide_hi, 1)
            else:
                eng.wait_ge(wide_hi, n + 1)
                nc.vector.tensor_tensor(dst[1][:, at:at + WIDE_CHUNK], raw[n % 3][:],
                                        dst[0][:, at:at + WIDE_CHUNK].bitcast(F32), ALU.subtract)\
                    .then_inc(wide_lo, 1)

        @block.scalar
        def _(act):
            act.wait_ge(loaded, 48)
            nc.scalar.copy(w[0][:], w32[:]).then_inc(w_hi, 1)
            nc.scalar.copy(up[0][:], u32[:]).then_inc(w_hi, 1)
            with act.Fori(0, NG) as it:
                norm.scalar_hi(act, it)
                act.wait_ge(d_ok, it + 1)
                nc.scalar.activation(prob[:], logit[:], ACT.Exp).then_inc(e_ok, 1)
                act.wait_ge(h_ps, it + 1)
                nc.scalar.copy(hT[0][:], b_h[:, :]).then_inc(h_hi, 1)
            for n in range(len(pieces)):
                split_piece(act, n, True)

        @block.vector
        def _(dve):
            dve.wait_ge(w_hi, 2)
            nc.vector.tensor_tensor(w[1][:], w32[:], w[0][:].bitcast(F32), ALU.subtract).then_inc(w_lo, 1)
            nc.vector.tensor_tensor(up[1][:], u32[:], up[0][:].bitcast(F32), ALU.subtract).then_inc(w_lo, 1)
            dve.sem_inc(x_ok, ONE)
            with dve.Fori(0, NG) as it:
                norm.vector_norm(dve, it)
                norm.vector_lo(dve, it)
                chain = Chain(dve, chain_s, it, 15)
                per_e = lambda t: t.unsqueeze(2).to_broadcast([P, G, E])
                for j in range(G):
                    dve.wait_ge(p_ps, it * G + j + 1)
                    last = nc.vector.tensor_copy(logit[:, j, :], b_o[j][:, D + E * R:W])
                chain.done(last)
                chain.done(nc.vector.tensor_reduce(stat[:, 0, :], logit[:], AX, ALU.max))
                nc.vector.tensor_tensor(logit[:], logit[:], per_e(stat[:, 0, :]), ALU.subtract).then_inc(d_ok, 1)
                dve.wait_ge(e_ok, it + 1)
                chain.done(nc.vector.tensor_reduce(stat[:, 1, :], prob[:], AX, ALU.add))
                chain.done(nc.vector.reciprocal(stat[:, 2, :], stat[:, 1, :]))
                chain.done(nc.vector.tensor_tensor(prob[:], prob[:], per_e(stat[:, 2, :]), ALU.mult))
                ahead = [prob[:, j, :].unsqueeze(1).to_broadcast([P, E, E]) for j in range(G)]
                self_ = [prob[:, j, :].unsqueeze(2).to_broadcast([P, E, E]) for j in range(G)]
                for j in range(G):
                    nc.vector.tensor_tensor(more[:, j], ahead[j], self_[j], ALU.is_gt)
                    last = nc.vector.tensor_tensor(tied[:, j], ahead[j], self_[j], ALU.is_equal)
                chain.done(last)
                chain.done(nc.vector.tensor_tensor(
                    tied[:], tied[:], before[:].unsqueeze(1).to_broadcast([P, G, E, E]), ALU.mult))
                chain.done(nc.vector.tensor_tensor(more[:], more[:], tied[:], ALU.add))
                chain.done(nc.vector.tensor_reduce(rank[:], more[:], AX, ALU.add))
                chain.done(nc.vector.scalar_tensor_tensor(rank[:], rank[:], TOP - 0.5, prob[:], ALU.is_lt, ALU.mult))
                chain.done(nc.vector.tensor_reduce(stat[:, 3, :], rank[:], AX, ALU.add))
                chain.done(nc.vector.reciprocal(stat[:, 3, :], stat[:, 3, :]))
                chain.done(nc.vector.tensor_scalar(stat[:, 3, :], stat[:, 3, :], ALPHA, None, ALU.mult))
                chain.done(nc.vector.tensor_tensor(rank[:], rank[:], per_e(stat[:, 3, :]), ALU.mult))
                for j in range(G):
                    last = nc.vector.tensor_tensor(hw[:, j, :].rearrange("p (e r) -> p e r", e=E),
                                                   b_o[j][:, D:D + E * R].rearrange("p (e r) -> p e r", e=E),
                                                   rank[:, j, :].unsqueeze(2).to_broadcast([P, E, R]), ALU.mult)
                last.then_inc(hw_ok, 1)
                dve.wait_ge(h_hi, it + 1)
                nc.vector.tensor_tensor(hT[1][:], b_h[:, :], hT[0][:].bitcast(F32), ALU.subtract).then_inc(h_lo, 1)
                chain.done(nc.vector.memset(pr.wait_slot[:], 0.0))
                for j in range(G):
                    dve.wait_ge(o_ps, it * G + j + 1)
                    nc.vector.tensor_tensor(x[:, it * G + j, :], b_o[j][:, 0:D], x[:, it * G + j, :],
                                            ALU.add).then_inc(x_ok, 1)
                chain.close()
            for n in range(len(pieces)):
                split_piece(dve, n, False)


WIDE_COLS = 4096
WIDE_CHUNK = 2048


def stage_wide_attention(pr):
    nc, io, x, banks = pr.nc, pr.io, pr.x, pr.banks
    H, HD = 16, 128
    VH = 4
    SCALE = HD ** -0.5
    b_p, b_s, b_t, b_z, b_o = banks[0:2], banks[2:4], banks[4], banks[5], banks[6:8]
    with ExitStack() as ctx:
        sb = lambda n, shape, dt=F32: ctx.enter_context(nc.sbuf_tensor(f"wa_{n}", shape, dt))
        sem = lambda n: pr.sem(f"wa_{n}")
        norm = Norm(pr, ctx, None, b_p, "wa")
        xT = norm.xT
        wq, wk, wv = [tuple(t[:].rearrange("p (c n) -> p c n", c=DC) for t in pr.wide[n]) for n in range(3)]
        wo = tuple(t[:].rearrange("p (h n) -> p h n", h=H) for t in pr.wide[3])
        causal = sb("causal", [P, GT], BF16)
        ident_b = sb("ident_b", [P, P], BF16)
        q = sb("q", [P, 2, GT])
        k = sb("k", [P, 2, GT])
        v = sb("v", [P, 2, G, VH * HD])
        negmax = sb("negmax", [P, 2, G])
        sums = sb("sums", [P, 2, G])
        rsum = sb("rsum", [P, 2, G])
        prob = sb("prob", [P, 2, G, P])
        probT = sb("probT", [P, 2, G, P])
        z = (sb("z_hi", [P, 2, GT], F32R), sb("z_lo", [P, 2, GT], F32R))

        loaded = sem("masks_loaded")
        q_ps, q_ok, k_ps, k_ok = sem("q_in_psum"), sem("q_ready"), sem("k_in_psum"), sem("k_ready")
        v_ps, v_ok = sem("v_in_psum"), sem("v_ready")
        s_ps, max_ok, exp_ok = sem("scores_in_psum"), sem("negmax_ready"), sem("exps_ready")
        r_ok, prob_ok = sem("rsum_ready"), sem("probs_ready")
        t_ps, t_ok = sem("probsT_in_psum"), sem("probsT_ready")
        z_ps, z_hi, z_lo = sem("z_in_psum"), sem("z_hi_ready"), sem("z_ready")
        o_ps, x_ok = sem("out_in_psum"), sem("x_updated")
        chain_s = sem("vector_chain")
        block = ctx.enter_context(nc.Block())

        STEPS = range(-2, H + 1)

        def v_units(t):
            return {-2: [0, 1], -1: [2, 3]}.get(t, [t + G] if 0 <= t < H - G else [])

        @block.sync
        def _(sp):
            sp.dma_start(causal[:], io["causal"]).then_inc(loaded, 16)
            sp.dma_start(ident_b[:], io["ident_b"]).then_inc(loaded, 16)

        @block.gpsimd
        def _(pool):
            with pool.Fori(0, NG) as it:
                norm.pool_rstd(pool, it)
                for h in range(H):
                    pool.wait_ge(r_ok, it * H + h + 1)
                    nc.gpsimd.tensor_tensor(prob[:, h % 2], prob[:, h % 2],
                                            rsum[:, h % 2, :].unsqueeze(2).to_broadcast([P, G, P]), ALU.mult)\
                        .then_inc(prob_ok, 1)

        @block.tensor
        def _(pe):
            pe.wait_ge(loaded, 32)
            with pe.Fori(0, NG) as it:
                pe.wait_ge(x_ok, ONE + it * G)
                norm.tensor_transpose(pe, it)
                pe.wait_ge(norm.s_lo, it * DC + DC)

                def scores(h):
                    pe.wait_ge(q_ok, it * H + h + 1)
                    pe.wait_ge(k_ok, it * H + h + 1)
                    if h >= 2:
                        pe.wait_ge(exp_ok, it * H + h - 1)
                    nc.tensor.matmul(b_s[h % 2][:, :], ident_b[:], causal[:], start=True, stop=False,
                                     skip_group_check=True)
                    for j in range(G):
                        t = slice(j * P, (j + 1) * P)
                        last = nc.tensor.matmul(b_s[h % 2][:, t], q[:, h % 2, t], k[:, h % 2, t], start=False,
                                                stop=True, skip_group_check=True)
                    last.then_inc(s_ps, 1)

                def qk(h, v_before):
                    cols = slice(h * HD, (h + 1) * HD)
                    if v_before:
                        pe.wait_ge(v_ok, it * H + v_before)
                    for c in range(DC):
                        last = product(nc, b_p[0][:, :], pair(wq, slice(None), c, cols), pair(xT, slice(None), c),
                                       c == 0, c == DC - 1)
                    last.then_inc(q_ps, 1)
                    if h >= 1:
                        pe.wait_ge(k_ok, it * H + h)
                    for c in range(DC):
                        last = product(nc, b_p[1][:, :], pair(wk, slice(None), c, cols), pair(xT, slice(None), c),
                                       c == 0, c == DC - 1)
                    last.then_inc(k_ps, 1)

                def values(n, q_before):
                    g, j = divmod(n, G)
                    pe.wait_ge(q_ok, it * H + q_before)
                    if n >= 1:
                        pe.wait_ge(v_ok, it * H + n)
                    for c in range(DC):
                        last = product(nc, b_p[0][:, :], pair(xT, slice(None), c, slice(j * P, (j + 1) * P)),
                                       pair(wv, slice(None), c, slice(g * VH * HD, (g + 1) * VH * HD)),
                                       c == 0, c == DC - 1)
                    last.then_inc(v_ps, 1)

                def turn(h):
                    pe.wait_ge(prob_ok, it * H + h + 1)
                    if h >= 1:
                        pe.wait_ge(t_ok, it * H + h)
                    for j in range(G):
                        last = nc.tensor.transpose(b_t[:, j * P:(j + 1) * P], prob[:, h % 2, j, :], pr.ident[:])
                    last.then_inc(t_ps, 1)

                def weigh(h):
                    g, n = divmod(h, VH)
                    pe.wait_ge(t_ok, it * H + h + 1)
                    pe.wait_ge(v_ok, it * H + G * (g + 1))
                    if h >= 1:
                        pe.wait_ge(z_lo, it * H + h)
                    for j in range(G):
                        last = nc.tensor.matmul(b_z[:, j * P:(j + 1) * P], v[:, g % 2, j, n * HD:(n + 1) * HD],
                                                probT[:, h % 2, j, :], start=True, stop=True)
                    last.then_inc(z_ps, 1)

                def project(h):
                    pe.wait_ge(z_lo, it * H + h + 1)
                    for j in range(G):
                        last = product(nc, b_o[j // 2][:, (j % 2) * D:(j % 2) * D + D],
                                       pair(z, slice(None), h % 2, slice(j * P, (j + 1) * P)),
                                       pair(wo, slice(None), h), h == 0 and j % 2 == 0, h == H - 1)
                    last.then_inc(o_ps, 1)

                n_v = 0
                for t in STEPS:
                    if 0 <= t + 1 < H:
                        scores(t + 1)
                    if t + 2 < H:
                        qk(t + 2, n_v)
                    if t >= 1:
                        project(t - 1)
                    if 0 <= t < H:
                        turn(t)
                    for n in v_units(t):
                        values(n, min(t + 3, H))
                        n_v += 1
                    if 0 <= t < H:
                        weigh(t)

        @block.scalar
        def _(act):
            with act.Fori(0, NG) as it:
                norm.scalar_hi(act, it)
                for t in STEPS:
                    h = t + 1
                    if 0 <= h < H:
                        act.wait_ge(max_ok, it * H + h + 1)
                        if h >= 2:
                            act.wait_ge(t_ps, it * H + h - 1)
                        for j in range(G):
                            last = nc.scalar.activation(prob[:, h % 2, j, :], b_s[h % 2][:, j * P:(j + 1) * P],
                                                        ACT.Exp, bias=negmax[:, h % 2, j:j + 1], scale=SCALE,
                                                        accum_out=sums[:, h % 2, j:j + 1])
                        last.then_inc(exp_ok, 1)
                    h = t + 2
                    if h < H:
                        act.wait_ge(q_ps, it * H + h + 1)
                        if h >= 2:
                            act.wait_ge(s_ps, it * H + h - 1)
                        nc.scalar.copy(q[:, h % 2, :], b_p[0][:, :]).then_inc(q_ok, 1)
                    for n in v_units(t):
                        g, j = divmod(n, G)
                        act.wait_ge(v_ps, it * H + n + 1)
                        if g >= 2:
                            act.wait_ge(z_ps, it * H + VH * (g - 1))
                        nc.scalar.copy(v[:, g % 2, j, :], b_p[0][:, :]).then_inc(v_ok, 1)
                    if 0 <= t < H:
                        act.wait_ge(z_ps, it * H + t + 1)
                        if t >= 2:
                            act.wait_ge(o_ps, it * H + t - 1)
                        nc.scalar.copy(z[0][:, t % 2, :], b_z[:, :]).then_inc(z_hi, 1)

        @block.vector
        def _(dve):
            dve.sem_inc(x_ok, ONE)
            with dve.Fori(0, NG) as it:
                norm.vector_norm(dve, it)
                norm.vector_lo(dve, it)
                chain = Chain(dve, chain_s, it, H)
                for t in STEPS:
                    h = t + 1
                    if 0 <= h < H:
                        dve.wait_ge(s_ps, it * H + h + 1)
                        if h >= 2:
                            dve.wait_ge(exp_ok, it * H + h - 1)
                        chain.done(nc.vector.tensor_reduce(
                            negmax[:, h % 2, :], b_s[h % 2][:, :].rearrange("p (j k) -> p j k", j=G), AX, ALU.max))
                        nc.vector.tensor_scalar(negmax[:, h % 2, :], negmax[:, h % 2, :], -SCALE, None, ALU.mult)\
                            .then_inc(max_ok, 1)
                    h = t + 2
                    if h < H:
                        dve.wait_ge(k_ps, it * H + h + 1)
                        if h >= 2:
                            dve.wait_ge(s_ps, it * H + h - 1)
                        nc.vector.tensor_copy(k[:, h % 2, :], b_p[1][:, :]).then_inc(k_ok, 1)
                    h = t + 1
                    if 0 <= h < H:
                        dve.wait_ge(exp_ok, it * H + h + 1)
                        if h >= 2:
                            dve.wait_ge(prob_ok, it * H + h - 1)
                        nc.vector.reciprocal(rsum[:, h % 2, :], sums[:, h % 2, :]).then_inc(r_ok, 1)
                    if 0 <= t < H:
                        dve.wait_ge(t_ps, it * H + t + 1)
                        if t >= 2:
                            dve.wait_ge(z_ps, it * H + t - 1)
                        nc.vector.tensor_copy(probT[:, t % 2], b_t[:, :].rearrange("p (j k) -> p j k", j=G))\
                            .then_inc(t_ok, 1)
                        dve.wait_ge(z_hi, it * H + t + 1)
                        nc.vector.tensor_tensor(z[1][:, t % 2, :], b_z[:, :], z[0][:, t % 2, :].bitcast(F32),
                                                ALU.subtract).then_inc(z_lo, 1)
                dve.wait_ge(o_ps, it * H + H)
                for j in range(G):
                    nc.vector.tensor_tensor(x[:, it * G + j, :], b_o[j // 2][:, (j % 2) * D:(j % 2) * D + D],
                                            x[:, it * G + j, :], ALU.add).then_inc(x_ok, 1)
                chain.close()


def stage_experts_and_wide_attention(pr):
    nc = pr.nc
    with ExitStack() as ctx:
        pr.wide = [tuple(ctx.enter_context(nc.sbuf_tensor(f"wide{n}_{part}", [P, WIDE_COLS], F32R))
                         for part in ("hi", "lo")) for n in range(4)]
        stage_lora_experts(pr)
        stage_wide_attention(pr)


def stage_linear_attention(pr):
    nc, io, x, banks = pr.nc, pr.io, pr.x, pr.banks
    H, HD, F = 16, 16, 64
    T = H // 2
    HF = H * F
    VW = HD + 1
    b_p = banks[0:2]
    b_k, b_kv, b_qkv, b_v, b_o = banks[2:4], banks[4], banks[5], banks[6], banks[7]
    with ExitStack() as ctx:
        sb = lambda n, shape, dt=F32: ctx.enter_context(nc.sbuf_tensor(f"li_{n}", shape, dt))
        both = lambda n, shape: (sb(f"{n}_hi", shape, F32R), sb(f"{n}_lo", shape, F32R))
        sem = lambda n: pr.sem(f"li_{n}")
        norm = Norm(pr, ctx, None, b_p, "li")
        wqk = sb("wqk", [HD, 2, H, D])
        wf = sb("wf", [HD, 2, 2 * F])
        bqk = sb("bqk", [HD, 2, H])
        vo32 = sb("vo32", [P, 2, DC, D])
        vo = both("vo", [P, 2, DC, D])
        vo_row = sb("vo_row", [1, 2, D])
        row = both("row", [1, 2, D])
        mqk = both("mqk", [P, 2, DC, HF])
        q_bias = sb("q_bias", [P, T])
        k_row = both("k_row", [1, HF])
        mask = sb("mask", [P, NB])
        kt32 = sb("kt32", [P, DC, NB, P])
        kt = both("kt", [P, DC, GT])
        qp = sb("qp", [P, T, GT])
        kp = sb("kp", [P, 2, HF])
        va = sb("va", [P, 2, H, VW])
        kv = sb("kv", [P, 2, T, 2 * VW])
        rden = sb("rden", [P, 2, H])
        o = sb("o", [P, 2, D])
        oT = both("oT", [P, 2, DC, P])

        loaded = sem("loaded")
        fold_ps, fold_hi, fold_lo = sem("folded_in_psum"), sem("folded_hi"), sem("folded_ready")
        w_hi, w_lo, clear = sem("vo_hi"), sem("vo_ready"), sem("cleared")
        kt_hi, kt_lo = sem("kt_hi"), sem("kt_ready")
        q_ps, q_ok = sem("q_in_psum"), sem("q_ready")
        k_ps, k_ok = sem("k_in_psum"), sem("k_ready")
        v_ps, v_ok = sem("v_in_psum"), sem("v_ready")
        kv_ps, kv_ok = sem("kv_in_psum"), sem("kv_ready")
        n_ps, n_ok = sem("qkv_in_psum"), sem("o_ready")
        ot_ps, ot_hi, ot_lo = sem("oT_in_psum"), sem("oT_hi_ready"), sem("oT_ready")
        o_ps, x_ok = sem("out_in_psum"), sem("x_updated")
        chain_s = sem("vector_chain")
        block = ctx.enter_context(nc.Block())
        NLOAD = 7
        FOLDS = [(w, c, half) for w in range(2) for c in range(DC) for half in range(2)]

        @block.sync
        def _(sp):
            sp.dma_start(wqk[:], io["li_wqk"]).then_inc(loaded, 16)
            sp.dma_start(wf[:], io["li_wf"]).then_inc(loaded, 16)
            sp.dma_start(bqk[:], io["li_bqk"]).then_inc(loaded, 16)
            sp.dma_start(vo32[:], io["li_vo"]).then_inc(loaded, 16)
            sp.dma_start(vo_row[:], io["li_vo_row"]).then_inc(loaded, 16)
            sp.dma_start(mask[:], io["li_mask"]).then_inc(loaded, 16)
            sp.dma_start(kt32[:], io["ctx_rev"]).then_inc(loaded, 16)

        @block.gpsimd
        def _(pool):
            nc.gpsimd.memset(va[:], 1.0).then_inc(clear, 1)
            nc.gpsimd.memset(kv[:], 0.0).then_inc(clear, 1)
            with pool.Fori(0, NG) as it:
                norm.pool_rstd(pool, it)

        @block.tensor
        def _(pe):
            pe.wait_ge(loaded, 16 * NLOAD)
            for n, (w, c, half) in enumerate(FOLDS):
                for h in range(8):
                    last = nc.tensor.matmul(banks[n][:, h * F:(h + 1) * F],
                                            wqk[:, w, 8 * half + h, c * P:(c + 1) * P], wf[:, w, 0:F],
                                            start=True, stop=True)
                last.then_inc(fold_ps, 1)
            pe.wait_ge(fold_lo, 3)
            nc.tensor.matmul(banks[0][:, 0:H], wf[:, 0, :], bqk[:, 0, :], start=True, stop=True)\
                .then_inc(fold_ps, 1)
            for half in range(2):
                for h in range(8):
                    last = nc.tensor.matmul(banks[1 + half][0:1, h * F:(h + 1) * F],
                                            bqk[:, 1, 8 * half + h:8 * half + h + 1], wf[:, 1, 0:F],
                                            start=True, stop=True)
                last.then_inc(fold_ps, 1)
            pe.wait_ge(fold_lo, len(FOLDS) + 3)
            pe.wait_ge(w_lo, 2)

            def bias(out, pair_, index):
                nc.tensor.matmul(out, pr.ones_row[:], pair_[0][index], start=True, stop=False,
                                 skip_group_check=True)
                nc.tensor.matmul(out, pr.ones_row[:], pair_[1][index], start=False, stop=False,
                                 skip_group_check=True)

            with pe.Fori(0, NG) as it:
                pe.wait_ge(x_ok, ONE + it * G)
                norm.tensor_transpose(pe, it)
                pe.wait_ge(kt_lo, it + 1)

                def keys(j):
                    t = slice(j * P, (j + 1) * P)
                    for half in range(2):
                        if j >= 1:
                            pe.wait_ge(k_ok, it * 2 * G + 2 * (j - 1) + half + 1)
                        bias(b_k[half][:, :], k_row, (slice(None), slice(half * 512, half * 512 + 512)))
                        for c in range(DC):
                            last = product(nc, b_k[half][:, :], pair(kt, slice(None), c, t),
                                           pair(mqk, slice(None), 1, c, slice(half * 512, half * 512 + 512)),
                                           False, c == DC - 1)
                        last.then_inc(k_ps, 1)
                    if j >= 1:
                        pe.wait_ge(v_ok, it * G + j)
                    bias(b_v[:, 0:D], row, (slice(None), 0))
                    for c in range(DC):
                        last = product(nc, b_v[:, 0:D], pair(kt, slice(None), c, t), pair(vo, slice(None), 0, c),
                                       False, c == DC - 1)
                    last.then_inc(v_ps, 1)

                def key_values(j):
                    pe.wait_ge(k_ok, it * 2 * G + 2 * j + 2)
                    pe.wait_ge(v_ok, it * G + j + 1)
                    if j >= 1:
                        pe.wait_ge(kv_ok, it * G + j)
                    for t in range(T):
                        last = nc.tensor.matmul(b_kv[:, t * 2 * VW:(t + 1) * 2 * VW],
                                                kp[:, j % 2, t * P:(t + 1) * P],
                                                va[:, j % 2, 2 * t:2 * t + 2, :], start=True, stop=True)
                    last.then_inc(kv_ps, 1)

                def queries(t):
                    if t >= 2:
                        pe.wait_ge(q_ok, it * T + t - 1)
                    for c in range(DC):
                        last = product(nc, b_p[t % 2][:, :], pair(mqk, slice(None), 0, c, slice(t * P, (t + 1) * P)),
                                       pair(norm.xT, slice(None), c), c == 0, c == DC - 1)
                    last.then_inc(q_ps, 1)

                def numerators(j):
                    pe.wait_ge(kv_ok, it * G + j + 1)
                    pe.wait_ge(q_ok, it * T + T)
                    if j >= 1:
                        pe.wait_ge(n_ok, it * G + j)
                    for t in range(T):
                        last = nc.tensor.matmul(b_qkv[:, t * 2 * VW:(t + 1) * 2 * VW],
                                                qp[:, t, j * P:(j + 1) * P], kv[:, j % 2, t, :],
                                                start=True, stop=True)
                    last.then_inc(n_ps, 1)

                def turn_o(j):
                    pe.wait_ge(n_ok, it * G + j + 1)
                    if j >= 1:
                        pe.wait_ge(ot_lo, it * G + j)
                    for c in range(DC):
                        last = nc.tensor.transpose(b_p[0][:, c * P:(c + 1) * P], o[:, j % 2, c * P:(c + 1) * P],
                                                   pr.ident[:])
                    last.then_inc(ot_ps, 1)

                def project(j):
                    pe.wait_ge(ot_lo, it * G + j + 1)
                    if j >= 1:
                        pe.wait_ge(x_ok, ONE + it * G + j)
                    bias(b_o[:, 0:D], row, (slice(None), 1))
                    for c in range(DC):
                        last = product(nc, b_o[:, 0:D], pair(oT, slice(None), j % 2, c), pair(vo, slice(None), 1, c),
                                       False, c == DC - 1)
                    last.then_inc(o_ps, 1)

                keys(0)
                pe.wait_ge(norm.s_lo, it * DC + DC)
                for t in range(T):
                    queries(t)
                for j in range(G + 2):
                    if j < G:
                        key_values(j)
                    if j + 1 < G:
                        keys(j + 1)
                    if j < G:
                        numerators(j)
                    if 1 <= j <= G:
                        turn_o(j - 1)
                    if j >= 2:
                        project(j - 2)

        @block.scalar
        def _(act):
            act.wait_ge(loaded, 16 * NLOAD)
            nc.scalar.copy(vo[0][:], vo32[:]).then_inc(w_hi, 1)
            nc.scalar.copy(row[0][:], vo_row[:]).then_inc(w_hi, 1)
            for n, (w, c, half) in enumerate(FOLDS):
                act.wait_ge(fold_ps, n + 1)
                nc.scalar.copy(mqk[0][:, w, c, half * 512:half * 512 + 512], banks[n][:, :]).then_inc(fold_hi, 1)
            for half in range(2):
                act.wait_ge(fold_ps, len(FOLDS) + 2 + half)
                nc.scalar.copy(k_row[0][:, half * 512:half * 512 + 512], banks[1 + half][0:1, :])\
                    .then_inc(fold_hi, 1)
            act.wait_ge(clear, 2)
            with act.Fori(0, NG) as it:
                act.wait_ge(x_ok, ONE + it * G)
                nc.scalar.copy(kt[0][:], kt32[:, :, bass.ds(it * G, G), :]
                               .rearrange("p c b t -> p c (b t)")).then_inc(kt_hi, 1)
                norm.scalar_hi(act, it)
                def values(j):
                    act.wait_ge(v_ps, it * G + j + 1)
                    if j >= 2:
                        act.wait_ge(kv_ps, it * G + j - 1)
                    nc.scalar.copy(va[:, j % 2, :, 0:HD], b_v[:, 0:D].rearrange("p (h d) -> p h d", h=H))\
                        .then_inc(v_ok, 1)

                values(0)
                for t in range(T):
                    act.wait_ge(q_ps, it * T + t + 1)
                    nc.scalar.activation(qp[:, t, :], b_p[t % 2][:, :], ACT.Relu, bias=q_bias[:, t:t + 1])\
                        .then_inc(q_ok, 1)
                for j in range(G + 1):
                    if j < G:
                        act.wait_ge(kv_ps, it * G + j + 1)
                        if j >= 2:
                            act.wait_ge(n_ps, it * G + j - 1)
                        src = b_kv[:, 0:T * 2 * VW].rearrange("p (t n) -> p t n", t=T)
                        nc.scalar.copy(kv[0:F, j % 2, :, 0:VW], src[0:F, :, 0:VW])
                        nc.scalar.copy(kv[F:2 * F, j % 2, :, VW:2 * VW], src[F:2 * F, :, VW:2 * VW])\
                            .then_inc(kv_ok, 1)
                    if j + 1 < G:
                        values(j + 1)
                    if j >= 1:
                        act.wait_ge(ot_ps, it * G + j)
                        nc.scalar.copy(oT[0][:, (j - 1) % 2, :, :],
                                       b_p[0][:, 0:D].rearrange("p (c t) -> p c t", c=DC)).then_inc(ot_hi, 1)

        @block.vector
        def _(dve):
            dve.wait_ge(w_hi, 2)
            nc.vector.tensor_tensor(vo[1][:], vo32[:], vo[0][:].bitcast(F32), ALU.subtract).then_inc(w_lo, 1)
            nc.vector.tensor_tensor(row[1][:], vo_row[:], row[0][:].bitcast(F32), ALU.subtract).then_inc(w_lo, 1)
            for n, (w, c, half) in enumerate(FOLDS):
                dve.wait_ge(fold_hi, n + 1)
                cols = slice(half * 512, half * 512 + 512)
                nc.vector.tensor_tensor(mqk[1][:, w, c, cols], banks[n][:, :], mqk[0][:, w, c, cols].bitcast(F32),
                                        ALU.subtract).then_inc(fold_lo, 1)
            dve.wait_ge(fold_ps, len(FOLDS) + 1)
            nc.vector.tensor_copy(q_bias[0:F, :], banks[0][0:F, 0:H].rearrange("p (t e) -> p t e", e=2)[:, :, 0])
            nc.vector.tensor_copy(q_bias[F:2 * F, :],
                                  banks[0][F:2 * F, 0:H].rearrange("p (t e) -> p t e", e=2)[:, :, 1])\
                .then_inc(fold_lo, 1)
            for half in range(2):
                dve.wait_ge(fold_hi, len(FOLDS) + half + 1)
                cols = slice(half * 512, half * 512 + 512)
                nc.vector.tensor_tensor(k_row[1][:, cols], banks[1 + half][0:1, :], k_row[0][:, cols].bitcast(F32),
                                        ALU.subtract).then_inc(fold_lo, 1)
            dve.sem_inc(x_ok, ONE)
            with dve.Fori(0, NG) as it:
                norm.vector_norm(dve, it)
                dve.wait_ge(kt_hi, it + 1)
                nc.vector.tensor_tensor(kt[1][:], kt32[:, :, bass.ds(it * G, G), :]
                                        .rearrange("p c b t -> p c (b t)"), kt[0][:].bitcast(F32),
                                        ALU.subtract).then_inc(kt_lo, 1)
                norm.vector_lo(dve, it)
                chain = Chain(dve, chain_s, it, 2 * G)

                def keys(j):
                    for half in range(2):
                        dve.wait_ge(k_ps, it * 2 * G + 2 * j + half + 1)
                        if j >= 2:
                            dve.wait_ge(kv_ps, it * G + j - 1)
                        nc.vector.tensor_scalar(kp[:, j % 2, half * 512:half * 512 + 512], b_k[half][:, :], 0.0,
                                                mask[:, bass.ds(it * G + j, 1)], ALU.max, ALU.mult)\
                            .then_inc(k_ok, 1)

                keys(0)
                for j in range(G + 2):
                    if j + 1 < G:
                        keys(j + 1)
                    if j < G:
                        dve.wait_ge(n_ps, it * G + j + 1)
                        src = b_qkv[:, 0:H * VW].rearrange("p (h n) -> p h n", h=H)
                        chain.done(nc.vector.tensor_scalar(rden[:, j % 2, :], src[:, :, HD], 1e-8, None, ALU.add))
                        chain.done(nc.vector.reciprocal(rden[:, j % 2, :], rden[:, j % 2, :]))
                        if j >= 2:
                            dve.wait_ge(ot_ps, it * G + j - 1)
                        nc.vector.tensor_tensor(o[:, j % 2, :].rearrange("p (h d) -> p h d", h=H),
                                                src[:, :, 0:HD],
                                                rden[:, j % 2, :].unsqueeze(2).to_broadcast([P, H, HD]), ALU.mult)\
                            .then_inc(n_ok, 1)
                    if 1 <= j <= G:
                        dve.wait_ge(ot_hi, it * G + j)
                        if j >= 3:
                            dve.wait_ge(o_ps, it * G + j - 2)
                        nc.vector.tensor_tensor(oT[1][:, (j - 1) % 2, :, :],
                                                b_p[0][:, 0:D].rearrange("p (c t) -> p c t", c=DC),
                                                oT[0][:, (j - 1) % 2, :, :].bitcast(F32), ALU.subtract)\
                            .then_inc(ot_lo, 1)
                    if j >= 2:
                        dve.wait_ge(o_ps, it * G + j - 1)
                        nc.vector.tensor_tensor(x[:, it * G + j - 2, :], b_o[:, 0:D], x[:, it * G + j - 2, :],
                                                ALU.add).then_inc(x_ok, 1)
                chain.close()


def stage_expert_mix(pr):
    nc, io, x, banks = pr.nc, pr.io, pr.x, pr.banks
    E, H, K = 32, 64, 16
    NW = 64
    BIG = 3e38
    with ExitStack() as ctx:
        sb = lambda n, shape, dt=F32: ctx.enter_context(nc.sbuf_tensor(f"em_{n}", shape, dt))
        sem = lambda n: pr.sem(f"em_{n}")
        norm = Norm(pr, ctx, None, banks[0:2], "em", split=False)
        w = sb("w", [P, NW, P])
        sim = sb("sim", [P, DC, E])
        gates = sb("gates", [NB, E])
        before = sb("before", [NB, E, E])
        xT = sb("xT_all", [P, DC, NB, P])
        rep = sb("rep", [P, DC, NB])
        rep2 = sb("rep2", [P, DC, NB])
        sim2 = sb("sim2", [P, DC, E])
        ones = sb("ones", [P, NB])
        minus_half = sb("minus_half", [NB, E])
        simn = sb("simn", [NB, E])
        repn = sb("repn", [NB, 1])
        logit = sb("logit", [NB, E])
        gated = sb("gated", [NB, E])
        act_mask = sb("act_mask", [NB, E])
        small = sb("small", [NB, 8])
        more = sb("more", [NB, E, E])
        tied = sb("tied", [NB, E, E])
        rank = sb("rank", [NB, E])
        sig = sb("sig", [NB, E])
        route = sb("route", [NB, 4, E])
        routeT = sb("routeT", [P, NB])
        wvT = sb("wvT", [P, DC, NB, 2, H])
        wo = sb("wo", [P, NB, P])
        hT = sb("hT", [P, 2, P])

        loaded, xT_ok, rep_ok = sem("loaded"), sem("xT_kept"), sem("rep_ready")
        const_ok, aff_ps, rn_in, rn_ok = sem("consts"), sem("affinity_in_psum"), sem("norms_in"), sem("rnorms_ready")
        exp_in, exp_ok, r_ok, rT_ps, rT_ok = (sem("exp_in"), sem("exp_ready"), sem("routing_ready"),
                                              sem("routingT_in_psum"), sem("routingT_ready"))
        mix_ps, mixv_ok, mixo_ok = sem("mix_in_psum"), sem("mix_v_ready"), sem("mix_o_ready")
        h_ps, h_ok, o_ps, x_ok = sem("hT_in_psum"), sem("hT_ready"), sem("out_in_psum"), sem("x_updated")
        chain_s, sig_ok, stored = sem("vector_chain"), sem("gate_exps"), sem("stored")
        block = ctx.enter_context(nc.Block())

        @block.sync
        def _(sp):
            sp.dma_start(sim[:], io["em_sim"]).then_inc(loaded, 16)
            sp.dma_start(gates[:], io["em_gates"]).then_inc(loaded, 16)
            sp.dma_start(before[:], io["before32"]).then_inc(loaded, 16)
            sp.dma_start(w[:], io["em_w"]).then_inc(loaded, 16)
            with sp.Fori(0, NG) as it:
                sp.wait_ge(x_ok, it * G + G)
                sp.dma_start(io["out"][bass.ds(it * G, G)].rearrange("b t d -> t b d"),
                             x[:, bass.ds(it * G, G), :]).then_inc(stored, 16)
            sp.wait_ge(stored, 16 * NG)

        @block.gpsimd
        def _(pool):
            nc.gpsimd.memset(ones[:], 1.0).then_inc(const_ok, 1)
            nc.gpsimd.memset(minus_half[:], -0.5).then_inc(const_ok, 1)
            with pool.Fori(0, NG) as it:
                norm.pool_rstd(pool, it)
            pool.wait_ge(rn_in, 2)
            pool.wait_ge(const_ok, 2)
            nc.gpsimd.tensor_tensor(simn[:], simn[:], minus_half[:], ALU.pow).then_inc(rn_ok, 1)
            nc.gpsimd.tensor_tensor(repn[:], repn[:], minus_half[:, 0:1], ALU.pow).then_inc(rn_ok, 1)

        @block.tensor
        def _(pe):
            with pe.Fori(0, NG) as it:
                pe.wait_ge(rep_ok, ONE + it)
                norm.tensor_transpose(pe, it)
            pe.wait_ge(rep_ok, ONE + NG + 3)
            pe.wait_ge(const_ok, 2)
            aff, s2, r2 = banks[2][0:NB, 0:E], banks[3][0:NB, 0:E], banks[4][0:NB, 0:1]
            for c in range(DC):
                nc.tensor.matmul(aff, rep[:, c, :], sim[:, c, :], start=(c == 0), stop=(c == DC - 1))
            for c in range(DC):
                nc.tensor.matmul(s2, ones[:], sim2[:, c, :], start=(c == 0), stop=(c == DC - 1))
            for c in range(DC):
                last = nc.tensor.matmul(r2, rep2[:, c, :], ones[:, 0:1], start=(c == 0), stop=(c == DC - 1))
            last.then_inc(aff_ps, 1)
            pe.wait_ge(r_ok, 1)
            nc.tensor.transpose(banks[5][:, 0:NB], route[:].rearrange("p r e -> p (r e)"),
                                pr.ident[0:NB, 0:NB]).then_inc(rT_ps, 1)
            pe.wait_ge(loaded, 64)
            pe.wait_ge(rT_ok, 1)
            for half in range(2):
                for n in range(NW // 2):
                    for g in range(4):
                        rows = slice(32 * g, 32 * g + 32)
                        last = nc.tensor.matmul(banks[2 * g + half][:, n * NB:(n + 1) * NB],
                                                w[rows, half * (NW // 2) + n, :], routeT[rows, :],
                                                start=True, stop=True)
                last.then_inc(mix_ps, 1)
            pe.wait_ge(mixv_ok, 2 * DC)
            pe.wait_ge(mixo_ok, 2 * 2)
            pe.wait_ge(mix_ps, 2)

            def hidden(b):
                if b >= 2:
                    pe.wait_ge(h_ok, b - 1)
                for c in range(DC):
                    last = nc.tensor.matmul(banks[b % 2][:, 0:P], wvT[:, c, b].rearrange("p e h -> p (e h)"),
                                            xT[:, c, b, :], start=(c == 0), stop=(c == DC - 1))
                last.then_inc(h_ps, 1)

            def outputs(b):
                pe.wait_ge(h_ok, b + 1)
                if b >= 2:
                    pe.wait_ge(x_ok, b - 1)
                for e in range(2):
                    rows = slice(H * e, H * e + H)
                    last = nc.tensor.matmul(banks[2 + 2 * (b % 2) + e][:, 0:P], hT[rows, b % 2, :],
                                            wo[rows, b, :], start=True, stop=True)
                last.then_inc(o_ps, 1)

            hidden(0)
            for b in range(NB):
                if b + 1 < NB:
                    hidden(b + 1)
                outputs(b)

        @block.scalar
        def _(act):
            with act.Fori(0, NG) as it:
                for c in range(DC):
                    act.wait_ge(norm.s_tr, it * DC + c + 1)
                    nc.scalar.copy(xT[:, c, bass.ds(it * G, G), :],
                                   banks[c][:, :].rearrange("p (j t) -> p j t", j=G)).then_inc(xT_ok, 1)
            act.wait_ge(loaded, 64)
            nc.scalar.activation(sig[:], gates[:], ACT.Exp, scale=-1.0).then_inc(sig_ok, 1)
            act.wait_ge(exp_in, 1)
            nc.scalar.activation(gated[:], gated[:], ACT.Exp, bias=small[:, 2:3],
                                 accum_out=small[:, 3:4]).then_inc(exp_ok, 1)
            for half in range(2):
                act.wait_ge(mix_ps, half + 1)
                for g in range(DC):
                    cols = slice(half * (NW // 2), (half + 1) * (NW // 2))
                    src = banks[2 * g + half][:, :].rearrange("p (n b) -> p b n", b=NB)
                    nc.scalar.copy(wvT[:, g, :, 0, cols], src)
                    nc.scalar.copy(wvT[:, g, :, 1, cols], src).then_inc(mixv_ok, 1)
            for b in range(NB):
                act.wait_ge(h_ps, b + 1)
                if b >= 2:
                    act.wait_ge(o_ps, b - 1)
                nc.scalar.copy(hT[:, b % 2, :], banks[b % 2][:, 0:P]).then_inc(h_ok, 1)

        @block.vector
        def _(dve):
            dve.sem_inc(rep_ok, ONE)
            with dve.Fori(0, NG) as it:
                norm.vector_norm(dve, it)
                for c in range(DC):
                    dve.wait_ge(xT_ok, it * DC + c + 1)
                    last = nc.vector.tensor_reduce(rep[:, c, bass.ds(it * G, G)],
                                                   banks[c][:, :].rearrange("p (j t) -> p j t", j=G), AX, ALU.add)
                last.then_inc(rep_ok, 1)
            chain = Chain(dve, chain_s, 0, 21)
            dve.wait_ge(loaded, 64)
            dve.wait_ge(rep_ok, ONE + NG)
            chain.done(nc.vector.tensor_scalar(rep[:], rep[:], 1.0 / P, None, ALU.mult))
            nc.vector.tensor_tensor(rep2[:], rep[:], rep[:], ALU.mult).then_inc(rep_ok, 1)
            nc.vector.tensor_tensor(sim2[:], sim[:], sim[:], ALU.mult).then_inc(rep_ok, 1)
            dve.wait_ge(sig_ok, 1)
            chain.done(nc.vector.tensor_scalar(sig[:], sig[:], 1.0, None, ALU.add))
            nc.vector.reciprocal(sig[:], sig[:]).then_inc(rep_ok, 1)
            dve.wait_ge(aff_ps, 1)
            nc.vector.tensor_copy(simn[:], banks[3][0:NB, 0:E]).then_inc(rn_in, 1)
            nc.vector.tensor_copy(repn[:], banks[4][0:NB, 0:1]).then_inc(rn_in, 1)
            dve.wait_ge(rn_ok, 2)
            chain.done(nc.vector.tensor_scalar(logit[:], banks[2][0:NB, 0:E], repn[:, 0:1], None, ALU.mult))
            chain.done(nc.vector.tensor_tensor(logit[:], logit[:], simn[:], ALU.mult))
            chain.done(nc.vector.tensor_tensor(logit[:], logit[:], sig[:], ALU.subtract))
            chain.done(nc.vector.tensor_scalar(gated[:], logit[:], 0.0, None, ALU.max))
            chain.done(nc.vector.tensor_scalar(act_mask[:], gated[:], 0.0, None, ALU.is_gt))
            chain.done(nc.vector.tensor_reduce(small[:, 0:1], act_mask[:], AX, ALU.add))
            chain.done(nc.vector.tensor_scalar(small[:, 1:2], small[:, 0:1], 0.0, None, ALU.is_equal))
            ahead = logit[:].unsqueeze(1).to_broadcast([NB, E, E])
            self_ = logit[:].unsqueeze(2).to_broadcast([NB, E, E])
            nc.vector.tensor_tensor(more[:], ahead, self_, ALU.is_gt)
            chain.done(nc.vector.tensor_tensor(tied[:], ahead, self_, ALU.is_equal))
            chain.done(nc.vector.tensor_tensor(tied[:], tied[:], before[:], ALU.mult))
            chain.done(nc.vector.tensor_tensor(more[:], more[:], tied[:], ALU.add))
            chain.done(nc.vector.tensor_reduce(rank[:], more[:], AX, ALU.add))
            chain.done(nc.vector.tensor_scalar(rank[:], rank[:], K - 0.5, small[:, 1:2], ALU.is_lt, ALU.mult))
            chain.done(nc.vector.tensor_tensor(act_mask[:], act_mask[:], rank[:], ALU.max))
            chain.done(nc.vector.tensor_tensor(gated[:], gated[:], act_mask[:], ALU.mult))
            chain.done(nc.vector.tensor_scalar(rank[:], act_mask[:], 1.0, BIG, ALU.subtract, ALU.mult))
            chain.done(nc.vector.tensor_tensor(gated[:], gated[:], rank[:], ALU.add))
            chain.done(nc.vector.tensor_reduce(small[:, 1:2], gated[:], AX, ALU.max))
            nc.vector.tensor_scalar(small[:, 2:3], small[:, 1:2], -1.0, None, ALU.mult).then_inc(exp_in, 1)
            dve.wait_ge(exp_ok, 1)
            chain.done(nc.vector.reciprocal(small[:, 4:5], small[:, 3:4]))
            for n in range(4):
                last = nc.vector.tensor_scalar(route[:, n, :], gated[:], small[:, 4:5], None, ALU.mult)
            chain.done(last)
            for n in range(2):
                last = nc.vector.tensor_tensor(route[:, n, :], route[:, n, :], act_mask[:], ALU.mult)
            last.then_inc(r_ok, 1)
            chain.close()
            dve.wait_ge(rT_ps, 1)
            nc.vector.tensor_copy(routeT[:], banks[5][:, 0:NB]).then_inc(rT_ok, 1)
            for half in range(2):
                dve.wait_ge(mix_ps, half + 1)
                for g in range(2):
                    cols = slice(g * NW + half * (NW // 2), g * NW + (half + 1) * (NW // 2))
                    nc.vector.tensor_copy(wo[:, :, cols], banks[4 + 2 * g + half][:, :]
                                          .rearrange("p (n b) -> p b n", b=NB)).then_inc(mixo_ok, 1)
            for b in range(NB):
                dve.wait_ge(o_ps, b + 1)
                for e in range(2):
                    cols = slice(e * P, (e + 1) * P)
                    last = nc.vector.tensor_tensor(x[:, b, cols], banks[2 + 2 * (b % 2) + e][:, 0:P], x[:, b, cols],
                                                   ALU.add)
                last.then_inc(x_ok, 1)


def store_output(pr):
    nc, io = pr.nc, pr.io
    stored = pr.sem("stored")
    with nc.Block() as block:
        @block.sync
        def _(sp):
            sp.dma_start(io["out"].rearrange("b t d -> t b d"), pr.x[:]).then_inc(stored, 16)
            sp.wait_ge(stored, 16)


def build(nc, io, stages):
    pr = Program(nc, io)
    with ExitStack() as ctx:
        pr.x = ctx.enter_context(nc.sbuf_tensor("x", [P, NB, D], F32))
        pr.ident = ctx.enter_context(nc.sbuf_tensor("ident", [P, P], F32))
        pr.wait_slot = ctx.enter_context(nc.sbuf_tensor("wait_slot", [1, 1], F32))
        pr.minus_half = ctx.enter_context(nc.sbuf_tensor("minus_half", [P, G], F32))
        pr.ones_row = ctx.enter_context(nc.sbuf_tensor("ones_row", [1, P], F32R))
        pr.ones_row32 = ctx.enter_context(nc.sbuf_tensor("ones_row32", [1, P], F32))
        pr.banks = [ctx.enter_context(nc.psum_tensor(f"bank{n}", [P, 512], F32)) for n in range(8)]
        pr.x_loaded = pr.sem("x_loaded")
        pr.const_ok = pr.sem("consts_ready")
        for stage in STAGES[:stages]:
            stage(pr)
            if stage is not STAGES[-1]:
                pr.release_semaphores()
        if stages < len(STAGES):
            store_output(pr)


STAGES = [stage_lora_attention, stage_long_conv, stage_experts_and_wide_attention,
          stage_linear_attention, stage_expert_mix]


def kernel(**inputs):
    import numpy as np
    import concourse.bacc as bacc
    from concourse.bass_utils import run_bass_kernel_spmd

    a = {n: np.asarray(v) for n, v in inputs.items()}

    def chunks(w):
        return w.reshape(DC, P, -1).transpose(1, 0, 2)

    r = {}
    r["x"] = a["x"]
    r["ident"] = np.eye(P, dtype=np.float32)
    odd = (np.arange(P) // 16) % 2
    r["parity"] = np.stack([1 - odd, odd], axis=1).astype(np.float32)
    qkvo = "qkvo"
    r["l0_w"] = np.stack([chunks(a[f"L0_attn_W{n}"].T) for n in qkvo], axis=1)
    r["l0_a"] = np.stack([a[f"L0_attn_A{n}"].T for n in qkvo], axis=1)
    r["l0_b"] = np.stack([a[f"L0_attn_B{n}"] for n in qkvo], axis=1)
    r["l0_qk_bias"] = np.stack([a["L0_attn_bq"].reshape(DC, P).T, a["L0_attn_bk"].reshape(DC, P).T], axis=1)
    r["l0_vo_bias"] = np.stack([a["L0_attn_bv"], a["L0_attn_bo"]])[None]

    r["ctx_rev"] = a["ctx_2048"].transpose(2, 0, 1).reshape(DC, P, NB, P)[:, ::-1].transpose(1, 0, 2, 3)
    kpad = np.concatenate([np.zeros((16, P - 1), np.float32), a["L0_xattn_ssm_kernel"]], axis=1)
    r["toeplitz"] = np.lib.stride_tricks.sliding_window_view(kpad, 2 * P, axis=1).transpose(1, 0, 2)
    r["conv_d"] = np.broadcast_to(a["L0_xattn_D"], (P, 16))
    r["anti"] = np.eye(P, dtype=np.float32)[::-1]
    r["le_w"] = np.concatenate([chunks(a["L0_ffn_W"].T), chunks(a["L0_ffn_A"].reshape(P, D).T),
                                chunks(a["L0_ffn_gate_w"].T)], axis=2)
    r["le_u"] = a["L0_ffn_B"].transpose(0, 2, 1).reshape(P, D)
    r["before8"] = np.broadcast_to(np.tril(np.ones((8, 8), np.float32), -1), (P, 8, 8))
    wide = [chunks(a[f"L1_attn_W_{n}"].reshape(-1, D).T).reshape(P, -1) for n in "QKV"]
    wide.append(a["L1_attn_W_O"].T.reshape(16, P, D).transpose(1, 0, 2).reshape(P, -1))
    r["wide_w"] = np.stack(wide)
    r["causal"] = np.tile(np.triu(np.full((P, P), -1e30, np.float32), 1), (1, G)).astype(mybir.dt.np(BF16))
    r["ident_b"] = np.eye(P, dtype=np.float32).astype(mybir.dt.np(BF16))

    by_head = lambda w: w.reshape(16, 16, D).transpose(1, 0, 2)
    reverse = lambda t: t.reshape(DC, P, -1)[:, ::-1].transpose(1, 0, 2)
    wk = a["L1_xattn_Wk"].reshape(D, DC, P)[:, :, ::-1].reshape(D, D)
    r["li_wqk"] = np.stack([by_head(a["L1_xattn_Wq"]), by_head(wk)], axis=1)
    r["li_wf"] = np.stack([np.tile(a[f"L1_xattn_W{n}f"].T, (1, 2)) for n in "qk"], axis=1)
    r["li_bqk"] = np.stack([a[f"L1_xattn_b{n}"].reshape(16, 16).T for n in "qk"], axis=1)
    r["li_vo"] = np.stack([reverse(a["L1_xattn_Wv"].T), chunks(a["L1_xattn_Wo"].T)], axis=1)
    r["li_vo_row"] = np.stack([a["L1_xattn_bv"], a["L1_xattn_bo"]])[None]
    r["li_mask"] = a["mask_BxS2_ff1"].T
    wv = a["L1_ffn_w_v"].reshape(32, 64, DC, P).transpose(2, 0, 1, 3)
    wo = a["L1_ffn_o_weights"].reshape(32, 64, 2, 2, 64)
    wo = wo.transpose(3, 0, 4, 2, 1).reshape(2, 32, 64, P)
    r["em_w"] = np.concatenate([wv, wo]).reshape(P, 64, P)
    r["em_sim"] = chunks(a["L1_ffn_sim_matrix"])
    r["em_gates"] = np.broadcast_to(a["L1_ffn_gates"], (NB, 32))
    r["before32"] = np.broadcast_to(np.tril(np.ones((32, 32), np.float32), -1), (NB, 32, 32))

    nc = bacc.Bacc("TRN2", target_bir_lowering=False, num_devices=1)
    arrays, io = {}, {}
    for name, v in r.items():
        v = np.ascontiguousarray(v)
        arrays[f"in_{name}"] = v
        io[name] = nc.dram_tensor(f"in_{name}", v.shape, mybir.dt.from_np(v.dtype), kind="ExternalInput").ap()
    io["out"] = nc.dram_tensor("out_x", (NB, P, D), F32, kind="ExternalOutput").ap()
    build(nc, io, len(STAGES))
    got = run_bass_kernel_spmd(nc, [arrays], core_ids=[0])
    return got.results[0]["out_x"]
```

```python
from contextlib import ExitStack

import concourse.bass as bass
from concourse import mybir

F32 = mybir.dt.float32
F32R = mybir.dt.float32r
BF16 = mybir.dt.bfloat16
ALU = mybir.AluOpType
ACT = mybir.ActivationFunctionType
AX = mybir.AxisListType.X

P = 128
NB = 16
G = 4
NG = NB // G
D = 256
DC = D // P
GT = G * P
EPS = 1e-5
ONE = 1
BASE = 2


class Chain:

    def __init__(self, eng, sem, it, per):
        self.eng, self.sem, self.it, self.per, self.n = eng, sem, it, per, 0

    def done(self, ins):
        self.n += 1
        ins.then_inc(self.sem, 1)
        self.eng.wait_ge(self.sem, self.it * self.per + self.n)

    def close(self):
        assert self.n == self.per, (self.n, self.per)


def product(nc, out, a, b, start, stop):
    nc.tensor.matmul(out, a[0], b[0], start=start, stop=False, skip_group_check=True)
    nc.tensor.matmul(out, a[0], b[1], start=False, stop=False, skip_group_check=True)
    return nc.tensor.matmul(out, a[1], b[0], start=False, stop=stop, skip_group_check=True)


def pair(t, *index):
    return t[0][index], t[1][index]


class Program:
    def __init__(self, nc, io):
        self.nc, self.io = nc, io
        self.sems = []

    def sem(self, name):
        self.sems.append(self.nc.alloc_semaphore(name=name))
        return self.sems[-1]

    def release_semaphores(self):
        self.nc.clear_and_free_semaphores(self.sems)
        self.nc.all_engine_barrier()
        self.sems = []


class Norm:

    def __init__(self, pr, ctx, st, banks, name, split=True):
        nc = pr.nc
        self.nc, self.pr, self.banks, self.split = nc, pr, banks, split
        sb = lambda n, shape, dt: ctx.enter_context(nc.sbuf_tensor(f"{name}_{n}", shape, dt))
        self.stats = sb("stats", [P, G, 6], F32)
        self.meanvar = sb("meanvar", [P, G, 2], F32)
        self.rstd = sb("rstd", [P, G], F32)
        self.xn = sb("xn", [P, G, D], F32)
        if split:
            self.xT = (sb("xT_hi", [P, DC, GT], F32R), sb("xT_lo", [P, DC, GT], F32R))
        else:
            self.xT = sb("xT", [P, DC, GT], F32)
        self.s_chain = pr.sem(f"{name}_norm_chain")
        self.s_var = pr.sem(f"{name}_var_ready")
        self.s_pool = pr.sem(f"{name}_rstd_ready")
        self.s_xn = pr.sem(f"{name}_xn_ready")
        self.s_tr = pr.sem(f"{name}_xT_in_psum")
        self.s_hi = pr.sem(f"{name}_xT_hi_ready")
        self.s_lo = pr.sem(f"{name}_xT_ready")

    def vector_norm(self, dve, it):
        self.vector_stats(dve, it)
        self.vector_apply(dve, it)

    def vector_stats(self, dve, it):
        nc, x = self.nc, self.pr.x
        chain = Chain(dve, self.s_chain, it, 2)
        for j in range(G):
            last = nc.vector.bn_stats(self.stats[:, j, :], x[:, it * G + j, :])
        chain.done(last)
        nc.vector.memset(self.pr.wait_slot[:], 0.0)
        for j in range(G):
            last = nc.vector.bn_aggr(self.meanvar[:, j, :], self.stats[:, j, :])
        chain.done(last)
        chain.close()
        nc.vector.tensor_scalar(self.rstd[:], self.meanvar[:, :, 1], EPS, None, ALU.add).then_inc(self.s_var, 1)

    def vector_apply(self, dve, it):
        nc, x = self.nc, self.pr.x
        dve.wait_ge(self.s_pool, it + 1)
        for j in range(G):
            last = nc.vector.tensor_scalar(self.xn[:, j, :], x[:, it * G + j, :], self.meanvar[:, j, 0:1],
                                           self.rstd[:, j:j + 1], ALU.subtract, ALU.mult)
        last.then_inc(self.s_xn, 1)

    def pool_rstd(self, pool, it):
        pool.wait_ge(self.s_var, it + 1)
        self.nc.gpsimd.tensor_tensor(self.rstd[:], self.rstd[:], self.pr.minus_half[:], ALU.pow)\
            .then_inc(self.s_pool, 1)

    def tensor_transpose(self, pe, it):
        pe.wait_ge(self.s_xn, it + 1)
        for c in range(DC):
            for j in range(G):
                last = self.nc.tensor.transpose(self.banks[c][:, j * P:(j + 1) * P],
                                                self.xn[:, j, c * P:(c + 1) * P], self.pr.ident[:])
            last.then_inc(self.s_tr, 1)

    def scalar_hi(self, act, it):
        for c in range(DC):
            act.wait_ge(self.s_tr, it * DC + c + 1)
            out = self.xT[0] if self.split else self.xT
            self.nc.scalar.copy(out[:, c, :], self.banks[c][:, :]).then_inc(self.s_hi, 1)

    def vector_lo(self, dve, it):
        for c in range(DC):
            dve.wait_ge(self.s_hi, it * DC + c + 1)
            self.nc.vector.tensor_tensor(self.xT[1][:, c, :], self.banks[c][:, :],
                                         self.xT[0][:, c, :].bitcast(F32), ALU.subtract).then_inc(self.s_lo, 1)


def stage_lora_attention(pr):
    nc, io, x, banks = pr.nc, pr.io, pr.x, pr.banks
    H, HD, R = 16, 16, 16
    RG = 4
    U = G * RG
    LORA = 0.5
    SCALE = HD ** -0.5
    b_p, b_s, b_t, b_v = banks[0:2], banks[2:6], banks[6], banks[7]
    with ExitStack() as ctx:
        sb = lambda n, shape, dt=F32: ctx.enter_context(nc.sbuf_tensor(f"la_{n}", shape, dt))
        sem = lambda n: pr.sem(f"la_{n}")
        norm = Norm(pr, ctx, None, b_p, "la")
        w_raw = sb("w_raw", [P, 4, DC, D])
        lora_a = sb("lora_a", [R, 4, D])
        lora_b = sb("lora_b", [R, 4, D])
        w = (sb("w_hi", [P, 4, DC, D], F32R), sb("w_lo", [P, 4, DC, D], F32R))
        qk_bias = sb("qk_bias", [P, 2, DC])
        v_bias = sb("v_bias", [P, DC])
        out_bias = sb("out_bias", [P, D])
        parity = sb("parity", [P, 2])
        q = sb("q", [P, 2, DC, GT])
        k = sb("k", [P, DC, GT])
        DIAG = P + HD
        v = sb("v", [P, 2, G * H * P + P])
        negmax = sb("negmax", [P, 2, 4])
        sums = sb("sums", [P, 2, H])
        rsum = sb("rsum", [P, 2, H])
        prob = sb("prob", [P, 2, 4, P])
        probT = sb("probT", [P, 2, 4, P])
        o = sb("o", [P, 2, D])
        oT = (sb("oT_hi", [P, 2, DC, P], F32R), sb("oT_lo", [P, 2, DC, P], F32R))

        loaded = sem("weights_loaded")
        w_ps, w_f32, w_hi, w_lo = sem("w_in_psum"), sem("w_f32"), sem("w_hi"), sem("w_ready")
        bias_ps, bias_ok, xb_ok = sem("bias_in_psum"), sem("bias_ready"), sem("x_biased")
        q_ps, q_ok = sem("q_in_psum"), sem("q_ready")
        k_ps, k_ok = sem("k_in_psum"), sem("k_ready")
        v_ps, v_ok = sem("v_in_psum"), sem("v_ready")
        s_ps, max_ok, exp_ok = sem("scores_in_psum"), sem("negmax_ready"), sem("probs_ready")
        t_ps, t_ok = sem("probsT_in_psum"), sem("probsT_ready")
        av_ps, av_ok = sem("av_in_psum"), sem("o_ready")
        ot_ps, ot_hi, ot_lo = sem("oT_in_psum"), sem("oT_hi_ready"), sem("oT_ready")
        o_ps, x_ok = sem("out_in_psum"), sem("x_updated")
        chain_s = sem("vector_chain")
        v_zero = sem("v_cleared")
        NLOAD = 8
        block = ctx.enter_context(nc.Block())

        T_STATS, T_APPLY, T_TURN, T_V, T_Q, T_K = 2, 4, 7, 8, 11, 12
        TURN_O, PROJECT = 5, 6

        def head(r, s):
            return (s // 2) * 8 + 2 * r + s % 2

        def due(u, first):
            return (u - first) // RG if u >= first and (u - first) % RG == 0 else None

        def load_x(eng, t):
            eng.dma_start(x[:, t * G:(t + 1) * G, :],
                          io["x"][t * G:(t + 1) * G].rearrange("b t d -> t b d")).then_inc(pr.x_loaded[t], 16)

        @block.sync
        def _(sp):
            load_x(sp, 0)
            sp.dma_start(w_raw[:], io["l0_w"]).then_inc(loaded, 16)
            for t in range(1, NG):
                load_x(sp, t)

        @block.gpsimd
        def _(pool):
            nc.gpsimd.memset(pr.minus_half[:], -0.5).then_inc(pr.const_ok, 1)
            nc.gpsimd.memset(pr.ones_row32[:], 1.0).then_inc(pr.const_ok, 1)
            pool.wait_ge(pr.const_ok, 2)
            nc.gpsimd.tensor_copy(pr.ones_row[:], pr.ones_row32[:]).then_inc(pr.const_ok, 1)
            norm.pool_rstd(pool, 0)
            for n in range(2):
                nc.gpsimd.memset(v[:, n, :], 0.0).then_inc(v_zero, 1)
            pool.wait_ge(bias_ok, 1)

            def add_bias(it):
                pool.wait_ge(norm.s_xn, it + 1)
                nc.gpsimd.tensor_tensor(x[:, bass.ds(it * G, G), :], x[:, bass.ds(it * G, G), :],
                                        out_bias[:].unsqueeze(1).to_broadcast([P, G, D]), ALU.add).then_inc(xb_ok, 1)

            add_bias(0)
            with pool.Fori(1, NG) as it:
                norm.pool_rstd(pool, it)
                add_bias(it)

        @block.tensor
        def _(pe):
            xT = norm.xT

            def q_or_k(it, n, done):
                for m in range(DC):
                    if n == 0:
                        pe.wait_ge(norm.s_lo, it * DC + DC)
                        pe.wait_ge(v_ok, it * 2 + m + 1)
                    else:
                        pe.wait_ge(q_ok, it * DC + m + 1)
                    for c in range(DC):
                        last = product(nc, b_p[m][:, :], pair(w, slice(None), n, c, slice(m * P, m * P + P)),
                                       pair(xT, slice(None), c), c == 0, c == DC - 1)
                    last.then_inc(done, 1)

            def values(it):
                pe.wait_ge(norm.s_lo, it * DC + DC)
                for half in range(2):
                    for jj in range(2):
                        j = 2 * half + jj
                        for c in range(DC):
                            last = product(nc, b_p[half][:, jj * D:(jj + 1) * D],
                                           pair(xT, slice(None), c, slice(j * P, j * P + P)),
                                           pair(w, slice(None), 2, c), jj == 0 and c == 0, c == DC - 1)
                    last.then_inc(v_ps, 1)

            def scores(it, u):
                for s in range(4):
                    for d in range(2):
                        j, r = divmod((u + d) % U, RG)
                        if s == 0:
                            pe.wait_ge(exp_ok, it * U + u + d + 1)
                        rows = slice(32 * r, 32 * r + 32)
                        m, e = divmod(s, 2)
                        last = nc.tensor.matmul(b_s[r][:, s * P:(s + 1) * P],
                                                q[rows, e, m, j * P:(j + 1) * P],
                                                k[rows, m, j * P:(j + 1) * P], start=True, stop=True)
                        if s == 3:
                            last.then_inc(s_ps, 1)

            def turn(it, u):
                pe.wait_ge(exp_ok, RG + it * U + u + 1)
                pe.wait_ge(t_ok, ONE + it * U + u)
                for s in range(4):
                    last = nc.tensor.transpose(b_t[:, s * P:(s + 1) * P], prob[:, u % 2, s, :], pr.ident[:])
                last.then_inc(t_ps, 1)

            def weigh(it, u):
                j, r = divmod(u, RG)
                pe.wait_ge(t_ok, ONE + it * U + u + 1)
                if r == 0:
                    pe.wait_ge(av_ok, BASE + it * G + j)
                for s in range(4):
                    at = (j * H + head(r, s)) * P
                    last = nc.tensor.matmul(b_v[:, s // 2 * P:(s // 2 + 1) * P], probT[:, u % 2, s, :],
                                            v[:, it % 2, at:at + P], start=(r == 0 and s == 0),
                                            stop=(r == RG - 1), skip_group_check=True)
                last.then_inc(av_ps, 1)

            def turn_o(it, j, last):
                pe.wait_ge(av_ok, BASE + it * G + j + 1)
                pe.wait_ge(ot_lo, ONE + it * G + j)
                if not last and j in (1, 2):
                    pe.wait_ge((v_ok, k_ok)[j - 1], (it + 1) * 2 + 1)
                for c in range(DC):
                    ins = nc.tensor.transpose(b_p[0][:, c * P:(c + 1) * P], o[:, j % 2, c * P:(c + 1) * P],
                                              pr.ident[:])
                ins.then_inc(ot_ps, 1)

            def project(it, j, last):
                pe.wait_ge(ot_lo, ONE + it * G + j + 1)
                pe.wait_ge(x_ok, ONE + it * G + j)
                if not last and j in (1, 2):
                    pe.wait_ge((v_ok, k_ok)[j - 1], (it + 1) * 2 + 2)
                for c in range(DC):
                    ins = product(nc, b_p[1][:, 0:D], pair(oT, slice(None), j % 2, c), pair(w, slice(None), 3, c),
                                  c == 0, c == DC - 1)
                ins.then_inc(o_ps, 1)

            def group(it, last):
                for u in range(U + 3):
                    if u < U:
                        turn(it, u)
                    if u % 2 == 1 and u < U and (u + 4 < U or not last):
                        if u + 3 == U:
                            pe.wait_ge(q_ok, (it + 1) * DC + DC)
                            pe.wait_ge(k_ok, (it + 1) * DC + DC)
                        scores(it, u + 3)
                    if 1 <= u <= U:
                        weigh(it, u - 1)
                    if due(u, TURN_O) is not None:
                        turn_o(it, due(u, TURN_O), last)
                    if due(u, PROJECT) is not None:
                        project(it, due(u, PROJECT), last)
                    if last:
                        continue
                    if u == T_TURN:
                        pe.wait_ge(x_ok, ONE + it * G + 1)
                        norm.tensor_transpose(pe, it + 1)
                    if u == T_V:
                        values(it + 1)
                    if u == T_Q:
                        pe.wait_ge(x_ok, ONE + it * G + 2)
                        q_or_k(it + 1, 0, q_ps)
                    if u == T_K:
                        q_or_k(it + 1, 1, k_ps)

            pe.wait_ge(loaded, 16 * NLOAD)
            pe.wait_ge(pr.const_ok, 3)
            for n in range(4):
                for c in range(DC):
                    last = nc.tensor.matmul(b_s[n][:, c * D:(c + 1) * D], lora_b[:, n, c * P:(c + 1) * P],
                                            lora_a[:, n, :], start=True, stop=True)
                last.then_inc(w_ps, 1)
            norm.tensor_transpose(pe, 0)
            pe.wait_ge(w_f32, 4)
            for c in range(DC):
                last = nc.tensor.matmul(b_t[:, 0:D], v_bias[:, c:c + 1].to_broadcast([P, P]), w_raw[:, 3, c, :],
                                        start=(c == 0), stop=(c == DC - 1))
            last.then_inc(bias_ps, 1)
            for event in (t_ps, av_ps, ot_ps, o_ps):
                pe.sem_inc(event, BASE)
            pe.wait_ge(w_lo, 4)
            values(0)
            q_or_k(0, 0, q_ps)
            q_or_k(0, 1, k_ps)
            pe.wait_ge(q_ok, DC)
            pe.wait_ge(k_ok, DC)
            scores(0, 0)
            scores(0, 2)
            with pe.Fori(0, NG - 1) as it:
                group(it, False)
            group(NG - 1, True)

        @block.scalar
        def _(act):
            act.dma_start(lora_b[:], io["l0_b"]).then_inc(loaded, 16)
            act.dma_start(lora_a[:], io["l0_a"]).then_inc(loaded, 16)
            act.dma_start(pr.ident[:], io["ident"]).then_inc(loaded, 16)
            act.dma_start(v_bias[:], io["l0_v_bias"]).then_inc(loaded, 16)
            act.dma_start(out_bias[:], io["l0_o_bias"]).then_inc(loaded, 16)
            act.dma_start(qk_bias[:], io["l0_qk_bias"]).then_inc(loaded, 16)
            act.dma_start(parity[:], io["parity"]).then_inc(loaded, 16)

            def keep_k(it):
                for m in range(DC):
                    act.wait_ge(k_ps, it * DC + m + 1)
                    nc.scalar.activation(k[:, m, :], b_p[m][:, :], ACT.Identity,
                                         bias=qk_bias[:, 1, m:m + 1]).then_inc(k_ok, 1)

            def keep_v(it):
                for half in range(2):
                    act.wait_ge(v_ps, it * 2 + half + 1)
                    for jj in range(2):
                        for m in range(DC):
                            at = ((2 * half + jj) * H + 8 * m) * P
                            src = b_p[half][:, jj * D + m * P:jj * D + m * P + P]
                            last = nc.scalar.copy(
                                v[:, it % 2, at:at + 8 * DIAG].rearrange("p (h s) -> p h s", s=DIAG)[:, :, 0:HD],
                                src.rearrange("p (h d) -> p h d", d=HD))
                    last.then_inc(v_ok, 1)

            def exps(it, u):
                n = it * U + u
                j, r = divmod(u % U, RG)
                act.wait_ge(max_ok, n + 1)
                act.wait_ge(t_ps, BASE + n - 1)
                if r == 0:
                    act.wait_ge(av_ok, BASE + it * G + u // RG - 1)
                for s in range(4):
                    h = head(r, s)
                    last = nc.scalar.activation(prob[:, u % 2, s, :], b_s[r][:, s * P:(s + 1) * P], ACT.Exp,
                                                bias=negmax[:, u % 2, s:s + 1], scale=SCALE,
                                                accum_out=sums[:, j % 2, h:h + 1])
                last.then_inc(exp_ok, 1)

            def group(it, last):
                for u in range(U + 2):
                    if u + 1 < U or (u + 1 == U and not last):
                        exps(it, u + 1)
                    j = due(u, TURN_O)
                    if j is not None:
                        act.wait_ge(ot_ps, BASE + it * G + j + 1)
                        nc.scalar.copy(oT[0][:, j % 2, :, :],
                                       b_p[0][:, 0:D].rearrange("p (c t) -> p c t", c=DC)).then_inc(ot_hi, 1)
                    if last:
                        continue
                    if u == T_TURN:
                        norm.scalar_hi(act, it + 1)
                    if u == T_V:
                        keep_v(it + 1)
                    if u == T_K:
                        keep_k(it + 1)

            act.sem_inc(exp_ok, RG)
            act.wait_ge(w_f32, 4)
            for n in range(4):
                nc.scalar.copy(w[0][:, n], w_raw[:, n]).then_inc(w_hi, 1)
            norm.scalar_hi(act, 0)
            act.wait_ge(v_zero, 2)
            keep_v(0)
            keep_k(0)
            exps(0, 0)
            with act.Fori(0, NG - 1) as it:
                group(it, False)
            group(NG - 1, True)

        @block.vector
        def _(dve):
            def keep_q(it):
                for m in range(DC):
                    dve.wait_ge(q_ps, it * DC + m + 1)
                    for e in range(2):
                        last = nc.vector.tensor_scalar(q[:, e, m, :], b_p[m][:, :], qk_bias[:, 0, m:m + 1],
                                                       parity[:, e:e + 1], ALU.add, ALU.mult)
                    last.then_inc(q_ok, 1)

            def row_max(it, u, chain):
                n = it * U + u
                dve.wait_ge(s_ps, n + 1)
                dve.wait_ge(exp_ok, RG + n - 1)
                chain.done(nc.vector.tensor_reduce(
                    negmax[:, u % 2, :], b_s[u % RG][:, :].rearrange("p (s k) -> p s k", s=4), AX, ALU.max))
                nc.vector.tensor_scalar(negmax[:, u % 2, :], negmax[:, u % 2, :], -SCALE, None, ALU.mult)\
                    .then_inc(max_ok, 1)

            def keep_probT(it, u):
                n = it * U + u
                dve.wait_ge(t_ps, BASE + n + 1)
                dve.wait_ge(av_ps, BASE + n - 1)
                nc.vector.tensor_copy(probT[:, u % 2, :, :], b_t[:, :].rearrange("p (s k) -> p s k", s=4))\
                    .then_inc(t_ok, 1)

            def normalise(it, j, chain):
                dve.wait_ge(exp_ok, RG + it * U + (j + 1) * RG)
                chain.done(nc.vector.reciprocal(rsum[:, j % 2, :], sums[:, j % 2, :]))
                dve.wait_ge(av_ps, BASE + it * U + (j + 1) * RG)
                dve.wait_ge(ot_ps, BASE + it * G + j - 1)
                nc.vector.tensor_tensor(o[:, j % 2, :].rearrange("p (h d) -> p h d", h=H),
                                        b_v[:, 0:D].rearrange("p (h d) -> p h d", h=H),
                                        rsum[:, j % 2, :].unsqueeze(2).to_broadcast([P, H, HD]), ALU.mult)\
                    .then_inc(av_ok, 1)

            def group(it, last):
                chain = Chain(dve, chain_s, it, U + G)
                chain.n = 2
                for u in range(U + 3):
                    if u + 2 < U or (u < U and not last):
                        row_max(it, u + 2, chain)
                    if u < U:
                        keep_probT(it, u)
                    if due(u, RG) is not None:
                        normalise(it, due(u, RG), chain)
                    j = due(u, TURN_O)
                    if j is not None:
                        dve.wait_ge(ot_hi, it * G + j + 1)
                        dve.wait_ge(o_ps, BASE + it * G + j - 1)
                        nc.vector.tensor_tensor(oT[1][:, j % 2, :, :],
                                                b_p[0][:, 0:D].rearrange("p (c t) -> p c t", c=DC),
                                                oT[0][:, j % 2, :, :].bitcast(F32), ALU.subtract).then_inc(ot_lo, 1)
                    j = due(u, PROJECT)
                    if j is not None:
                        if j == 0:
                            dve.wait_ge(xb_ok, it + 1)
                        dve.wait_ge(o_ps, BASE + it * G + j + 1)
                        nc.vector.tensor_tensor(x[:, it * G + j, :], b_p[1][:, 0:D], x[:, it * G + j, :],
                                                ALU.add).then_inc(x_ok, 1)
                    if last:
                        continue
                    if u == T_STATS:
                        norm.vector_stats(dve, it + 1)
                    if u == T_APPLY:
                        norm.vector_apply(dve, it + 1)
                    if u == T_TURN:
                        norm.vector_lo(dve, it + 1)
                    if u == T_Q:
                        keep_q(it + 1)
                if not last:
                    chain.n -= 2
                chain.close()

            for event in (t_ok, ot_lo, x_ok):
                dve.sem_inc(event, ONE)
            dve.sem_inc(av_ok, BASE)
            dve.wait_ge(pr.x_loaded[0], 16)
            norm.vector_norm(dve, 0)
            dve.wait_ge(loaded, 16 * NLOAD)
            for n in range(4):
                dve.wait_ge(w_ps, n + 1)
                nc.vector.scalar_tensor_tensor(w_raw[:, n], b_s[n][:, :].rearrange("p (c o) -> p c o", c=DC),
                                               LORA, w_raw[:, n], ALU.mult, ALU.add).then_inc(w_f32, 1)
            norm.vector_lo(dve, 0)
            for n in (2, 0, 1, 3):
                dve.wait_ge(w_hi, 4)
                nc.vector.tensor_tensor(w[1][:, n], w_raw[:, n], w[0][:, n].bitcast(F32), ALU.subtract)\
                    .then_inc(w_lo, 1)
            dve.wait_ge(bias_ps, 1)
            nc.vector.tensor_tensor(out_bias[:], b_t[:, 0:D], out_bias[:], ALU.add).then_inc(bias_ok, 1)
            keep_q(0)
            first = Chain(dve, chain_s, 0, 2)
            row_max(0, 0, first)
            row_max(0, 1, first)
            for t in range(1, NG):
                dve.wait_ge(pr.x_loaded[t], 16)
            with dve.Fori(0, NG - 1) as it:
                group(it, False)
            group(NG - 1, True)


def stage_long_conv(pr):
    nc, io, x, banks = pr.nc, pr.io, pr.x, pr.banks
    H, C = 16, 8
    HALF = 2
    NPAIR = C * (C + 1) // 2
    OFF = [d * C - d * (d - 1) // 2 for d in range(C)]
    BH = HALF * G * H
    HS = 3
    N = G * NPAIR
    GROUPS = [range(h, min(h + HS, H)) for h in range(0, H, HS)]
    NGR = len(GROUPS)
    b_n, b_c, b_x = banks[0:2], banks[2:6], banks[6:8]
    with ExitStack() as ctx:
        sb = lambda n, shape, dt=F32: ctx.enter_context(nc.sbuf_tensor(f"lc_{n}", shape, dt))
        sem = lambda n: pr.sem(f"lc_{n}")
        norm = Norm(pr, ctx, None, b_n, "lc", split=False)
        toep = sb("toep", [P, H, HALF * P])
        skip = sb("skip", [P, H])
        anti = sb("anti", [P, P])
        kt = sb("kt", [P, HALF, NB * H, C])
        kk = sb("kk", [P, HALF, G * H, NPAIR])
        y = sb("y", [P, 2, HALF * G * H * NPAIR])
        yq = sb("yq", [P, C, BH, C])

        loaded, kt_loaded = sem("consts_loaded"), sem("kt_loaded")
        toep_ok, kk_ok, sq_ok = sem("toeplitz_ready"), sem("kk_ready"), sem("kk_squares")
        c_ps, c_ok = sem("conv_in_psum"), sem("conv_ready")
        yq_ok, slot_ps, x_ok = sem("yq_ready"), sem("slot_turned"), sem("x_updated")
        block = ctx.enter_context(nc.Block())

        @block.sync
        def _(sp):
            sp.dma_start(kt[:], io["ctx_rev"].rearrange("p a b (h c) -> p a (b h) c", c=C)).then_inc(kt_loaded, 16)
            sp.dma_start(toep[:], io["toeplitz"]).then_inc(loaded, 16)
            sp.dma_start(skip[:], io["conv_d"]).then_inc(loaded, 16)
            sp.dma_start(anti[:], io["anti"]).then_inc(loaded, 16)

        def schedule(eng, body):
            body(0, True, False)
            with eng.Fori(1, NG - 1) as it:
                body(it, False, False)
            body(NG - 1, False, True)

        @block.gpsimd
        def _(pool):
            with pool.Fori(0, NG) as it:
                norm.pool_rstd(pool, it)

        @block.tensor
        def _(pe):
            def conv(i):
                pe.wait_ge(kk_ok, i + 1)
                pe.wait_ge(sq_ok, i + 1)
                for g, heads in enumerate(GROUPS):
                    lo_bank, hi_bank = b_c[2 * (g % 2)], b_c[2 * (g % 2) + 1]
                    pe.wait_ge(c_ok, BASE + i * NGR + g - 1)
                    for n, h in enumerate(heads):
                        cols = slice(n * N, (n + 1) * N)
                        early, late = [kk[:, half, :, :].rearrange("p (b h) n -> p b h n", h=H)[:, :, h, :]
                                       for half in range(HALF)]
                        same, across = toep[:, h, 0:P], toep[:, h, P:2 * P]
                        nc.tensor.matmul(lo_bank[:, cols], same, early, start=True, stop=True)
                        nc.tensor.matmul(hi_bank[:, cols], same, late, start=True, stop=False)
                        last = nc.tensor.matmul(hi_bank[:, cols], across, early, start=False, stop=True)
                    last.then_inc(c_ps, 1)

            def sum_slots(i):
                for s in range(C):
                    pe.wait_ge(yq_ok, i * C + s + 1)
                    for j in range(G):
                        for half in range(HALF):
                            first = (half * G + j) * H
                            last = nc.tensor.matmul(
                                b_x[j // 2][:, (j % 2) * D + half * P:(j % 2) * D + half * P + P],
                                yq[:, s, first:first + H, :], pr.ident[:], is_transpose=True,
                                start=(s == 0 and j % 2 == 0 and half == 0), stop=(s == C - 1),
                                skip_group_check=True)
                    last.then_inc(slot_ps, 1)

            def group(i, first, last):
                if not last:
                    conv(i + 1)
                if not first:
                    pe.wait_ge(x_ok, i * G)
                sum_slots(i)
                if not last:
                    norm.tensor_transpose(pe, i + 1)

            pe.wait_ge(toep_ok, 1)
            norm.tensor_transpose(pe, 0)
            conv(0)
            schedule(pe, group)

        @block.scalar
        def _(act):
            def squares(i):
                nc.scalar.activation(kk[:, :, :, 0:C], kt[:, :, bass.ds(i * (G * H), G * H), :],
                                     ACT.Square).then_inc(sq_ok, 1)

            def keep_conv(i):
                buf = y[:, i % 2, :].rearrange("p (a bh n) -> p a bh n", a=HALF, n=NPAIR)
                for g, heads in enumerate(GROUPS):
                    act.wait_ge(c_ps, i * NGR + g + 1)
                    for half in range(HALF):
                        src = b_c[2 * (g % 2) + half][:, 0:len(heads) * N]
                        dst = buf[:, half].rearrange("p (b h) n -> p h b n", h=H)[:, heads[0]:heads[-1] + 1]
                        ins = nc.scalar.copy(dst, src.rearrange("p (h b n) -> p h b n", b=G, n=NPAIR))
                    ins.then_inc(c_ok, 1)

            def group(i, first, last):
                if last:
                    return
                act.wait_ge(c_ps, (i + 1) * NGR)
                squares(i + 1)
                if not first:
                    act.wait_ge(yq_ok, i * C)
                keep_conv(i + 1)
                act.wait_ge(yq_ok, (i + 1) * C)
                norm.scalar_hi(act, i + 1)

            act.sem_inc(c_ok, BASE)
            act.wait_ge(kt_loaded, 16)
            squares(0)
            norm.scalar_hi(act, 0)
            keep_conv(0)
            schedule(act, group)

        @block.vector
        def _(dve):
            def products(i):
                own = kt[:, :, bass.ds(i * (G * H), G * H), :]
                for d in range(1, C):
                    last = nc.vector.tensor_tensor(kk[:, :, :, OFF[d]:OFF[d] + C - d], own[:, :, :, 0:C - d],
                                                   own[:, :, :, d:C], ALU.mult)
                last.then_inc(kk_ok, 1)

            def add_sums(i):
                dve.wait_ge(slot_ps, (i + 1) * C)
                for j in range(G):
                    nc.vector.tensor_tensor(x[:, i * G + j, :], b_x[j // 2][:, (j % 2) * D:(j % 2) * D + D],
                                            x[:, i * G + j, :], ALU.add).then_inc(x_ok, 1)

            def group(i, first, last):
                if not last:
                    dve.wait_ge(c_ps, (i + 1) * NGR)
                    products(i + 1)
                if not first:
                    add_sums(i - 1)
                dve.wait_ge(norm.s_hi, (i + 1) * DC)
                if not last:
                    norm.vector_norm(dve, i + 1)
                dve.wait_ge(c_ok, BASE + (i + 1) * NGR)
                yv = y[:, i % 2, :].rearrange("p (bh n) -> p bh n", n=NPAIR)
                qv = norm.xT[:].rearrange("p a (bh c) -> p (a bh) c", c=C)
                for s in range(C):
                    if not first:
                        dve.wait_ge(slot_ps, (i - 1) * C + s + 1)
                    ins = nc.vector.tensor_tensor(yq[:, s, :, s:C], yv[:, :, OFF[s]:OFF[s] + C - s],
                                                  qv[:, :, 0:C - s], ALU.mult)
                    if s > 0:
                        d = C - s
                        ins = nc.vector.tensor_tensor(yq[:, s, :, 0:s], yv[:, :, OFF[d]:OFF[d] + s],
                                                      qv[:, :, d:C], ALU.mult)
                    ins.then_inc(yq_ok, 1)
                if last:
                    add_sums(i)

            dve.wait_ge(kt_loaded, 16)
            products(0)
            dve.wait_ge(loaded, 16 * 3)
            for h in range(H):
                ins = nc.vector.scalar_tensor_tensor(toep[:, h, 0:P], anti[:], skip[:, h:h + 1],
                                                     toep[:, h, 0:P], ALU.mult, ALU.add)
            ins.then_inc(toep_ok, 1)
            norm.vector_norm(dve, 0)
            schedule(dve, group)


def stage_lora_experts(pr):
    nc, io, x, banks = pr.nc, pr.io, pr.x, pr.banks
    E, R, TOP, ALPHA = 8, 16, 2, 16.0
    W = D + E * R + E
    b_p, b_o, b_h = banks[0:2], banks[2:6], banks[6]
    with ExitStack() as ctx:
        sb = lambda n, shape, dt=F32: ctx.enter_context(nc.sbuf_tensor(f"le_{n}", shape, dt))
        sem = lambda n: pr.sem(f"le_{n}")
        norm = Norm(pr, ctx, None, b_p, "le")
        w32 = sb("w32", [P, DC, W])
        w = (sb("w_hi", [P, DC, W], F32R), sb("w_lo", [P, DC, W], F32R))
        u32 = sb("u32", [P, D])
        up = (sb("u_hi", [P, D], F32R), sb("u_lo", [P, D], F32R))
        before = sb("before", [P, E, E])
        logit = sb("logit", [P, G, E])
        stat = sb("stat", [P, 4, G])
        prob = sb("prob", [P, G, E])
        more = sb("more", [P, G, E, E])
        tied = sb("tied", [P, G, E, E])
        rank = sb("rank", [P, G, E])
        hw = sb("hw", [P, G, E * R])
        hT = (sb("hT_hi", [P, G * P], F32R), sb("hT_lo", [P, G * P], F32R))
        raw = [sb(f"raw{n}", [P, WIDE_CHUNK]) for n in range(3)]

        loaded, w_hi, w_lo = sem("weights_loaded"), sem("w_hi"), sem("w_ready")
        p_ps, d_ok, e_ok, hw_ok = sem("proj_in_psum"), sem("logits_ready"), sem("exps_ready"), sem("hw_ready")
        h_ps, h_hi, h_lo = sem("hT_in_psum"), sem("hT_hi_ready"), sem("hT_ready")
        o_ps, x_ok = sem("out_in_psum"), sem("x_updated")
        chain_s = sem("vector_chain")
        wide_in = [sem(f"wide_loaded{n}") for n in range(3)]
        wide_hi, wide_lo = sem("wide_hi"), sem("wide_ready")
        block = ctx.enter_context(nc.Block())

        pieces = [(n, at) for n in range(4) for at in range(0, WIDE_COLS, WIDE_CHUNK)]

        @block.sync
        def _(sp):
            sp.dma_start(w32[:], io["le_w"]).then_inc(loaded, 16)
            sp.dma_start(u32[:], io["le_u"]).then_inc(loaded, 16)
            sp.dma_start(before[:], io["before8"]).then_inc(loaded, 16)
            for n, (m, at) in enumerate(pieces):
                if n >= 3:
                    sp.wait_ge(wide_lo, n - 2)
                sp.dma_start(raw[n % 3][:], io["wide_w"][m, :, at:at + WIDE_CHUNK]).then_inc(wide_in[n % 3], 16)

        @block.gpsimd
        def _(pool):
            with pool.Fori(0, NG) as it:
                norm.pool_rstd(pool, it)

        @block.tensor
        def _(pe):
            pe.wait_ge(w_lo, 2)
            with pe.Fori(0, NG) as it:
                pe.wait_ge(x_ok, ONE + it * G)
                norm.tensor_transpose(pe, it)
                pe.wait_ge(norm.s_lo, it * DC + DC)
                for j in range(G):
                    for c in range(DC):
                        last = product(nc, b_o[j][:, 0:W], pair(norm.xT, slice(None), c, slice(j * P, j * P + P)),
                                       pair(w, slice(None), c), c == 0, c == DC - 1)
                    last.then_inc(p_ps, 1)
                pe.wait_ge(hw_ok, it + 1)
                for j in range(G):
                    last = nc.tensor.transpose(b_h[:, j * P:(j + 1) * P], hw[:, j, :], pr.ident[:])
                last.then_inc(h_ps, 1)
                pe.wait_ge(h_lo, it + 1)
                for j in range(G):
                    product(nc, b_o[j][:, 0:D], pair(hT, slice(None), slice(j * P, j * P + P)),
                            (up[0][:], up[1][:]), False, True).then_inc(o_ps, 1)

        def split_piece(eng, n, hi):
            m, at = pieces[n]
            dst = pr.wide[m]
            if hi:
                eng.wait_ge(wide_in[n % 3], 16 * (n // 3 + 1))
                nc.scalar.copy(dst[0][:, at:at + WIDE_CHUNK], raw[n % 3][:]).then_inc(wide_hi, 1)
            else:
                eng.wait_ge(wide_hi, n + 1)
                nc.vector.tensor_tensor(dst[1][:, at:at + WIDE_CHUNK], raw[n % 3][:],
                                        dst[0][:, at:at + WIDE_CHUNK].bitcast(F32), ALU.subtract)\
                    .then_inc(wide_lo, 1)

        @block.scalar
        def _(act):
            act.wait_ge(loaded, 48)
            nc.scalar.copy(w[0][:], w32[:]).then_inc(w_hi, 1)
            nc.scalar.copy(up[0][:], u32[:]).then_inc(w_hi, 1)
            with act.Fori(0, NG) as it:
                norm.scalar_hi(act, it)
                act.wait_ge(d_ok, it + 1)
                nc.scalar.activation(prob[:], logit[:], ACT.Exp).then_inc(e_ok, 1)
                act.wait_ge(h_ps, it + 1)
                nc.scalar.copy(hT[0][:], b_h[:, :]).then_inc(h_hi, 1)
            for n in range(len(pieces)):
                split_piece(act, n, True)

        @block.vector
        def _(dve):
            dve.wait_ge(w_hi, 2)
            nc.vector.tensor_tensor(w[1][:], w32[:], w[0][:].bitcast(F32), ALU.subtract).then_inc(w_lo, 1)
            nc.vector.tensor_tensor(up[1][:], u32[:], up[0][:].bitcast(F32), ALU.subtract).then_inc(w_lo, 1)
            dve.sem_inc(x_ok, ONE)
            with dve.Fori(0, NG) as it:
                norm.vector_norm(dve, it)
                norm.vector_lo(dve, it)
                chain = Chain(dve, chain_s, it, 15)
                per_e = lambda t: t.unsqueeze(2).to_broadcast([P, G, E])
                for j in range(G):
                    dve.wait_ge(p_ps, it * G + j + 1)
                    last = nc.vector.tensor_copy(logit[:, j, :], b_o[j][:, D + E * R:W])
                chain.done(last)
                chain.done(nc.vector.tensor_reduce(stat[:, 0, :], logit[:], AX, ALU.max))
                nc.vector.tensor_tensor(logit[:], logit[:], per_e(stat[:, 0, :]), ALU.subtract).then_inc(d_ok, 1)
                dve.wait_ge(e_ok, it + 1)
                chain.done(nc.vector.tensor_reduce(stat[:, 1, :], prob[:], AX, ALU.add))
                chain.done(nc.vector.reciprocal(stat[:, 2, :], stat[:, 1, :]))
                chain.done(nc.vector.tensor_tensor(prob[:], prob[:], per_e(stat[:, 2, :]), ALU.mult))
                ahead = [prob[:, j, :].unsqueeze(1).to_broadcast([P, E, E]) for j in range(G)]
                self_ = [prob[:, j, :].unsqueeze(2).to_broadcast([P, E, E]) for j in range(G)]
                for j in range(G):
                    nc.vector.tensor_tensor(more[:, j], ahead[j], self_[j], ALU.is_gt)
                    last = nc.vector.tensor_tensor(tied[:, j], ahead[j], self_[j], ALU.is_equal)
                chain.done(last)
                chain.done(nc.vector.tensor_tensor(
                    tied[:], tied[:], before[:].unsqueeze(1).to_broadcast([P, G, E, E]), ALU.mult))
                chain.done(nc.vector.tensor_tensor(more[:], more[:], tied[:], ALU.add))
                chain.done(nc.vector.tensor_reduce(rank[:], more[:], AX, ALU.add))
                chain.done(nc.vector.scalar_tensor_tensor(rank[:], rank[:], TOP - 0.5, prob[:], ALU.is_lt, ALU.mult))
                chain.done(nc.vector.tensor_reduce(stat[:, 3, :], rank[:], AX, ALU.add))
                chain.done(nc.vector.reciprocal(stat[:, 3, :], stat[:, 3, :]))
                chain.done(nc.vector.tensor_scalar(stat[:, 3, :], stat[:, 3, :], ALPHA, None, ALU.mult))
                chain.done(nc.vector.tensor_tensor(rank[:], rank[:], per_e(stat[:, 3, :]), ALU.mult))
                for j in range(G):
                    last = nc.vector.tensor_tensor(hw[:, j, :].rearrange("p (e r) -> p e r", e=E),
                                                   b_o[j][:, D:D + E * R].rearrange("p (e r) -> p e r", e=E),
                                                   rank[:, j, :].unsqueeze(2).to_broadcast([P, E, R]), ALU.mult)
                last.then_inc(hw_ok, 1)
                dve.wait_ge(h_hi, it + 1)
                nc.vector.tensor_tensor(hT[1][:], b_h[:, :], hT[0][:].bitcast(F32), ALU.subtract).then_inc(h_lo, 1)
                chain.done(nc.vector.memset(pr.wait_slot[:], 0.0))
                for j in range(G):
                    dve.wait_ge(o_ps, it * G + j + 1)
                    nc.vector.tensor_tensor(x[:, it * G + j, :], b_o[j][:, 0:D], x[:, it * G + j, :],
                                            ALU.add).then_inc(x_ok, 1)
                chain.close()
            for n in range(len(pieces)):
                split_piece(dve, n, False)


WIDE_COLS = 4096
WIDE_CHUNK = 2048


def stage_wide_attention(pr):
    nc, io, x, banks = pr.nc, pr.io, pr.x, pr.banks
    H, HD = 16, 128
    VH = 4
    SCALE = HD ** -0.5
    b_p, b_s, b_t, b_z, b_o = banks[0:2], banks[2:4], banks[4], banks[5], banks[6:8]
    with ExitStack() as ctx:
        sb = lambda n, shape, dt=F32: ctx.enter_context(nc.sbuf_tensor(f"wa_{n}", shape, dt))
        sem = lambda n: pr.sem(f"wa_{n}")
        norm = Norm(pr, ctx, None, b_p, "wa")
        xT = norm.xT
        wq, wk, wv = [tuple(t[:].rearrange("p (c n) -> p c n", c=DC) for t in pr.wide[n]) for n in range(3)]
        wo = tuple(t[:].rearrange("p (h n) -> p h n", h=H) for t in pr.wide[3])
        causal = sb("causal", [P, GT], BF16)
        ident_b = sb("ident_b", [P, P], BF16)
        q = sb("q", [P, 2, GT])
        k = sb("k", [P, 2, GT])
        v = sb("v", [P, 2, G, VH * HD])
        negmax = sb("negmax", [P, 2, G])
        sums = sb("sums", [P, 2, G])
        rsum = sb("rsum", [P, 2, G])
        prob = sb("prob", [P, 2, G, P])
        probT = sb("probT", [P, 2, G, P])
        z = (sb("z_hi", [P, 2, GT], F32R), sb("z_lo", [P, 2, GT], F32R))

        loaded = sem("masks_loaded")
        q_ps, q_ok, k_ps, k_ok = sem("q_in_psum"), sem("q_ready"), sem("k_in_psum"), sem("k_ready")
        v_ps, v_ok = sem("v_in_psum"), sem("v_ready")
        s_ps, max_ok, exp_ok = sem("scores_in_psum"), sem("negmax_ready"), sem("exps_ready")
        r_ok, prob_ok = sem("rsum_ready"), sem("probs_ready")
        t_ps, t_ok = sem("probsT_in_psum"), sem("probsT_ready")
        z_ps, z_hi, z_lo = sem("z_in_psum"), sem("z_hi_ready"), sem("z_ready")
        o_ps, x_ok = sem("out_in_psum"), sem("x_updated")
        chain_s = sem("vector_chain")
        block = ctx.enter_context(nc.Block())

        V_UNITS = {t: [t + G] for t in range(H - G)}
        V_UNITS |= {H - 2: [H, H + 1], H - 1: [H + 2, H + 3]}
        T_STATS, T_APPLY, T_TURN = 4, 5, H - 3

        def in_range(h, last):
            return h < H or not last

        @block.sync
        def _(sp):
            sp.dma_start(causal[:], io["causal"]).then_inc(loaded, 16)
            sp.dma_start(ident_b[:], io["ident_b"]).then_inc(loaded, 16)

        @block.gpsimd
        def _(pool):
            def normalise(n, s):
                pool.wait_ge(r_ok, BASE + n + 1)
                nc.gpsimd.tensor_tensor(prob[:, s], prob[:, s], rsum[:, s, :].unsqueeze(2).to_broadcast([P, G, P]),
                                        ALU.mult).then_inc(prob_ok, 1)

            def group(it, last):
                for t in range(H):
                    if in_range(t + 1, last):
                        normalise(it * H + t + 1, (t + 1) % 2)
                    if t == T_STATS and not last:
                        norm.pool_rstd(pool, it + 1)

            pool.sem_inc(prob_ok, BASE)
            norm.pool_rstd(pool, 0)
            normalise(0, 0)
            with pool.Fori(0, NG - 1) as it:
                group(it, False)
            group(NG - 1, True)

        @block.tensor
        def _(pe):
            def scores(n, s):
                pe.wait_ge(q_ok, BASE + n + 1)
                pe.wait_ge(k_ok, BASE + n + 1)
                pe.wait_ge(exp_ok, BASE + n - 1)
                nc.tensor.matmul(b_s[s][:, :], ident_b[:], causal[:], start=True, stop=False,
                                 skip_group_check=True)
                for j in range(G):
                    t = slice(j * P, (j + 1) * P)
                    last = nc.tensor.matmul(b_s[s][:, t], q[:, s, t], k[:, s, t], start=False,
                                            stop=True, skip_group_check=True)
                last.then_inc(s_ps, 1)

            def qk(n, h, v_before):
                cols = slice(h * HD, (h + 1) * HD)
                pe.wait_ge(q_ok, BASE + n)
                pe.wait_ge(v_ok, BASE + v_before)
                for c in range(DC):
                    last = product(nc, b_p[0][:, :], pair(wq, slice(None), c, cols), pair(xT, slice(None), c),
                                   c == 0, c == DC - 1)
                last.then_inc(q_ps, 1)
                pe.wait_ge(k_ok, BASE + n)
                for c in range(DC):
                    last = product(nc, b_p[1][:, :], pair(wk, slice(None), c, cols), pair(xT, slice(None), c),
                                   c == 0, c == DC - 1)
                last.then_inc(k_ps, 1)

            def values(n, unit, q_before):
                g, j = divmod(unit, G)
                pe.wait_ge(q_ok, BASE + q_before)
                pe.wait_ge(v_ok, BASE + n)
                for c in range(DC):
                    last = product(nc, b_p[0][:, :], pair(xT, slice(None), c, slice(j * P, (j + 1) * P)),
                                   pair(wv, slice(None), c, slice(g * VH * HD, (g + 1) * VH * HD)),
                                   c == 0, c == DC - 1)
                last.then_inc(v_ps, 1)

            def turn(n, s):
                pe.wait_ge(prob_ok, BASE + n + 1)
                pe.wait_ge(t_ok, BASE + n)
                for j in range(G):
                    last = nc.tensor.transpose(b_t[:, j * P:(j + 1) * P], prob[:, s, j, :], pr.ident[:])
                last.then_inc(t_ps, 1)

            def weigh(it, h):
                n = it * H + h
                g, m = divmod(h, VH)
                pe.wait_ge(t_ok, BASE + n + 1)
                pe.wait_ge(v_ok, BASE + it * H + G * (g + 1))
                pe.wait_ge(z_lo, BASE + n)
                for j in range(G):
                    last = nc.tensor.matmul(b_z[:, j * P:(j + 1) * P], v[:, g % 2, j, m * HD:(m + 1) * HD],
                                            probT[:, h % 2, j, :], start=True, stop=True)
                last.then_inc(z_ps, 1)

            def project(it, h):
                pe.wait_ge(z_lo, BASE + it * H + h + 1)
                if h == 0:
                    pe.wait_ge(x_ok, ONE + it * G)
                for j in range(G):
                    last = product(nc, b_o[j // 2][:, (j % 2) * D:(j % 2) * D + D],
                                   pair(z, slice(None), h % 2, slice(j * P, (j + 1) * P)),
                                   pair(wo, slice(None), h), h == 0 and j % 2 == 0, h == H - 1)
                last.then_inc(o_ps, 1)

            def group(it, last):
                n_v = G
                for t in range(H):
                    n = it * H + t
                    if in_range(t + 1, last):
                        scores(n + 1, (t + 1) % 2)
                    if t == H - 2 and not last:
                        project(it, t - 1)
                        pe.wait_ge(norm.s_lo, (it + 1) * DC + DC)
                    if in_range(t + 2, last) and t < H - 1:
                        qk(n + 2, (t + 2) % H, it * H + n_v)
                    if t >= 1 and not (t == H - 2 and not last):
                        project(it, t - 1)
                    turn(n, t % 2)
                    if t < H - 2 or not last:
                        for unit in V_UNITS.get(t, []):
                            values(it * H + n_v, unit % H, it * H + min(t + 3, H + 1))
                            n_v += 1
                    if t == T_TURN and not last:
                        pe.wait_ge(q_ok, BASE + it * H + H)
                        pe.wait_ge(v_ok, BASE + it * H + H)
                        pe.wait_ge(k_ok, BASE + it * H + H)
                        norm.tensor_transpose(pe, it + 1)
                    weigh(it, t)
                    if t == H - 1:
                        if not last:
                            qk(n + 2, 1, it * H + n_v)
                        project(it, t)

            for event in (s_ps, t_ps, z_ps, o_ps):
                pe.sem_inc(event, BASE)
            pe.wait_ge(loaded, 32)
            norm.tensor_transpose(pe, 0)
            pe.wait_ge(norm.s_lo, DC)
            qk(0, 0, 0)
            values(0, 0, 1)
            values(1, 1, 1)
            scores(0, 0)
            qk(1, 1, 2)
            values(2, 2, 2)
            values(3, 3, 2)
            with pe.Fori(0, NG - 1) as it:
                group(it, False)
            group(NG - 1, True)

        @block.scalar
        def _(act):
            def exps(n, s):
                act.wait_ge(max_ok, BASE + n + 1)
                act.wait_ge(t_ps, BASE + n - 1)
                for j in range(G):
                    last = nc.scalar.activation(prob[:, s, j, :], b_s[s][:, j * P:(j + 1) * P], ACT.Exp,
                                                bias=negmax[:, s, j:j + 1], scale=SCALE,
                                                accum_out=sums[:, s, j:j + 1])
                last.then_inc(exp_ok, 1)

            def keep_q(n, s):
                act.wait_ge(q_ps, n + 1)
                act.wait_ge(s_ps, BASE + n - 1)
                nc.scalar.copy(q[:, s, :], b_p[0][:, :]).then_inc(q_ok, 1)

            def keep_v(it, unit):
                g, j = divmod(unit, G)
                act.wait_ge(v_ps, it * H + unit + 1)
                if g >= 2:
                    act.wait_ge(z_ps, BASE + it * H + VH * (g - 1))
                nc.scalar.copy(v[:, g % 2, j, :], b_p[0][:, :]).then_inc(v_ok, 1)

            def group(it, last):
                for t in range(H):
                    n = it * H + t
                    if in_range(t + 1, last):
                        exps(n + 1, (t + 1) % 2)
                    if in_range(t + 2, last) and t < H - 1:
                        keep_q(n + 2, t % 2)
                    if t < H - 2 or not last:
                        for unit in V_UNITS.get(t, []):
                            keep_v(it, unit)
                    if t == T_TURN and not last:
                        norm.scalar_hi(act, it + 1)
                    act.wait_ge(z_ps, BASE + n + 1)
                    act.wait_ge(o_ps, BASE + n - 1)
                    nc.scalar.copy(z[0][:, t % 2, :], b_z[:, :]).then_inc(z_hi, 1)
                    if t == H - 1 and not last:
                        keep_q(n + 2, t % 2)

            for event in (exp_ok, q_ok, v_ok):
                act.sem_inc(event, BASE)
            norm.scalar_hi(act, 0)
            keep_q(0, 0)
            keep_v(0, 0)
            keep_v(0, 1)
            exps(0, 0)
            keep_q(1, 1)
            keep_v(0, 2)
            keep_v(0, 3)
            with act.Fori(0, NG - 1) as it:
                group(it, False)
            group(NG - 1, True)

        @block.vector
        def _(dve):
            def row_max(n, s, chain):
                dve.wait_ge(s_ps, BASE + n + 1)
                dve.wait_ge(exp_ok, BASE + n - 1)
                chain.done(nc.vector.tensor_reduce(
                    negmax[:, s, :], b_s[s][:, :].rearrange("p (j k) -> p j k", j=G), AX, ALU.max))
                nc.vector.tensor_scalar(negmax[:, s, :], negmax[:, s, :], -SCALE, None, ALU.mult)\
                    .then_inc(max_ok, 1)

            def keep_k(n, s):
                dve.wait_ge(k_ps, n + 1)
                dve.wait_ge(s_ps, BASE + n - 1)
                nc.vector.tensor_copy(k[:, s, :], b_p[1][:, :]).then_inc(k_ok, 1)

            def inverse_sums(n, s):
                dve.wait_ge(exp_ok, BASE + n + 1)
                dve.wait_ge(prob_ok, BASE + n - 1)
                nc.vector.reciprocal(rsum[:, s, :], sums[:, s, :]).then_inc(r_ok, 1)

            def group(it, last):
                chain = Chain(dve, chain_s, it, H)
                chain.n = 1
                for t in range(H):
                    n = it * H + t
                    if in_range(t + 1, last):
                        row_max(n + 1, (t + 1) % 2, chain)
                    if in_range(t + 2, last) and t < H - 1:
                        keep_k(n + 2, t % 2)
                    if in_range(t + 1, last):
                        inverse_sums(n + 1, (t + 1) % 2)
                    dve.wait_ge(t_ps, BASE + n + 1)
                    dve.wait_ge(z_ps, BASE + n - 1)
                    nc.vector.tensor_copy(probT[:, t % 2], b_t[:, :].rearrange("p (j k) -> p j k", j=G))\
                        .then_inc(t_ok, 1)
                    if not last:
                        if t == T_STATS:
                            norm.vector_stats(dve, it + 1)
                        if t == T_APPLY:
                            norm.vector_apply(dve, it + 1)
                        if t == T_TURN:
                            norm.vector_lo(dve, it + 1)
                    dve.wait_ge(z_hi, n + 1)
                    nc.vector.tensor_tensor(z[1][:, t % 2, :], b_z[:, :], z[0][:, t % 2, :].bitcast(F32),
                                            ALU.subtract).then_inc(z_lo, 1)
                    if t == H - 1 and not last:
                        keep_k(n + 2, t % 2)
                dve.wait_ge(o_ps, BASE + it * H + H)
                for j in range(G):
                    nc.vector.tensor_tensor(x[:, it * G + j, :], b_o[j // 2][:, (j % 2) * D:(j % 2) * D + D],
                                            x[:, it * G + j, :], ALU.add).then_inc(x_ok, 1)
                if not last:
                    chain.n -= 1
                chain.close()

            for event in (max_ok, k_ok, r_ok, t_ok, z_lo):
                dve.sem_inc(event, BASE)
            dve.sem_inc(x_ok, ONE)
            norm.vector_norm(dve, 0)
            norm.vector_lo(dve, 0)
            keep_k(0, 0)
            first = Chain(dve, chain_s, 0, 1)
            row_max(0, 0, first)
            keep_k(1, 1)
            inverse_sums(0, 0)
            with dve.Fori(0, NG - 1) as it:
                group(it, False)
            group(NG - 1, True)


def stage_experts_and_wide_attention(pr):
    nc = pr.nc
    with ExitStack() as ctx:
        pr.wide = [tuple(ctx.enter_context(nc.sbuf_tensor(f"wide{n}_{part}", [P, WIDE_COLS], F32R))
                         for part in ("hi", "lo")) for n in range(4)]
        stage_lora_experts(pr)
        stage_wide_attention(pr)


def stage_linear_attention(pr):
    nc, io, x, banks = pr.nc, pr.io, pr.x, pr.banks
    H, HD, F = 16, 16, 64
    T = H // 2
    HF = H * F
    VW = HD + 1
    HH = H // DC
    HC = HH * F
    b_p = banks[0:2]
    b_k, b_kv, b_qkv, b_v = banks[2:4], banks[4], banks[5], banks[6]
    b_o, b_ot = banks[7][:, 0:D], banks[7][:, D:2 * D]
    with ExitStack() as ctx:
        sb = lambda n, shape, dt=F32: ctx.enter_context(nc.sbuf_tensor(f"li_{n}", shape, dt))
        both = lambda n, shape: (sb(f"{n}_hi", shape, F32R), sb(f"{n}_lo", shape, F32R))
        sem = lambda n: pr.sem(f"li_{n}")
        norm = Norm(pr, ctx, None, b_p, "li")
        wqk = sb("wqk", [P, 2, DC, D])
        wf = sb("wf", [P, 2, HC])
        bqk = sb("bqk", [P, 2, DC, 2])
        vo32 = sb("vo32", [P, 2, DC, D])
        vo = both("vo", [P, 2, DC, D])
        v_row32 = sb("v_row32", [2, D])
        sign32 = sb("sign32", [2, P + 1])
        sign = sb("sign", [2, P], F32R)
        v_row_hi = sb("v_row_hi", [2, D], F32R)
        v_row = sb("v_row", [2, D], F32R)
        k_row_hi = sb("k_row_hi", [2, HF], F32R)
        k_row = sb("k_row", [2, HF], F32R)
        out_bias = sb("out_bias", [P, D])
        mqk = both("mqk", [P, 2, DC, HF])
        q_bias = sb("q_bias", [P, T])
        mask = sb("mask", [P, NB])
        kt32 = sb("kt32", [P, DC, NB, P])
        kt = both("kt", [P, 2, DC, P])
        qp = sb("qp", [P, T, GT])
        kp = sb("kp", [P, 2, HF])
        va = sb("va", [P, 2, H, VW])
        kv = sb("kv", [P, 2, T, 2 * VW])
        rden = sb("rden", [P, 2, H])
        o = sb("o", [P, 2, D])
        oT = both("oT", [P, 2, DC, P])

        loaded, late_loaded = sem("loaded"), sem("late_loaded")
        fold_ps, fold_hi, fold_lo = sem("folded_in_psum"), sem("folded_hi"), sem("folded_ready")
        w_hi, w_lo, clear = sem("vo_hi"), sem("vo_ready"), sem("cleared")
        kt_hi, kt_lo = sem("kt_hi"), sem("kt_ready")
        q_ps, q_ok = sem("q_in_psum"), sem("q_ready")
        k_ps, k_ok = sem("k_in_psum"), sem("k_ready")
        v_ps, v_ok = sem("v_in_psum"), sem("v_ready")
        kv_ps, kv_ok = sem("kv_in_psum"), sem("kv_ready")
        n_ps, n_ok = sem("qkv_in_psum"), sem("o_ready")
        ot_ps, ot_hi, ot_lo = sem("oT_in_psum"), sem("oT_hi_ready"), sem("oT_ready")
        o_ps, xb_ok, x_ok = sem("out_in_psum"), sem("x_biased"), sem("x_updated")
        chain_s = sem("vector_chain")
        block = ctx.enter_context(nc.Block())
        NLOAD, NLATE = 5, 4
        FOLDS = [(w, c, half) for w in range(2) for c in range(DC) for half in range(2)]

        T_STATS, T_APPLY, T_TURN = 0, 1, 2
        def query_steps(it, j):
            return (it + j // 2, 1 - j // 2, range(T // 2 * (j % 2), T // 2 * (j % 2) + T // 2))

        @block.sync
        def _(sp):
            for t, name in ((wqk, "li_wqk"), (wf, "li_wf"), (bqk, "li_bqk"), (v_row32, "li_v_row"),
                            (sign32, "li_sign")):
                sp.dma_start(t[:], io[name]).then_inc(loaded, 16)
            sp.dma_start(kt32[:], io["ctx_rev"]).then_inc(late_loaded, 16)
            sp.dma_start(pr.em_w[:], io["em_w"]).then_inc(pr.em_loaded, 16)

        @block.gpsimd
        def _(pool):
            norm.pool_rstd(pool, 0)
            nc.gpsimd.memset(va[:], 1.0).then_inc(clear, 1)
            nc.gpsimd.memset(kv[:], 0.0).then_inc(clear, 1)
            pool.wait_ge(late_loaded, 16 * NLATE)

            def add_bias(it):
                pool.wait_ge(norm.s_xn, it + 1)
                nc.gpsimd.tensor_tensor(x[:, bass.ds(it * G, G), :], x[:, bass.ds(it * G, G), :],
                                        out_bias[:].unsqueeze(1).to_broadcast([P, G, D]), ALU.add).then_inc(xb_ok, 1)

            add_bias(0)
            with pool.Fori(1, NG) as it:
                norm.pool_rstd(pool, it)
                add_bias(it)

        @block.tensor
        def _(pe):
            def keys(n, s):
                pe.wait_ge(kt_lo, n + 1)
                for half in range(2):
                    cols = slice(half * HC, (half + 1) * HC)
                    pe.wait_ge(k_ok, BASE + 2 * n + half - 1)
                    nc.tensor.matmul(b_k[half][:, :], sign[:], k_row[:, cols], start=True, stop=False,
                                     skip_group_check=True)
                    for c in range(DC):
                        last = product(nc, b_k[half][:, :], pair(kt, slice(None), s, c),
                                       pair(mqk, slice(None), 1, c, cols), False, c == DC - 1)
                    last.then_inc(k_ps, 1)
                pe.wait_ge(v_ok, ONE + n)
                nc.tensor.matmul(b_v[:, 0:D], sign[:], v_row[:], start=True, stop=False, skip_group_check=True)
                for c in range(DC):
                    last = product(nc, b_v[:, 0:D], pair(kt, slice(None), s, c), pair(vo, slice(None), 0, c),
                                   False, c == DC - 1)
                last.then_inc(v_ps, 1)

            def key_values(n, s):
                pe.wait_ge(k_ok, BASE + 2 * n + 2)
                pe.wait_ge(v_ok, ONE + n + 1)
                pe.wait_ge(kv_ok, ONE + n)
                for t in range(T):
                    last = nc.tensor.matmul(b_kv[:, t * 2 * VW:(t + 1) * 2 * VW], kp[:, s, t * P:(t + 1) * P],
                                            va[:, s, 2 * t:2 * t + 2, :], start=True, stop=True)
                last.then_inc(kv_ps, 1)

            def queries(it, p, heads):
                pe.wait_ge(norm.s_lo, it * DC + DC)
                for t in heads:
                    pe.wait_ge(q_ok, BASE + it * 2 * T + p * T + t - 1)
                    tokens = slice(2 * P * p, 2 * P * (p + 1))
                    for c in range(DC):
                        last = product(nc, b_p[t % 2][:, 0:2 * P],
                                       pair(mqk, slice(None), 0, c, slice(t * P, (t + 1) * P)),
                                       pair(norm.xT, slice(None), c, tokens), c == 0, c == DC - 1)
                    last.then_inc(q_ps, 1)

            def numerators(it, j):
                n = it * G + j
                pe.wait_ge(kv_ok, ONE + n + 1)
                pe.wait_ge(q_ok, BASE + it * 2 * T + (j // 2 + 1) * T)
                pe.wait_ge(n_ok, ONE + n)
                for t in range(T):
                    last = nc.tensor.matmul(b_qkv[:, t * 2 * VW:(t + 1) * 2 * VW], qp[:, t, j * P:(j + 1) * P],
                                            kv[:, j % 2, t, :], start=True, stop=True)
                last.then_inc(n_ps, 1)

            def turn_o(n, s):
                pe.wait_ge(n_ok, ONE + n + 1)
                pe.wait_ge(ot_lo, ONE + n)
                for c in range(DC):
                    last = nc.tensor.transpose(b_ot[:, c * P:(c + 1) * P], o[:, s, c * P:(c + 1) * P], pr.ident[:])
                last.then_inc(ot_ps, 1)

            def project(n, s):
                pe.wait_ge(ot_lo, ONE + n + 1)
                pe.wait_ge(x_ok, ONE + n)
                for c in range(DC):
                    last = product(nc, b_o, pair(oT, slice(None), s, c), pair(vo, slice(None), 1, c),
                                   c == 0, c == DC - 1)
                last.then_inc(o_ps, 1)

            def group(it, last):
                for j in range(G):
                    n = it * G + j
                    more = not last or j + 1 < G
                    if j == T_TURN and not last:
                        pe.wait_ge(q_ok, BASE + (it + 1) * 2 * T)
                        norm.tensor_transpose(pe, it + 1)
                    if more:
                        keys(n + 1, (j + 1) % 2)
                    numerators(it, j)
                    if not last or j < 2:
                        queries(*query_steps(it, j))
                    turn_o(n, j % 2)
                    if more:
                        key_values(n + 1, (j + 1) % 2)
                    project(n, j % 2)

            for event in (kv_ps, n_ps, ot_ps, o_ps):
                pe.sem_inc(event, BASE)
            pe.wait_ge(loaded, 16 * NLOAD)
            for n, (w, c, half) in enumerate(FOLDS):
                nc.tensor.matmul(banks[n][:, :], wqk[:, w, half, c * P:(c + 1) * P], wf[:, w, :],
                                 start=True, stop=True).then_inc(fold_ps, 1)
            pe.wait_ge(fold_lo, 3)
            for t in range(T):
                half, m = divmod(t, T // 2)
                last = nc.tensor.matmul(banks[2][:, t:t + 1], wf[:, 0, m * P:(m + 1) * P], bqk[:, 0, half, 0:1],
                                        start=True, stop=True)
            last.then_inc(fold_ps, 1)
            for half in range(2):
                pe.wait_ge(fold_lo, 4 + half)
                nc.tensor.matmul(banks[3 + half][0:2, :], bqk[:, 1, half, :], wf[:, 1, :],
                                 start=True, stop=True).then_inc(fold_ps, 1)
            norm.tensor_transpose(pe, 0)
            pe.wait_ge(fold_lo, len(FOLDS) + 3)
            pe.wait_ge(w_lo, 2)
            keys(0, 0)
            queries(0, 0, range(T))
            key_values(0, 0)
            with pe.Fori(0, NG - 1) as it:
                group(it, False)
            group(NG - 1, True)

        @block.scalar
        def _(act):
            for t, src in ((vo32[:], io["li_vo"]), (mask[:], io["li_mask"]), (out_bias[:], io["li_o_bias"])):
                act.dma_start(t, src).then_inc(late_loaded, 16)

            def keep_kt(n, s):
                nc.scalar.copy(kt[0][:, s], kt32[:, :, bass.ds(n, 1), :].rearrange("p c b t -> p c (b t)"))\
                    .then_inc(kt_hi, 1)

            def values(n, s):
                act.wait_ge(v_ps, n + 1)
                act.wait_ge(kv_ps, BASE + n - 1)
                nc.scalar.copy(va[:, s, :, 0:HD], b_v[:, 0:D].rearrange("p (h d) -> p h d", h=H)).then_inc(v_ok, 1)

            def keep_kv(n, s):
                act.wait_ge(kv_ps, BASE + n + 1)
                act.wait_ge(n_ps, BASE + n - 1)
                src = b_kv[:, 0:T * 2 * VW].rearrange("p (t n) -> p t n", t=T)
                nc.scalar.copy(kv[0:F, s, :, 0:VW], src[0:F, :, 0:VW])
                nc.scalar.copy(kv[F:2 * F, s, :, VW:2 * VW], src[F:2 * F, :, VW:2 * VW]).then_inc(kv_ok, 1)

            def keep_q(it, p, heads):
                act.wait_ge(n_ps, BASE + it * G + 2 * p - 2)
                for t in heads:
                    act.wait_ge(q_ps, it * 2 * T + p * T + t + 1)
                    nc.scalar.activation(qp[:, t, 2 * P * p:2 * P * (p + 1)], b_p[t % 2][:, 0:2 * P], ACT.Relu,
                                         bias=q_bias[:, t:t + 1]).then_inc(q_ok, 1)

            def group(it, last):
                for j in range(G):
                    n = it * G + j
                    if j == T_TURN and not last:
                        norm.scalar_hi(act, it + 1)
                    if not last or j + 2 < G:
                        keep_kt(n + 2, j % 2)
                    if not last or j + 1 < G:
                        values(n + 1, (j + 1) % 2)
                    if not last or j < 2:
                        keep_q(*query_steps(it, j))
                    act.wait_ge(ot_ps, BASE + n + 1)
                    act.wait_ge(o_ps, BASE + n - 1)
                    nc.scalar.copy(oT[0][:, j % 2, :, :], b_ot.rearrange("p (c t) -> p c t", c=DC))\
                        .then_inc(ot_hi, 1)
                    if not last or j + 1 < G:
                        keep_kv(n + 1, (j + 1) % 2)

            act.sem_inc(q_ok, BASE)
            act.sem_inc(v_ok, ONE)
            act.sem_inc(kv_ok, ONE)
            act.wait_ge(loaded, 16 * NLOAD)
            nc.scalar.copy(sign[:], sign32[:, 0:P])
            nc.scalar.copy(v_row_hi[:], v_row32[:]).then_inc(w_hi, 1)
            for n, (w, c, half) in enumerate(FOLDS):
                act.wait_ge(fold_ps, n + 1)
                nc.scalar.copy(mqk[0][:, w, c, half * HC:(half + 1) * HC], banks[n][:, :]).then_inc(fold_hi, 1)
            for half in range(2):
                act.wait_ge(fold_ps, len(FOLDS) + 2 + half)
                nc.scalar.copy(k_row_hi[:, half * HC:(half + 1) * HC], banks[3 + half][0:2, :])\
                    .then_inc(fold_hi, 1)
            act.wait_ge(late_loaded, 16 * (NLATE))
            nc.scalar.copy(vo[0][:], vo32[:]).then_inc(w_hi, 1)
            keep_kt(0, 0)
            keep_kt(1, 1)
            norm.scalar_hi(act, 0)
            act.wait_ge(fold_lo, len(FOLDS) + 1)
            act.wait_ge(clear, 2)
            values(0, 0)
            for t in range(T):
                act.wait_ge(q_ps, t + 1)
                nc.scalar.activation(qp[:, t, 0:2 * P], b_p[t % 2][:, 0:2 * P], ACT.Relu,
                                     bias=q_bias[:, t:t + 1]).then_inc(q_ok, 1)
            keep_kv(0, 0)
            with act.Fori(0, NG - 1) as it:
                group(it, False)
            group(NG - 1, True)

        @block.vector
        def _(dve):
            def kt_rest(n, s):
                dve.wait_ge(kt_hi, n + 1)
                nc.vector.tensor_tensor(kt[1][:, s], kt32[:, :, bass.ds(n, 1), :].rearrange("p c b t -> p c (b t)"),
                                        kt[0][:, s].bitcast(F32), ALU.subtract).then_inc(kt_lo, 1)

            def keep_keys(n, s):
                dve.wait_ge(kv_ps, BASE + n - 1)
                for half in range(2):
                    dve.wait_ge(k_ps, 2 * n + half + 1)
                    nc.vector.tensor_scalar(kp[:, s, half * HC:(half + 1) * HC], b_k[half][:, :], 0.0,
                                            mask[:, bass.ds(n, 1)], ALU.max, ALU.mult).then_inc(k_ok, 1)

            def group(it, last):
                chain = Chain(dve, chain_s, it, 2 * G)
                for j in range(G):
                    n, s = it * G + j, j % 2
                    if j == T_TURN and not last:
                        norm.vector_lo(dve, it + 1)
                    if not last or j + 2 < G:
                        kt_rest(n + 2, s)
                    if not last or j + 1 < G:
                        keep_keys(n + 1, 1 - s)
                    dve.wait_ge(n_ps, BASE + n + 1)
                    src = b_qkv[:, 0:H * VW].rearrange("p (h n) -> p h n", h=H)
                    chain.done(nc.vector.tensor_scalar(rden[:, s, :], src[:, :, HD], 1e-8, None, ALU.add))
                    chain.done(nc.vector.reciprocal(rden[:, s, :], rden[:, s, :]))
                    dve.wait_ge(ot_ps, BASE + n - 1)
                    nc.vector.tensor_tensor(o[:, s, :].rearrange("p (h d) -> p h d", h=H), src[:, :, 0:HD],
                                            rden[:, s, :].unsqueeze(2).to_broadcast([P, H, HD]), ALU.mult)\
                        .then_inc(n_ok, 1)
                    if j == T_STATS and not last:
                        norm.vector_stats(dve, it + 1)
                    if j == T_APPLY and not last:
                        norm.vector_apply(dve, it + 1)
                    dve.wait_ge(ot_hi, n + 1)
                    nc.vector.tensor_tensor(oT[1][:, s, :, :], b_ot.rearrange("p (c t) -> p c t", c=DC),
                                            oT[0][:, s, :, :].bitcast(F32), ALU.subtract).then_inc(ot_lo, 1)
                    if j == 0:
                        dve.wait_ge(xb_ok, it + 1)
                    dve.wait_ge(o_ps, BASE + n + 1)
                    nc.vector.tensor_tensor(x[:, n, :], b_o, x[:, n, :], ALU.add).then_inc(x_ok, 1)
                chain.close()

            dve.sem_inc(k_ok, BASE)
            for event in (n_ok, ot_lo, x_ok):
                dve.sem_inc(event, ONE)
            norm.vector_norm(dve, 0)
            dve.wait_ge(w_hi, 1)
            nc.vector.scalar_tensor_tensor(v_row[:], v_row32[:], sign32[:, P:P + 1], v_row_hi[:].bitcast(F32),
                                           ALU.mult, ALU.subtract).then_inc(w_lo, 1)
            for n, (w, c, half) in enumerate(FOLDS):
                dve.wait_ge(fold_hi, n + 1)
                cols = slice(half * HC, (half + 1) * HC)
                nc.vector.tensor_tensor(mqk[1][:, w, c, cols], banks[n][:, :], mqk[0][:, w, c, cols].bitcast(F32),
                                        ALU.subtract).then_inc(fold_lo, 1)
            dve.wait_ge(fold_ps, len(FOLDS) + 1)
            nc.vector.tensor_copy(q_bias[:], banks[2][:, 0:T]).then_inc(fold_lo, 1)
            for half in range(2):
                dve.wait_ge(fold_hi, len(FOLDS) + half + 1)
                cols = slice(half * HC, (half + 1) * HC)
                nc.vector.scalar_tensor_tensor(k_row[:, cols], banks[3 + half][0:2, :], sign32[:, P:P + 1],
                                               k_row_hi[:, cols].bitcast(F32), ALU.mult, ALU.subtract)\
                    .then_inc(fold_lo, 1)
            dve.wait_ge(w_hi, 2)
            nc.vector.tensor_tensor(vo[1][:], vo32[:], vo[0][:].bitcast(F32), ALU.subtract).then_inc(w_lo, 1)
            kt_rest(0, 0)
            kt_rest(1, 1)
            norm.vector_lo(dve, 0)
            keep_keys(0, 0)
            with dve.Fori(0, NG - 1) as it:
                group(it, False)
            group(NG - 1, True)


def stage_expert_mix(pr):
    nc, io, x, banks = pr.nc, pr.io, pr.x, pr.banks
    E, H, K = 32, 64, 16
    RG = P // E
    HQ = H // RG
    WC = HQ * D
    MC = 512
    NMIX = 2 * WC // MC
    NP = NB // 2
    BIG = 3e38
    w = pr.em_w
    b_m = banks[2:8]
    with ExitStack() as ctx:
        sb = lambda n, shape, dt=F32: ctx.enter_context(nc.sbuf_tensor(f"em_{n}", shape, dt))
        sem = lambda n: pr.sem(f"em_{n}")
        norm = Norm(pr, ctx, None, banks[0:2], "em", split=False)
        sim = sb("sim", [P, DC, E])
        gates = sb("gates", [NB, E])
        before = sb("before", [NB, E, E])
        row_group = sb("row_group", [P, RG])
        xT = sb("xT_all", [P, DC, NB, P])
        rep = sb("rep", [P, DC, NB])
        rep2 = sb("rep2", [P, DC, NB])
        sim2 = sb("sim2", [P, DC, E])
        ones = sb("ones", [P, NB])
        minus_half = sb("minus_half", [NB, E])
        simn = sb("simn", [NB, E])
        repn = sb("repn", [NB, 1])
        logit = sb("logit", [NB, E])
        gated = sb("gated", [NB, E])
        act_mask = sb("act_mask", [NB, E])
        small = sb("small", [NB, 8])
        more = sb("more", [NB, E, E])
        tied = sb("tied", [NB, E, E])
        rank = sb("rank", [NB, E])
        sig = sb("sig", [NB, E])
        route = sb("route", [NB, 2, RG, E])
        routeT = sb("routeT", [P, 2, RG, NB])
        mixed = sb("mixed", [P, 2, NP, D])
        wvT = sb("wvT", [P, DC, NP, P])
        hT = sb("hT", [P, 2, P])
        scratch = nc.dram_tensor("em_scratch", (RG, NB, 2, WC), F32, kind="Internal").ap()

        loaded, xT_ok, rep_ps, rep_ok = sem("loaded"), sem("xT_kept"), sem("rep_in_psum"), sem("rep_ready")
        const_ok, aff_ps, rn_in, rn_ok = sem("consts"), sem("affinity_in_psum"), sem("norms_in"), sem("rnorms_ready")
        exp_in, exp_ok, r_ok, rT_ps, rT_ok = (sem("exp_in"), sem("exp_ready"), sem("routing_ready"),
                                              sem("routingT_in_psum"), sem("routingT_ready"))
        mix_ps = sem("mix_in_psum")
        mix_ok = [sem("mix_kept_even"), sem("mix_kept_odd")]
        spilled = [sem("mix_v_in_dram"), sem("mix_o_in_dram")]
        mixed_in = [sem("mix_v_loaded"), sem("mix_o_loaded")]
        wt_ps = sem("wvT_in_psum")
        wt_ok = [sem("wvT_ready_act"), sem("wvT_ready_vec")]
        h_ps, h_ok, o_ps, x_ok = sem("hT_in_psum"), sem("hT_ready"), sem("out_in_psum"), sem("x_updated")
        chain_s, sig_ok, stored = sem("vector_chain"), sem("gate_exps"), sem("stored")
        block = ctx.enter_context(nc.Block())

        def reload(eng, kind, groups):
            eng.wait_ge(spilled[kind], 16 * 2)
            for g in groups:
                for odd in range(2):
                    first = odd * H + g * HQ
                    eng.dma_start(mixed[first:first + HQ, kind],
                                  scratch[g, odd::2, kind].rearrange("b (h c) -> h b c", c=D))\
                        .then_inc(mixed_in[kind], 16)

        @block.sync
        def _(sp):
            sp.dma_start(sim[:], io["em_sim"]).then_inc(loaded, 16)
            sp.dma_start(gates[:], io["em_gates"]).then_inc(loaded, 16)
            sp.dma_start(before[:], io["before32"]).then_inc(loaded, 16)
            sp.dma_start(row_group[:], io["em_row_group"]).then_inc(loaded, 16)
            for n in range(4):
                for parity in range(2):
                    sp.wait_ge(mix_ok[parity], (n + 1) * NMIX // 8)
                kind, half = divmod(n, 2)
                sp.dma_start(scratch[:, :, kind, half * WC // 2:(half + 1) * WC // 2],
                             w[0:RG * NB, kind, half * WC // 2:(half + 1) * WC // 2]).then_inc(spilled[kind], 16)
                if half:
                    reload(sp, kind, range(RG))
            for it in range(NG):
                sp.wait_ge(x_ok, (it + 1) * G // 2)
                sp.dma_start(io["out"][it * G:(it + 1) * G].rearrange("b t d -> t b d"),
                             x[:, it * G:(it + 1) * G, :]).then_inc(stored, 16)
            sp.wait_ge(stored, 16 * NG)

        @block.gpsimd
        def _(pool):
            nc.gpsimd.memset(ones[:], 1.0).then_inc(const_ok, 1)
            nc.gpsimd.memset(minus_half[:], -0.5).then_inc(const_ok, 1)
            with pool.Fori(0, NG) as it:
                norm.pool_rstd(pool, it)
            pool.wait_ge(rn_in, 2)
            pool.wait_ge(const_ok, 2)
            nc.gpsimd.tensor_tensor(simn[:], simn[:], minus_half[:], ALU.pow).then_inc(rn_ok, 1)
            nc.gpsimd.tensor_tensor(repn[:], repn[:], minus_half[:, 0:1], ALU.pow).then_inc(rn_ok, 1)

        @block.tensor
        def _(pe):
            def turn_group(it):
                if not isinstance(it, int):
                    pe.wait_ge(xT_ok, it * DC)
                norm.tensor_transpose(pe, it)
                for c in range(DC):
                    for j in range(G):
                        last = nc.tensor.matmul(banks[7][:, bass.ds(it * G + (c * NB + j), 1)],
                                                norm.xn[:, j, c * P:(c + 1) * P], ones[:, 0:1],
                                                start=True, stop=True)
                last.then_inc(rep_ps, 1)

            pe.wait_ge(const_ok, 2)
            turn_group(0)
            with pe.Fori(1, NG) as it:
                turn_group(it)
            pe.wait_ge(rep_ok, 3)
            aff, s2, r2 = banks[2][0:NB, 0:E], banks[3][0:NB, 0:E], banks[4][0:NB, 0:1]
            for c in range(DC):
                nc.tensor.matmul(aff, rep[:, c, :], sim[:, c, :], start=(c == 0), stop=(c == DC - 1))
            for c in range(DC):
                nc.tensor.matmul(s2, ones[:], sim2[:, c, :], start=(c == 0), stop=(c == DC - 1))
            for c in range(DC):
                last = nc.tensor.matmul(r2, rep2[:, c, :], ones[:, 0:1], start=(c == 0), stop=(c == DC - 1))
            last.then_inc(aff_ps, 1)
            pe.wait_ge(r_ok, 1)
            for kind in range(2):
                last = nc.tensor.transpose(banks[1][:, kind * NB:(kind + 1) * NB],
                                           route[:, kind].rearrange("p r e -> p (r e)"), pr.ident[0:NB, 0:NB])
            last.then_inc(rT_ps, 1)
            pe.wait_ge(pr.em_loaded, 16)
            pe.wait_ge(rT_ok, 1)
            for n in range(NMIX):
                kind, m = divmod(n, NMIX // 2)
                if n >= len(b_m):
                    before_n = n - len(b_m)
                    pe.wait_ge(mix_ok[before_n % 2], before_n // 2 + 1)
                nc.tensor.matmul(b_m[n % len(b_m)][0:RG * NB, :], routeT[:, kind].rearrange("p g b -> p (g b)"),
                                 w[:, kind, m * MC:(m + 1) * MC], start=True, stop=True).then_inc(mix_ps, 1)
            pe.wait_ge(mixed_in[0], 16 * 2 * RG)
            for parity in range(2):
                pe.wait_ge(mix_ok[parity], NMIX // 2)
            for n in range(4):
                c, half = n % 2, n // 2
                for b in range(4):
                    last = nc.tensor.transpose(banks[4 + n][:, b * P:(b + 1) * P],
                                               mixed[:, 0, 4 * half + b, c * P:(c + 1) * P], pr.ident[:])
                last.then_inc(wt_ps, 1)

            def hidden(b):
                if b >= 2:
                    pe.wait_ge(h_ok, b - 1)
                for c in range(DC):
                    last = nc.tensor.matmul(banks[b % 2][:, 0:2 * P], wvT[:, c, b, :],
                                            xT[:, c, 2 * b:2 * b + 2, :].rearrange("p b t -> p (b t)"),
                                            start=(c == 0), stop=(c == DC - 1))
                last.then_inc(h_ps, 1)

            def outputs(b):
                pe.wait_ge(h_ok, b + 1)
                if b >= 2:
                    pe.wait_ge(x_ok, b - 1)
                for odd in range(2):
                    rows = slice(H * odd, H * odd + H)
                    last = nc.tensor.matmul(banks[2 + 2 * (b % 2) + odd][:, 0:D], hT[rows, b % 2, :],
                                            mixed[rows, 1, b, :], start=True, stop=True)
                last.then_inc(o_ps, 1)

            pe.wait_ge(xT_ok, NG * DC)
            for part in wt_ok:
                pe.wait_ge(part, 1)
            hidden(0)
            hidden(1)
            for b in range(NP):
                if b == 0:
                    pe.wait_ge(mixed_in[1], 16 * 2 * RG)
                    for part in wt_ok:
                        pe.wait_ge(part, 2)
                outputs(b)
                if b + 2 < NP:
                    hidden(b + 2)

        @block.scalar
        def _(act):
            with act.Fori(0, NG) as it:
                for c in range(DC):
                    act.wait_ge(norm.s_tr, it * DC + c + 1)
                    nc.scalar.copy(xT[:, c, bass.ds(it * G, G), :],
                                   banks[c][:, :].rearrange("p (j t) -> p j t", j=G)).then_inc(xT_ok, 1)
            act.wait_ge(loaded, 64)
            nc.scalar.activation(sig[:], gates[:], ACT.Exp, scale=-1.0).then_inc(sig_ok, 1)
            act.wait_ge(exp_in, 1)
            nc.scalar.activation(gated[:], gated[:], ACT.Exp, bias=small[:, 2:3],
                                 accum_out=small[:, 3:4]).then_inc(exp_ok, 1)
            for n in range(0, NMIX, 2):
                kind, m = divmod(n, NMIX // 2)
                act.wait_ge(mix_ps, n + 1)
                nc.scalar.copy(w[0:RG * NB, kind, m * MC:(m + 1) * MC], b_m[n % len(b_m)][0:RG * NB, :])\
                    .then_inc(mix_ok[0], 1)
            for n in (0, 2):
                act.wait_ge(wt_ps, n + 1)
                nc.scalar.copy(wvT[:, 0, 2 * n:2 * n + 4, :], banks[4 + n][:, :]
                               .rearrange("p (b h) -> p b h", b=4)).then_inc(wt_ok[0], 1)
            for b in range(NP):
                act.wait_ge(h_ps, b + 1)
                if b >= 2:
                    act.wait_ge(o_ps, b - 1)
                nc.scalar.copy(hT[0:H, b % 2, :], banks[b % 2][0:H, 0:P])
                nc.scalar.copy(hT[H:P, b % 2, :], banks[b % 2][H:P, P:2 * P]).then_inc(h_ok, 1)

        @block.vector
        def _(dve):
            def mean_group(it):
                norm.vector_stats(dve, it)
                if not isinstance(it, int):
                    dve.wait_ge(rep_ps, it)
                norm.vector_apply(dve, it)

            mean_group(0)
            with dve.Fori(1, NG) as it:
                mean_group(it)
            chain = Chain(dve, chain_s, 0, 21)
            dve.wait_ge(loaded, 64)
            nc.vector.tensor_tensor(sim2[:], sim[:], sim[:], ALU.mult).then_inc(rep_ok, 1)
            dve.wait_ge(sig_ok, 1)
            chain.done(nc.vector.tensor_scalar(sig[:], sig[:], 1.0, None, ALU.add))
            chain.done(nc.vector.reciprocal(sig[:], sig[:]))
            dve.wait_ge(rep_ps, NG)
            chain.done(nc.vector.tensor_scalar(rep[:], banks[7][:, 0:DC * NB].rearrange("p (c b) -> p c b", c=DC),
                                               1.0 / P, None, ALU.mult))
            nc.vector.tensor_tensor(rep2[:], rep[:], rep[:], ALU.mult).then_inc(rep_ok, 2)
            dve.wait_ge(aff_ps, 1)
            nc.vector.tensor_copy(simn[:], banks[3][0:NB, 0:E]).then_inc(rn_in, 1)
            nc.vector.tensor_copy(repn[:], banks[4][0:NB, 0:1]).then_inc(rn_in, 1)
            dve.wait_ge(rn_ok, 2)
            chain.done(nc.vector.tensor_scalar(logit[:], banks[2][0:NB, 0:E], repn[:, 0:1], None, ALU.mult))
            chain.done(nc.vector.tensor_tensor(logit[:], logit[:], simn[:], ALU.mult))
            chain.done(nc.vector.tensor_tensor(logit[:], logit[:], sig[:], ALU.subtract))
            chain.done(nc.vector.tensor_scalar(gated[:], logit[:], 0.0, None, ALU.max))
            chain.done(nc.vector.tensor_scalar(act_mask[:], gated[:], 0.0, None, ALU.is_gt))
            chain.done(nc.vector.tensor_reduce(small[:, 0:1], act_mask[:], AX, ALU.add))
            chain.done(nc.vector.tensor_scalar(small[:, 1:2], small[:, 0:1], 0.0, None, ALU.is_equal))
            ahead = logit[:].unsqueeze(1).to_broadcast([NB, E, E])
            self_ = logit[:].unsqueeze(2).to_broadcast([NB, E, E])
            nc.vector.tensor_tensor(more[:], ahead, self_, ALU.is_gt)
            chain.done(nc.vector.tensor_tensor(tied[:], ahead, self_, ALU.is_equal))
            chain.done(nc.vector.tensor_tensor(tied[:], tied[:], before[:], ALU.mult))
            chain.done(nc.vector.tensor_tensor(more[:], more[:], tied[:], ALU.add))
            chain.done(nc.vector.tensor_reduce(rank[:], more[:], AX, ALU.add))
            chain.done(nc.vector.tensor_scalar(rank[:], rank[:], K - 0.5, small[:, 1:2], ALU.is_lt, ALU.mult))
            chain.done(nc.vector.tensor_tensor(act_mask[:], act_mask[:], rank[:], ALU.max))
            chain.done(nc.vector.tensor_tensor(gated[:], gated[:], act_mask[:], ALU.mult))
            chain.done(nc.vector.tensor_scalar(rank[:], act_mask[:], 1.0, BIG, ALU.subtract, ALU.mult))
            chain.done(nc.vector.tensor_tensor(gated[:], gated[:], rank[:], ALU.add))
            chain.done(nc.vector.tensor_reduce(small[:, 1:2], gated[:], AX, ALU.max))
            nc.vector.tensor_scalar(small[:, 2:3], small[:, 1:2], -1.0, None, ALU.mult).then_inc(exp_in, 1)
            dve.wait_ge(exp_ok, 1)
            nc.vector.reciprocal(small[:, 4:5], small[:, 3:4]).then_inc(chain_s, 1)
            dve.wait_ge(chain_s, chain.n + 1)
            nc.vector.tensor_scalar(route[:, 1], gated[:].unsqueeze(1).to_broadcast([NB, RG, E]), small[:, 4:5],
                                    None, ALU.mult).then_inc(chain_s, 1)
            dve.wait_ge(chain_s, chain.n + 2)
            nc.vector.tensor_tensor(route[:, 0], route[:, 1], act_mask[:].unsqueeze(1).to_broadcast([NB, RG, E]),
                                    ALU.mult).then_inc(r_ok, 1)
            dve.wait_ge(rT_ps, 1)
            for kind in range(2):
                last = nc.vector.tensor_tensor(
                    routeT[:, kind], banks[1][:, kind * NB:(kind + 1) * NB].unsqueeze(1).to_broadcast([P, RG, NB]),
                    row_group[:].unsqueeze(2).to_broadcast([P, RG, NB]), ALU.mult)
            last.then_inc(rT_ok, 1)
            for n in range(1, NMIX, 2):
                kind, m = divmod(n, NMIX // 2)
                dve.wait_ge(mix_ps, n + 1)
                nc.vector.tensor_copy(w[0:RG * NB, kind, m * MC:(m + 1) * MC], b_m[n % len(b_m)][0:RG * NB, :])\
                    .then_inc(mix_ok[1], 1)
            for n in (1, 3):
                dve.wait_ge(wt_ps, n + 1)
                nc.vector.tensor_copy(wvT[:, 1, 2 * (n - 1):2 * (n - 1) + 4, :], banks[4 + n][:, :]
                                      .rearrange("p (b h) -> p b h", b=4)).then_inc(wt_ok[1], 1)
            for b in range(NP):
                dve.wait_ge(o_ps, b + 1)
                for odd in range(2):
                    last = nc.vector.tensor_tensor(x[:, 2 * b + odd, :], banks[2 + 2 * (b % 2) + odd][:, 0:D],
                                                   x[:, 2 * b + odd, :], ALU.add)
                last.then_inc(x_ok, 1)


def stage_linear_attention_and_expert_mix(pr):
    nc = pr.nc
    with ExitStack() as ctx:
        pr.em_w = ctx.enter_context(nc.sbuf_tensor("em_w", [P, 2, 4096], F32))
        stage_linear_attention(pr)
        pr.release_semaphores()
        stage_expert_mix(pr)


def store_output(pr):
    nc, io = pr.nc, pr.io
    stored = pr.sem("stored")
    with nc.Block() as block:
        @block.sync
        def _(sp):
            sp.dma_start(io["out"].rearrange("b t d -> t b d"), pr.x[:]).then_inc(stored, 16)
            sp.wait_ge(stored, 16)


def build(nc, io, stages):
    pr = Program(nc, io)
    with ExitStack() as ctx:
        pr.x = ctx.enter_context(nc.sbuf_tensor("x", [P, NB, D], F32))
        pr.ident = ctx.enter_context(nc.sbuf_tensor("ident", [P, P], F32))
        pr.wait_slot = ctx.enter_context(nc.sbuf_tensor("wait_slot", [1, 1], F32))
        pr.minus_half = ctx.enter_context(nc.sbuf_tensor("minus_half", [P, G], F32))
        pr.ones_row = ctx.enter_context(nc.sbuf_tensor("ones_row", [1, P], F32R))
        pr.ones_row32 = ctx.enter_context(nc.sbuf_tensor("ones_row32", [1, P], F32))
        pr.banks = [ctx.enter_context(nc.psum_tensor(f"bank{n}", [P, 512], F32)) for n in range(8)]
        pr.x_loaded = [pr.sem(f"x_loaded{t}") for t in range(NG)]
        pr.const_ok = pr.sem("consts_ready")
        pr.em_loaded = nc.alloc_semaphore(name="em_w_loaded")
        for stage in STAGES[:stages]:
            stage(pr)
            if stage is not STAGES[-1]:
                pr.release_semaphores()
        if stages < len(STAGES):
            store_output(pr)


STAGES = [stage_lora_attention, stage_long_conv, stage_experts_and_wide_attention,
          stage_linear_attention_and_expert_mix]


def kernel(**inputs):
    import numpy as np
    import concourse.bacc as bacc
    from concourse.bass_utils import run_bass_kernel_spmd

    a = {n: np.asarray(v) for n, v in inputs.items()}

    def chunks(w):
        return w.reshape(DC, P, -1).transpose(1, 0, 2)

    r = {}
    r["x"] = a["x"]
    r["ident"] = np.eye(P, dtype=np.float32)
    odd = (np.arange(P) // 16) % 2
    r["parity"] = np.stack([1 - odd, odd], axis=1).astype(np.float32)
    qkvo = "qkvo"
    r["l0_w"] = np.stack([chunks(a[f"L0_attn_W{n}"].T) for n in qkvo], axis=1)
    r["l0_a"] = np.stack([a[f"L0_attn_A{n}"].T for n in qkvo], axis=1)
    r["l0_b"] = np.stack([a[f"L0_attn_B{n}"] for n in qkvo], axis=1)
    r["l0_qk_bias"] = np.stack([a["L0_attn_bq"].reshape(DC, P).T, a["L0_attn_bk"].reshape(DC, P).T], axis=1)
    r["l0_v_bias"] = a["L0_attn_bv"].reshape(DC, P).T
    r["l0_o_bias"] = np.broadcast_to(a["L0_attn_bo"], (P, D))

    r["ctx_rev"] = a["ctx_2048"].transpose(2, 0, 1).reshape(DC, P, NB, P)[:, ::-1].transpose(1, 0, 2, 3)
    kpad = np.concatenate([np.zeros((16, P - 1), np.float32), a["L0_xattn_ssm_kernel"]], axis=1)
    r["toeplitz"] = np.lib.stride_tricks.sliding_window_view(kpad, 2 * P, axis=1).transpose(1, 0, 2)
    r["conv_d"] = np.broadcast_to(a["L0_xattn_D"], (P, 16))
    r["anti"] = np.eye(P, dtype=np.float32)[::-1]
    r["le_w"] = np.concatenate([chunks(a["L0_ffn_W"].T), chunks(a["L0_ffn_A"].reshape(P, D).T),
                                chunks(a["L0_ffn_gate_w"].T)], axis=2)
    r["le_u"] = a["L0_ffn_B"].transpose(0, 2, 1).reshape(P, D)
    r["before8"] = np.broadcast_to(np.tril(np.ones((8, 8), np.float32), -1), (P, 8, 8))
    wide = [chunks(a[f"L1_attn_W_{n}"].reshape(-1, D).T).reshape(P, -1) for n in "QKV"]
    wide.append(a["L1_attn_W_O"].T.reshape(16, P, D).transpose(1, 0, 2).reshape(P, -1))
    r["wide_w"] = np.stack(wide)
    r["causal"] = np.tile(np.triu(np.full((P, P), -1e30, np.float32), 1), (1, G)).astype(mybir.dt.np(BF16))
    r["ident_b"] = np.eye(P, dtype=np.float32).astype(mybir.dt.np(BF16))

    reverse = lambda t: t.reshape(DC, P, -1)[:, ::-1].transpose(1, 0, 2)
    wk = a["L1_xattn_Wk"].reshape(D, DC, P)[:, :, ::-1].reshape(D, D)
    r["li_wqk"] = np.stack([chunks(a["L1_xattn_Wq"]), chunks(wk)], axis=1)
    wf = np.zeros((8, 16, 2, 8, 64), np.float32)
    for n, name in enumerate("qk"):
        for h in range(8):
            wf[h, :, n, h] = a[f"L1_xattn_W{name}f"].T
    r["li_wf"] = wf.reshape(P, 2, 512)
    bqk = np.stack([a[f"L1_xattn_b{n}"].reshape(DC, P).T for n in "qk"], axis=1)
    r["li_bqk"] = np.repeat(bqk[..., None], 2, axis=-1)
    r["li_vo"] = np.stack([reverse(a["L1_xattn_Wv"].T), chunks(a["L1_xattn_Wo"].T)], axis=1)
    r["li_v_row"] = np.stack([a["L1_xattn_bv"]] * 2)
    r["li_o_bias"] = np.broadcast_to(a["L1_xattn_bo"], (P, D))
    r["li_sign"] = np.stack([np.r_[-np.ones(P), 0], np.ones(P + 1)]).astype(np.float32)
    r["li_mask"] = a["mask_BxS2_ff1"].T
    by_quarter = lambda w: w.reshape(32, 4, -1).transpose(1, 0, 2).reshape(P, -1)
    r["em_w"] = np.stack([by_quarter(a["L1_ffn_w_v"]), by_quarter(a["L1_ffn_o_weights"])], axis=1)
    r["em_row_group"] = np.repeat(np.eye(4, dtype=np.float32), 32, axis=0)
    r["em_sim"] = chunks(a["L1_ffn_sim_matrix"])
    r["em_gates"] = np.broadcast_to(a["L1_ffn_gates"], (NB, 32))
    r["before32"] = np.broadcast_to(np.tril(np.ones((32, 32), np.float32), -1), (NB, 32, 32))

    nc = bacc.Bacc("TRN2", target_bir_lowering=False, num_devices=1)
    arrays, io = {}, {}
    for name, v in r.items():
        v = np.ascontiguousarray(v)
        arrays[f"in_{name}"] = v
        io[name] = nc.dram_tensor(f"in_{name}", v.shape, mybir.dt.from_np(v.dtype), kind="ExternalInput").ap()
    io["out"] = nc.dram_tensor("out_x", (NB, P, D), F32, kind="ExternalOutput").ap()
    build(nc, io, len(STAGES))
    got = run_bass_kernel_spmd(nc, [arrays], core_ids=[0])
    return got.results[0]["out_x"]
```

```python
from contextlib import ExitStack

import concourse.bass as bass
from concourse import mybir

F32 = mybir.dt.float32
F32R = mybir.dt.float32r
ALU = mybir.AluOpType
ACT = mybir.ActivationFunctionType
AX = mybir.AxisListType.X

P = 128
NB = 16
G = 4
NG = NB // G
D = 256
DC = D // P
GT = G * P
EPS = 1e-5
ONE = 1
BASE = 2


class Chain:

    def __init__(self, eng, sem, it, per):
        self.eng, self.sem, self.it, self.per, self.n = eng, sem, it, per, 0

    def done(self, ins):
        self.n += 1
        ins.then_inc(self.sem, 1)
        self.eng.wait_ge(self.sem, self.it * self.per + self.n)

    def close(self):
        assert self.n == self.per, (self.n, self.per)


def product(nc, out, a, b, start, stop):
    nc.tensor.matmul(out, a[0], b[0], start=start, stop=False, skip_group_check=True)
    nc.tensor.matmul(out, a[0], b[1], start=False, stop=False, skip_group_check=True)
    return nc.tensor.matmul(out, a[1], b[0], start=False, stop=stop, skip_group_check=True)


def pair(t, *index):
    return t[0][index], t[1][index]


class Program:
    def __init__(self, nc, io):
        self.nc, self.io = nc, io
        self.sems = []

    def sem(self, name):
        self.sems.append(self.nc.alloc_semaphore(name=name))
        return self.sems[-1]

    def release_semaphores(self):
        self.nc.clear_and_free_semaphores(self.sems)
        self.nc.all_engine_barrier()
        self.sems = []


class Norm:

    def __init__(self, pr, ctx):
        nc = pr.nc
        self.nc, self.pr = nc, pr
        sb = lambda n, shape, dt: ctx.enter_context(nc.sbuf_tensor(f"norm_{n}", shape, dt))
        self.stats = sb("stats", [P, G, 6], F32)
        self.meanvar = sb("meanvar", [P, G, 2], F32)
        self.rstd = sb("rstd", [P, G], F32)
        self.xn = sb("xn", [P, G, D], F32)
        self.xT = (sb("xT_hi", [P, DC, GT], F32R), sb("xT_lo", [P, DC, GT], F32R))
        sem = lambda n: nc.alloc_semaphore(name=f"norm_{n}")
        self.s_chain = sem("chain")
        self.s_var = sem("var_ready")
        self.s_pool = sem("rstd_ready")
        self.s_xn = sem("xn_ready")
        self.s_tr = sem("xT_in_psum")
        self.s_hi = sem("xT_hi_ready")
        self.s_lo = sem("xT_ready")

    def enter_stage(self, stage, split_stages, banks):
        self.base, self.split_base, self.banks = stage * NG, split_stages * NG, banks

    def done(self, it):
        return it + (self.base + 1)

    def split(self, it):
        return it + (self.split_base + 1)

    def vector_norm(self, dve, it):
        self.vector_stats(dve, it)
        self.vector_apply(dve, it)

    def vector_stats(self, dve, it):
        nc, x = self.nc, self.pr.x
        g = it % NG if isinstance(it, int) else it
        chain = Chain(dve, self.s_chain, self.base + it, 2)
        for j in range(G):
            last = nc.vector.bn_stats(self.stats[:, j, :], x[:, g * G + j, :])
        chain.done(last)
        nc.vector.memset(self.pr.wait_slot[:], 0.0)
        for j in range(G):
            last = nc.vector.bn_aggr(self.meanvar[:, j, :], self.stats[:, j, :])
        chain.done(last)
        chain.close()
        nc.vector.tensor_scalar(self.rstd[:], self.meanvar[:, :, 1], EPS, None, ALU.add).then_inc(self.s_var, 1)

    def vector_apply(self, dve, it):
        nc, x = self.nc, self.pr.x
        g = it % NG if isinstance(it, int) else it
        dve.wait_ge(self.s_pool, self.done(it))
        for j in range(G):
            last = nc.vector.tensor_scalar(self.xn[:, j, :], x[:, g * G + j, :], self.meanvar[:, j, 0:1],
                                           self.rstd[:, j:j + 1], ALU.subtract, ALU.mult)
        last.then_inc(self.s_xn, 1)

    def pool_rstd(self, pool, it):
        pool.wait_ge(self.s_var, self.done(it))
        self.nc.gpsimd.tensor_tensor(self.rstd[:], self.rstd[:], self.pr.minus_half[:], ALU.pow)\
            .then_inc(self.s_pool, 1)

    def tensor_transpose(self, pe, it):
        pe.wait_ge(self.s_xn, self.done(it))
        for c in range(DC):
            for j in range(G):
                last = self.nc.tensor.transpose(self.banks[c][:, j * P:(j + 1) * P],
                                                self.xn[:, j, c * P:(c + 1) * P], self.pr.ident[:])
            last.then_inc(self.s_tr, 1)

    def scalar_hi(self, act, it, out=None):
        for c in range(DC):
            act.wait_ge(self.s_tr, DC * (self.done(it) - 1) + c + 1)
            self.nc.scalar.copy((self.xT[0] if out is None else out)[:, c, :], self.banks[c][:, :])\
                .then_inc(self.s_hi, 1)

    def vector_lo(self, dve, it):
        for c in range(DC):
            dve.wait_ge(self.s_hi, DC * (self.done(it) - 1) + c + 1)
            self.nc.vector.tensor_tensor(self.xT[1][:, c, :], self.banks[c][:, :],
                                         self.xT[0][:, c, :].bitcast(F32), ALU.subtract).then_inc(self.s_lo, 1)


def stage_lora_attention(pr):
    nc, io, x, banks = pr.nc, pr.io, pr.x, pr.banks
    H, HD, R = 16, 16, 16
    RG = 4
    U = G * RG
    LORA = 0.5
    SCALE = HD ** -0.5
    b_p, b_s, b_t, b_v = banks[0:2], banks[2:6], banks[6], banks[7]
    with ExitStack() as ctx:
        sb = lambda n, shape, dt=F32: ctx.enter_context(nc.sbuf_tensor(f"la_{n}", shape, dt))
        sem = lambda n: pr.sem(f"la_{n}")
        norm = pr.norm
        norm.enter_stage(0, 0, b_p)
        w_raw = sb("w_raw", [P, 4, DC, D])
        lora_a = sb("lora_a", [R, 4, D])
        lora_b = sb("lora_b", [R, 4, D])
        w = (sb("w_hi", [P, 4, DC, D], F32R), sb("w_lo", [P, 4, DC, D], F32R))
        qk_bias = sb("qk_bias", [P, 2, DC])
        v_bias = sb("v_bias", [P, DC])
        out_bias = sb("out_bias", [P, D])
        parity = sb("parity", [P, 2])
        q = sb("q", [P, 2, DC, GT])
        k = sb("k", [P, DC, GT])
        DIAG = P + HD
        v = pr.shared[:, 0:2 * (G * H * P + P)].rearrange("p (n c) -> p n c", n=2)
        negmax = sb("negmax", [P, 2, 4])
        sums = sb("sums", [P, 2, H])
        rsum = sb("rsum", [P, 2, H])
        prob = sb("prob", [P, 2, 4, P])
        probT = sb("probT", [P, 2, 4, P])
        o = sb("o", [P, 2, D])
        oT = (sb("oT_hi", [P, 2, DC, P], F32R), sb("oT_lo", [P, 2, DC, P], F32R))

        loaded = sem("weights_loaded")
        w_ps, w_f32, w_hi, w_lo = sem("w_in_psum"), sem("w_f32"), sem("w_hi"), sem("w_ready")
        bias_ps, bias_ok, xb_ok = sem("bias_in_psum"), sem("bias_ready"), sem("x_biased")
        q_ps, q_ok = sem("q_in_psum"), sem("q_ready")
        k_ps, k_ok = sem("k_in_psum"), sem("k_ready")
        v_ps, v_ok = sem("v_in_psum"), sem("v_ready")
        s_ps, max_ok, exp_ok = sem("scores_in_psum"), sem("negmax_ready"), sem("probs_ready")
        t_ps, t_ok = sem("probsT_in_psum"), sem("probsT_ready")
        av_ps, av_ok = sem("av_in_psum"), sem("o_ready")
        ot_ps, ot_hi, ot_lo = sem("oT_in_psum"), sem("oT_hi_ready"), sem("oT_ready")
        o_ps, x_ok = sem("out_in_psum"), sem("x_updated")
        chain_s = sem("vector_chain")
        v_zero = sem("v_cleared")
        lora_loaded = sem("lora_loaded")
        NLOAD = 6
        block = ctx.enter_context(nc.Block())

        T_STATS, T_APPLY, T_TURN, T_V, T_Q, T_K = 2, 4, 7, 8, 11, 12
        T_SKIP = (7, 8, 11, 12)
        TURN_O, PROJECT = 5, 6

        ORDER = (2, 0, 1, 3)

        def head(r, s):
            return (s // 2) * 8 + 2 * r + s % 2

        def due(u, first):
            return (u - first) // RG if u >= first and (u - first) % RG == 0 else None

        def load_x(eng, t):
            eng.dma_start(x[:, t * G:(t + 1) * G, :],
                          io["x"][t * G:(t + 1) * G].rearrange("b t d -> t b d")).then_inc(pr.x_loaded[t], 16)

        @block.sync
        def _(sp):
            sp.dma_start(lora_b[:], io["l0_b"]).then_inc(lora_loaded, 16)
            sp.dma_start(lora_a[:], io["l0_a"]).then_inc(lora_loaded, 16)
            load_x(sp, 0)
            sp.dma_start(w_raw[:], io["l0_w"]).then_inc(loaded, 16)
            sp.wait_ge(loaded, 16 * NLOAD)
            for t in range(1, NG):
                load_x(sp, t)
            sp.dma_start(pr.kt[:], io["ctx_rev"].rearrange("p a b (h c) -> p a (b h) c", c=CONV_C))\
                .then_inc(pr.conv_loaded, 16)
            sp.dma_start(pr.toep[:], io["toeplitz"]).then_inc(pr.conv_loaded, 16)
            sp.dma_start(pr.skip[:], io["conv_d"]).then_inc(pr.conv_loaded, 16)
            sp.dma_start(pr.anti[:], io["anti"]).then_inc(pr.conv_loaded, 16)

        @block.gpsimd
        def _(pool):
            nc.gpsimd.memset(pr.minus_half[:], -0.5).then_inc(pr.const_ok, 1)
            pool.wait_ge(pr.const_ok, 1)
            nc.gpsimd.memset(v[:, 0, :], 0.0).then_inc(v_zero, 1)
            norm.pool_rstd(pool, 0)
            nc.gpsimd.memset(v[:, 1, :], 0.0).then_inc(v_zero, 1)
            pool.wait_ge(bias_ok, 1)

            def add_bias(it):
                pool.wait_ge(norm.s_xn, norm.done(it))
                nc.gpsimd.tensor_tensor(x[:, bass.ds(it * G, G), :], x[:, bass.ds(it * G, G), :],
                                        out_bias[:].unsqueeze(1).to_broadcast([P, G, D]), ALU.add).then_inc(xb_ok, 1)

            add_bias(0)
            with pool.Fori(1, NG) as it:
                norm.pool_rstd(pool, it)
                add_bias(it)
            norm.pool_rstd(pool, NG)
            pool.wait_ge(pr.conv_loaded, 16 * 4)
            pool.wait_ge(av_ok, BASE + (NG - 1) * G)
            conv_products(pr, nc.gpsimd, 0)
            conv_squares(pr, nc.gpsimd, 0)

        @block.tensor
        def _(pe):
            xT = norm.xT

            def q_or_k(it, n, done):
                for m in range(DC):
                    if n == 0:
                        pe.wait_ge(norm.s_lo, DC * norm.split(it))
                        pe.wait_ge(v_ok, it * 2 + m + 1)
                    else:
                        pe.wait_ge(q_ok, it * DC + m + 1)
                    for c in range(DC):
                        last = product(nc, b_p[m][:, :], pair(w, slice(None), n, c, slice(m * P, m * P + P)),
                                       pair(xT, slice(None), c), c == 0, c == DC - 1)
                    last.then_inc(done, 1)

            def values(it):
                pe.wait_ge(norm.s_lo, DC * norm.split(it))
                for half in range(2):
                    for jj in range(2):
                        j = 2 * half + jj
                        for c in range(DC):
                            last = product(nc, b_p[half][:, jj * D:(jj + 1) * D],
                                           pair(xT, slice(None), c, slice(j * P, j * P + P)),
                                           pair(w, slice(None), 2, c), jj == 0 and c == 0, c == DC - 1)
                    last.then_inc(v_ps, 1)

            def scores(it, u):
                for s in range(4):
                    for d in range(2):
                        j, r = divmod((u + d) % U, RG)
                        if s == 0:
                            pe.wait_ge(exp_ok, it * U + u + d + 1)
                        rows = slice(32 * r, 32 * r + 32)
                        m, e = divmod(s, 2)
                        last = nc.tensor.matmul(b_s[r][:, s * P:(s + 1) * P],
                                                q[rows, e, m, j * P:(j + 1) * P],
                                                k[rows, m, j * P:(j + 1) * P], start=True, stop=True)
                        if s == 3:
                            last.then_inc(s_ps, 1)

            def turn(it, u):
                pe.wait_ge(exp_ok, RG + it * U + u + 1)
                pe.wait_ge(t_ok, ONE + it * U + u)
                for s in range(4):
                    last = nc.tensor.transpose(b_t[:, s * P:(s + 1) * P], prob[:, u % 2, s, :], pr.ident[:])
                last.then_inc(t_ps, 1)

            def weigh(it, u):
                j, r = divmod(u, RG)
                pe.wait_ge(t_ok, ONE + it * U + u + 1)
                if r == 0:
                    pe.wait_ge(av_ok, BASE + it * G + j)
                for s in range(4):
                    at = (j * H + head(r, s)) * P
                    last = nc.tensor.matmul(b_v[:, s // 2 * P:(s // 2 + 1) * P], probT[:, u % 2, s, :],
                                            v[:, it % 2, at:at + P], start=(r == 0 and s == 0),
                                            stop=(r == RG - 1), skip_group_check=True)
                last.then_inc(av_ps, 1)

            def turn_o(it, j, last):
                pe.wait_ge(av_ok, BASE + it * G + j + 1)
                pe.wait_ge(ot_lo, ONE + it * G + j)
                if not last and j in (1, 2):
                    pe.wait_ge((v_ok, k_ok)[j - 1], (it + 1) * 2 + 1)
                for c in range(DC):
                    ins = nc.tensor.transpose(b_p[0][:, c * P:(c + 1) * P], o[:, j % 2, c * P:(c + 1) * P],
                                              pr.ident[:])
                ins.then_inc(ot_ps, 1)

            def project(it, j, last):
                pe.wait_ge(ot_lo, ONE + it * G + j + 1)
                pe.wait_ge(x_ok, ONE + it * G + j)
                if not last and j in (1, 2):
                    pe.wait_ge((v_ok, k_ok)[j - 1], (it + 1) * 2 + 2)
                for c in range(DC):
                    ins = product(nc, b_p[1][:, 0:D], pair(oT, slice(None), j % 2, c), pair(w, slice(None), 3, c),
                                  c == 0, c == DC - 1)
                ins.then_inc(o_ps, 1)

            def group(it, last):
                for u in range(U + 3):
                    if u < U and u != 1:
                        turn(it, u)
                    if u % 2 == 1 and u + 1 < U and (u + 4 < U or not last):
                        if u + 3 == U:
                            pe.wait_ge(q_ok, (it + 1) * DC + DC)
                            pe.wait_ge(k_ok, (it + 1) * DC + DC)
                        scores(it, u + 3)
                    if u == 1:
                        turn(it, u)
                    if 1 <= u <= U:
                        weigh(it, u - 1)
                    if u == U and not last:
                        scores(it, U + 2)
                    if due(u, TURN_O) is not None:
                        turn_o(it, due(u, TURN_O), last)
                    if due(u, PROJECT) is not None:
                        project(it, due(u, PROJECT), last)
                    if last:
                        continue
                    if u == T_TURN:
                        pe.wait_ge(x_ok, ONE + it * G + 1)
                        norm.tensor_transpose(pe, it + 1)
                    if u == T_V:
                        values(it + 1)
                    if u == T_Q:
                        pe.wait_ge(x_ok, ONE + it * G + 2)
                        q_or_k(it + 1, 0, q_ps)
                    if u == T_K:
                        q_or_k(it + 1, 1, k_ps)

            pe.wait_ge(lora_loaded, 16 * 2)
            for n in ORDER:
                for c in range(DC):
                    last = nc.tensor.matmul(b_s[n][:, c * D:(c + 1) * D], lora_b[:, n, c * P:(c + 1) * P],
                                            lora_a[:, n, :], start=True, stop=True)
                last.then_inc(w_ps, 1)
            pe.wait_ge(loaded, 16 * NLOAD)
            norm.tensor_transpose(pe, 0)
            pe.wait_ge(w_f32, 4)
            for c in range(DC):
                last = nc.tensor.matmul(b_t[:, 0:D], v_bias[:, c:c + 1].to_broadcast([P, P]), w_raw[:, 3, c, :],
                                        start=(c == 0), stop=(c == DC - 1))
            last.then_inc(bias_ps, 1)
            for event in (t_ps, av_ps, ot_ps, o_ps):
                pe.sem_inc(event, BASE)
            pe.wait_ge(w_lo, 1)
            values(0)
            pe.wait_ge(w_lo, 2)
            q_or_k(0, 0, q_ps)
            pe.wait_ge(w_lo, 4)
            q_or_k(0, 1, k_ps)
            pe.wait_ge(q_ok, DC)
            pe.wait_ge(k_ok, DC)
            scores(0, 0)
            scores(0, 2)
            with pe.Fori(0, NG - 1) as it:
                group(it, False)
            group(NG - 1, True)

        @block.scalar
        def _(act):
            act.dma_start(pr.ident[:], io["ident"]).then_inc(loaded, 16)
            act.dma_start(v_bias[:], io["l0_v_bias"]).then_inc(loaded, 16)
            act.dma_start(out_bias[:], io["l0_o_bias"]).then_inc(loaded, 16)
            act.dma_start(qk_bias[:], io["l0_qk_bias"]).then_inc(loaded, 16)
            act.dma_start(parity[:], io["parity"]).then_inc(loaded, 16)

            def keep_k(it):
                for m in range(DC):
                    act.wait_ge(k_ps, it * DC + m + 1)
                    nc.scalar.activation(k[:, m, :], b_p[m][:, :], ACT.Identity,
                                         bias=qk_bias[:, 1, m:m + 1]).then_inc(k_ok, 1)

            def keep_v(it):
                for half in range(2):
                    act.wait_ge(v_ps, it * 2 + half + 1)
                    for jj in range(2):
                        for m in range(DC):
                            at = ((2 * half + jj) * H + 8 * m) * P
                            src = b_p[half][:, jj * D + m * P:jj * D + m * P + P]
                            last = nc.scalar.copy(
                                v[:, it % 2, at:at + 8 * DIAG].rearrange("p (h s) -> p h s", s=DIAG)[:, :, 0:HD],
                                src.rearrange("p (h d) -> p h d", d=HD))
                    last.then_inc(v_ok, 1)

            def exps(it, u):
                n = it * U + u
                j, r = divmod(u % U, RG)
                act.wait_ge(max_ok, n + 1)
                act.wait_ge(t_ps, BASE + n - 1)
                if r == 0:
                    act.wait_ge(av_ok, BASE + it * G + u // RG - 1)
                for s in range(4):
                    h = head(r, s)
                    last = nc.scalar.activation(prob[:, u % 2, s, :], b_s[r][:, s * P:(s + 1) * P], ACT.Exp,
                                                bias=negmax[:, u % 2, s:s + 1], scale=SCALE,
                                                accum_out=sums[:, j % 2, h:h + 1])
                last.then_inc(exp_ok, 1)

            def group(it, last):
                for u in range(U + 2):
                    if 0 < u < U - 1 or (U - 1 <= u <= U and not last):
                        exps(it, u + 1)
                    j = due(u, TURN_O)
                    if j is not None:
                        act.wait_ge(ot_ps, BASE + it * G + j + 1)
                        nc.scalar.copy(oT[0][:, j % 2, :, :],
                                       b_p[0][:, 0:D].rearrange("p (c t) -> p c t", c=DC)).then_inc(ot_hi, 1)
                    if last:
                        continue
                    if u == T_TURN:
                        norm.scalar_hi(act, it + 1)
                    if u == T_V:
                        keep_v(it + 1)
                    if u == T_K:
                        keep_k(it + 1)

            act.sem_inc(exp_ok, RG)
            for m, n in enumerate(ORDER):
                act.wait_ge(w_f32, m + 1)
                nc.scalar.copy(w[0][:, n], w_raw[:, n]).then_inc(w_hi, 1)
                if m == 1:
                    norm.scalar_hi(act, 0)
            act.wait_ge(v_zero, 1)
            keep_v(0)
            keep_k(0)
            exps(0, 0)
            exps(0, 1)
            act.wait_ge(v_zero, 2)
            with act.Fori(0, NG - 1) as it:
                group(it, False)
            group(NG - 1, True)

        @block.vector
        def _(dve):
            def keep_q(it):
                for m in range(DC):
                    dve.wait_ge(q_ps, it * DC + m + 1)
                    for e in range(2):
                        last = nc.vector.tensor_scalar(q[:, e, m, :], b_p[m][:, :], qk_bias[:, 0, m:m + 1],
                                                       parity[:, e:e + 1], ALU.add, ALU.mult)
                    last.then_inc(q_ok, 1)

            def row_max(it, u, chain):
                n = it * U + u
                dve.wait_ge(s_ps, n + 1)
                dve.wait_ge(exp_ok, RG + n - 1)
                chain.done(nc.vector.tensor_reduce(
                    negmax[:, u % 2, :], b_s[u % RG][:, :].rearrange("p (s k) -> p s k", s=4), AX, ALU.max))
                nc.vector.tensor_scalar(negmax[:, u % 2, :], negmax[:, u % 2, :], -SCALE, None, ALU.mult)\
                    .then_inc(max_ok, 1)

            def keep_probT(it, u):
                n = it * U + u
                dve.wait_ge(t_ps, BASE + n + 1)
                dve.wait_ge(av_ps, BASE + n - 1)
                nc.vector.tensor_copy(probT[:, u % 2, :, :], b_t[:, :].rearrange("p (s k) -> p s k", s=4))\
                    .then_inc(t_ok, 1)

            def normalise(it, j, chain):
                dve.wait_ge(exp_ok, RG + it * U + (j + 1) * RG)
                chain.done(nc.vector.reciprocal(rsum[:, j % 2, :], sums[:, j % 2, :]))
                dve.wait_ge(av_ps, BASE + it * U + (j + 1) * RG)
                dve.wait_ge(ot_ps, BASE + it * G + j - 1)
                nc.vector.tensor_tensor(o[:, j % 2, :].rearrange("p (h d) -> p h d", h=H),
                                        b_v[:, 0:D].rearrange("p (h d) -> p h d", h=H),
                                        rsum[:, j % 2, :].unsqueeze(2).to_broadcast([P, H, HD]), ALU.mult)\
                    .then_inc(av_ok, 1)

            def group(it, last):
                chain = Chain(dve, chain_s, it, U + G)
                chain.n = 2
                for u in range(U + 3):
                    if u == 0:
                        keep_probT(it, u)
                    if u + 2 < U or (u < U and not last):
                        row_max(it, u + 2, chain)
                    if 0 < u < U:
                        keep_probT(it, u)
                    if due(u, RG) is not None:
                        normalise(it, due(u, RG), chain)
                    j = due(u, TURN_O)
                    if j is not None:
                        dve.wait_ge(ot_hi, it * G + j + 1)
                        dve.wait_ge(o_ps, BASE + it * G + j - 1)
                        nc.vector.tensor_tensor(oT[1][:, j % 2, :, :],
                                                b_p[0][:, 0:D].rearrange("p (c t) -> p c t", c=DC),
                                                oT[0][:, j % 2, :, :].bitcast(F32), ALU.subtract).then_inc(ot_lo, 1)
                    j = due(u, PROJECT)
                    if j is not None:
                        if j == 0:
                            dve.wait_ge(xb_ok, it + 1)
                        dve.wait_ge(o_ps, BASE + it * G + j + 1)
                        nc.vector.tensor_tensor(x[:, it * G + j, :], b_p[1][:, 0:D], x[:, it * G + j, :],
                                                ALU.add).then_inc(x_ok, 1)
                    if last:
                        if u == T_STATS:
                            dve.wait_ge(x_ok, ONE + G)
                            norm.vector_stats(dve, NG)
                        if u == T_APPLY:
                            norm.vector_apply(dve, NG)
                        if u in T_SKIP:
                            dve.wait_ge(pr.conv_loaded, 16 * 4)
                            n = T_SKIP.index(u) * (CONV_H // 4)
                            add_skip(pr, range(n, n + CONV_H // 4))
                        continue
                    if u == T_STATS:
                        norm.vector_stats(dve, it + 1)
                    if u == T_APPLY:
                        norm.vector_apply(dve, it + 1)
                    if u == T_TURN:
                        norm.vector_lo(dve, it + 1)
                    if u == T_Q:
                        keep_q(it + 1)
                if not last:
                    chain.n -= 2
                chain.close()

            for event in (t_ok, ot_lo, x_ok):
                dve.sem_inc(event, ONE)
            dve.sem_inc(av_ok, BASE)
            dve.wait_ge(pr.x_loaded[0], 16)
            norm.vector_norm(dve, 0)
            dve.wait_ge(loaded, 16 * NLOAD)
            for m, n in enumerate(ORDER):
                dve.wait_ge(w_ps, m + 1)
                nc.vector.scalar_tensor_tensor(w_raw[:, n], b_s[n][:, :].rearrange("p (c o) -> p c o", c=DC),
                                               LORA, w_raw[:, n], ALU.mult, ALU.add).then_inc(w_f32, 1)
            for m, n in enumerate(ORDER):
                if m == 1:
                    norm.vector_lo(dve, 0)
                dve.wait_ge(w_hi, m + 1)
                nc.vector.tensor_tensor(w[1][:, n], w_raw[:, n], w[0][:, n].bitcast(F32), ALU.subtract)\
                    .then_inc(w_lo, 1)
            dve.wait_ge(bias_ps, 1)
            nc.vector.tensor_tensor(out_bias[:], b_t[:, 0:D], out_bias[:], ALU.add).then_inc(bias_ok, 1)
            keep_q(0)
            first = Chain(dve, chain_s, 0, 2)
            row_max(0, 0, first)
            row_max(0, 1, first)
            for t in range(1, NG):
                dve.wait_ge(pr.x_loaded[t], 16)
            with dve.Fori(0, NG - 1) as it:
                group(it, False)
            group(NG - 1, True)


CONV_H, CONV_C = 16, 8
NPAIR = CONV_C * (CONV_C + 1) // 2
OFF = [d * CONV_C - d * (d - 1) // 2 for d in range(CONV_C)]
GH = G * CONV_H


def conv_input(pr, i):
    return pr.kt[:, :, bass.ds(i * GH, GH), :]


def conv_products(pr, eng, i, distances=range(1, CONV_C)):
    own = conv_input(pr, i)
    for d in distances:
        last = eng.tensor_tensor(pr.kk[:, :, :, OFF[d]:OFF[d] + CONV_C - d], own[:, :, :, 0:CONV_C - d],
                                 own[:, :, :, d:CONV_C], ALU.mult)
    return last


def conv_squares(pr, eng, i):
    own = conv_input(pr, i)
    return eng.tensor_tensor(pr.kk[:, :, :, 0:CONV_C], own, own, ALU.mult)


def add_skip(pr, heads):
    for h in heads:
        pr.nc.vector.scalar_tensor_tensor(pr.toep[:, h, 0:P], pr.anti[:], pr.skip[:, h:h + 1], pr.toep[:, h, 0:P],
                                          ALU.mult, ALU.add)


def stage_long_conv(pr):
    nc, io, x, banks = pr.nc, pr.io, pr.x, pr.banks
    H, C = CONV_H, CONV_C
    HALF = 2
    BH = HALF * G * H
    HS = 3
    N = G * NPAIR
    GROUPS = [range(h, min(h + HS, H)) for h in range(0, H, HS)]
    NGR = len(GROUPS)
    b_n, b_c, b_x = banks[0:2], banks[2:6], banks[6:8]
    with ExitStack() as ctx:
        sb = lambda n, shape, dt=F32: ctx.enter_context(nc.sbuf_tensor(f"lc_{n}", shape, dt))
        sem = lambda n: pr.sem(f"lc_{n}")
        norm = pr.norm
        norm.enter_stage(1, 0, b_n)
        xT = sb("xT", [P, DC, GT])
        toep, kk = pr.toep, pr.kk
        YC = HALF * GH * NPAIR
        y = pr.shared[:, YC:3 * YC].rearrange("p (n c) -> p n c", n=2)
        yq = sb("yq", [P, C, BH, C])

        kk_ok, sq_ok = sem("kk_ready"), sem("kk_squares")
        c_ps, c_ok = sem("conv_in_psum"), sem("conv_ready")
        yq_ok, slot_ps, x_ok = sem("yq_ready"), sem("slot_turned"), sem("x_updated")
        block = ctx.enter_context(nc.Block())

        @block.sync
        def _(sp):
            sp.dma_start(pr.le_w32[:], io["le_w"]).then_inc(pr.le_loaded, 16)
            sp.dma_start(pr.le_u32[:], io["le_u"]).then_inc(pr.le_loaded, 16)
            sp.dma_start(pr.le_order[:], io["le_order"]).then_inc(pr.le_loaded, 16)

        VECTOR_D = (4, 2)

        def schedule(eng, body):
            body(0, True, False)
            with eng.Fori(1, NG - 1) as it:
                body(it, False, False)
            body(NG - 1, False, True)

        @block.gpsimd
        def _(pool):
            pool.wait_ge(pr.le_hi, 2)
            nc.gpsimd.tensor_tensor(pr.le_w[1], pr.le_w32[:], pr.le_w[0].bitcast(F32), ALU.subtract)
            nc.gpsimd.tensor_tensor(pr.le_u[1][:], pr.le_u32[:], pr.le_u[0][:].bitcast(F32), ALU.subtract)
            def products(i, distances):
                pool.wait_ge(c_ps, i * NGR)
                conv_products(pr, nc.gpsimd, i, distances).then_inc(kk_ok, 1)
                norm.pool_rstd(pool, i)

            products(1, range(VECTOR_D[0], C))
            with pool.Fori(2, NG) as it:
                products(it, range(VECTOR_D[1], C))
            norm.pool_rstd(pool, NG)

        @block.tensor
        def _(pe):
            def conv(i, first=False):
                if not first:
                    pe.wait_ge(kk_ok, 2 * i)
                    pe.wait_ge(sq_ok, i)
                for g, heads in enumerate(GROUPS):
                    lo_bank, hi_bank = b_c[2 * (g % 2)], b_c[2 * (g % 2) + 1]
                    pe.wait_ge(c_ok, BASE + i * NGR + g - 1)
                    for n, h in enumerate(heads):
                        cols = slice(n * N, (n + 1) * N)
                        early, late = [kk[:, half, :, :].rearrange("p (b h) n -> p b h n", h=H)[:, :, h, :]
                                       for half in range(HALF)]
                        same, across = toep[:, h, 0:P], toep[:, h, P:2 * P]
                        nc.tensor.matmul(lo_bank[:, cols], same, early, start=True, stop=True)
                        nc.tensor.matmul(hi_bank[:, cols], same, late, start=True, stop=False)
                        last = nc.tensor.matmul(hi_bank[:, cols], across, early, start=False, stop=True)
                    last.then_inc(c_ps, 1)

            def sum_slots(i):
                for s in range(C):
                    pe.wait_ge(yq_ok, i * C + s + 1)
                    for j in range(G):
                        for half in range(HALF):
                            first = (half * G + j) * H
                            last = nc.tensor.matmul(
                                b_x[j // 2][:, (j % 2) * D + half * P:(j % 2) * D + half * P + P],
                                yq[:, s, first:first + H, :], pr.ident[:], is_transpose=True,
                                start=(s == 0 and j % 2 == 0 and half == 0), stop=(s == C - 1),
                                skip_group_check=True)
                    last.then_inc(slot_ps, 1)

            def group(i, first, last):
                if not last:
                    conv(i + 1)
                if not first:
                    pe.wait_ge(x_ok, i * G)
                if last:
                    pe.wait_ge(norm.s_hi, DC * norm.done(i))
                    norm.tensor_transpose(pe, NG)
                sum_slots(i)
                if not last:
                    norm.tensor_transpose(pe, i + 1)

            conv(0, first=True)
            norm.tensor_transpose(pe, 0)
            schedule(pe, group)

        @block.scalar
        def _(act):
            def squares(i):
                nc.scalar.activation(kk[:, :, :, 0:C], conv_input(pr, i), ACT.Square).then_inc(sq_ok, 1)

            def keep_conv(i):
                buf = y[:, i % 2, :].rearrange("p (a bh n) -> p a bh n", a=HALF, n=NPAIR)
                for g, heads in enumerate(GROUPS):
                    act.wait_ge(c_ps, i * NGR + g + 1)
                    for half in range(HALF):
                        src = b_c[2 * (g % 2) + half][:, 0:len(heads) * N]
                        dst = buf[:, half].rearrange("p (b h) n -> p h b n", h=H)[:, heads[0]:heads[-1] + 1]
                        ins = nc.scalar.copy(dst, src.rearrange("p (h b n) -> p h b n", b=G, n=NPAIR))
                    ins.then_inc(c_ok, 1)

            def group(i, first, more):
                if not first:
                    act.wait_ge(yq_ok, i * C)
                keep_conv(i + 1)
                if more:
                    squares(i + 2)
                act.wait_ge(yq_ok, (i + 1) * C)
                norm.scalar_hi(act, i + 1, xT)

            act.sem_inc(c_ok, BASE)
            act.wait_ge(pr.le_loaded, 16 * 3)
            nc.scalar.copy(pr.le_w[0], pr.le_w32[:]).then_inc(pr.le_hi, 1)
            nc.scalar.copy(pr.le_u[0][:], pr.le_u32[:]).then_inc(pr.le_hi, 1)
            keep_conv(0)
            squares(1)
            norm.scalar_hi(act, 0, xT)
            group(0, True, True)
            with act.Fori(1, NG - 2) as it:
                group(it, False, True)
            group(NG - 2, False, False)
            norm.scalar_hi(act, NG)

        @block.vector
        def _(dve):
            def add_sums(i):
                dve.wait_ge(slot_ps, (i + 1) * C)
                for j in range(G):
                    nc.vector.tensor_tensor(x[:, i * G + j, :], b_x[j // 2][:, (j % 2) * D:(j % 2) * D + D],
                                            x[:, i * G + j, :], ALU.add).then_inc(x_ok, 1)

            def group(i, first, last):
                if not last:
                    dve.wait_ge(c_ps, (i + 1) * NGR)
                    conv_products(pr, nc.vector, i + 1, range(1, VECTOR_D[0 if first else 1]))\
                        .then_inc(kk_ok, 1)
                if not first:
                    add_sums(i - 1)
                if last:
                    dve.wait_ge(x_ok, G)
                norm.vector_stats(dve, NG if last else i + 1)
                dve.wait_ge(norm.s_hi, DC * norm.done(i))
                norm.vector_apply(dve, NG if last else i + 1)
                dve.wait_ge(c_ok, BASE + (i + 1) * NGR)
                yv = y[:, i % 2, :].rearrange("p (bh n) -> p bh n", n=NPAIR)
                qv = xT[:].rearrange("p a (bh c) -> p (a bh) c", c=C)
                for s in range(C):
                    if not first:
                        dve.wait_ge(slot_ps, (i - 1) * C + s + 1)
                    ins = nc.vector.tensor_tensor(yq[:, s, :, s:C], yv[:, :, OFF[s]:OFF[s] + C - s],
                                                  qv[:, :, 0:C - s], ALU.mult)
                    if s > 0:
                        d = C - s
                        ins = nc.vector.tensor_tensor(yq[:, s, :, 0:s], yv[:, :, OFF[d]:OFF[d] + s],
                                                      qv[:, :, d:C], ALU.mult)
                    ins.then_inc(yq_ok, 1)
                if last:
                    norm.vector_lo(dve, NG)
                    add_sums(i)

            schedule(dve, group)


def stage_lora_experts(pr):
    nc, io, x, banks = pr.nc, pr.io, pr.x, pr.banks
    E, R, TOP, ALPHA = 8, 16, 2, 16.0
    W = D + E * R + E
    b_p, b_o, b_h = banks[0:2], banks[2:6], banks[6:8]
    w, up = pr.le_w, pr.le_u
    with ExitStack() as ctx:
        sb = lambda n, shape, dt=F32: ctx.enter_context(nc.sbuf_tensor(f"le_{n}", shape, dt))
        sem = lambda n: pr.sem(f"le_{n}")
        norm = pr.norm
        norm.enter_stage(2, 1, b_p)
        h = pr.h_or_fold[:].rearrange("p (b n) -> p b n", b=NB)
        logit = sb("logit", [P, NB, E])
        stat = sb("stat", [P, 4, NB])
        prob = sb("prob", [P, NB, E])
        left = sb("left", [P, NB, E])
        is_best = sb("is_best", [P, NB, E])
        order = pr.le_order[:].unsqueeze(1).to_broadcast([P, NB, E])
        rank = sb("rank", [P, NB, E])
        hw = sb("hw", [P, G, E * R])
        hT = (sb("hT_hi", [P, 2, G * P], F32R), sb("hT_lo", [P, 2, G * P], F32R))
        RING = 4
        raw = [sb(f"raw{n}", [P, WIDE_CHUNK]) for n in range(RING)]

        p_ps, main_ok, h_ok = sem("proj_in_psum"), sem("main_added"), sem("h_kept")
        d_ok, e_ok, hw_ok = sem("logits_ready"), sem("exps_ready"), sem("hw_ready")
        h_ps, h_hi, h_lo = sem("hT_in_psum"), sem("hT_hi_ready"), sem("hT_ready")
        o_ps, x_ok = sem("out_in_psum"), sem("x_updated")
        chain_s = sem("vector_chain")
        wide_in = [sem(f"wide_loaded{n}") for n in range(RING)]
        wide_hi, wide_lo = sem("wide_hi"), sem("wide_ready")
        block = ctx.enter_context(nc.Block())

        T_TURN = NG - 1
        PIECES = (0, 3, 6, 9, 11)
        pieces = [(n, at) for n in range(4) for at in range(0, WIDE_COLS, WIDE_CHUNK)]

        @block.sync
        def _(sp):
            for n, (m, at) in enumerate(pieces):
                if n >= RING:
                    sp.wait_ge(wide_lo, n - RING + 1)
                sp.dma_start(raw[n % RING][:], io["wide_w"][m, :, at:at + WIDE_CHUNK]).then_inc(wide_in[n % RING], 16)

        @block.gpsimd
        def _(pool):
            def low_parts(first, last):
                for n in range(first, last):
                    m, at = pieces[n]
                    hi, lo = [t[:, at:at + WIDE_CHUNK] for t in pr.wide[m]]
                    pool.wait_ge(wide_hi, n + 1)
                    nc.gpsimd.tensor_tensor(lo, raw[n % RING][:], hi.bitcast(F32), ALU.subtract).then_inc(wide_lo, 1)

            for it in range(1, NG):
                norm.pool_rstd(pool, it)
                low_parts(PIECES[it - 1], PIECES[it])
            low_parts(PIECES[NG - 1], len(pieces) - 2)
            norm.pool_rstd(pool, NG)
            low_parts(len(pieces) - 2, len(pieces))

        @block.tensor
        def _(pe):
            def products(it):
                pe.wait_ge(norm.s_lo, DC * norm.split(it))
                for j in range(G):
                    pe.wait_ge(main_ok, it * G + j + 1)
                    for c in range(DC):
                        last = product(nc, b_o[j][:, 0:W], pair(norm.xT, slice(None), c, slice(j * P, j * P + P)),
                                       pair(w, slice(None), c), c == 0, c == DC - 1)
                    last.then_inc(p_ps, 1)
            products(0)
            with pe.Fori(1, NG) as it:
                norm.tensor_transpose(pe, it)
                products(it)

            def turn(it):
                pe.wait_ge(hw_ok, it + 1)
                if it >= 2:
                    pe.wait_ge(h_lo, it - 1)
                for j in range(G):
                    last = nc.tensor.transpose(b_h[it % 2][:, j * P:(j + 1) * P], hw[:, j, :], pr.ident[:])
                last.then_inc(h_ps, 1)

            turn(0)
            for it in range(NG):
                if it + 1 < NG:
                    turn(it + 1)
                if it == T_TURN:
                    norm.tensor_transpose(pe, NG)
                pe.wait_ge(h_lo, it + 1)
                for j in range(G):
                    pe.wait_ge(x_ok, it * G + j + 1)
                    product(nc, b_o[j][:, 0:D], pair(hT, slice(None), it % 2, slice(j * P, j * P + P)),
                            (up[0][:], up[1][:]), True, True).then_inc(o_ps, 1)

        @block.scalar
        def _(act):
            def high_parts(first, last):
                for n in range(first, last):
                    m, at = pieces[n]
                    act.wait_ge(wide_in[n % RING], 16 * (n // RING + 1))
                    nc.scalar.copy(pr.wide[m][0][:, at:at + WIDE_CHUNK], raw[n % RING][:]).then_inc(wide_hi, 1)

            for it in range(NG):
                if it > 0:
                    norm.scalar_hi(act, it)
                high_parts(PIECES[it], PIECES[it + 1])
                for j in range(G):
                    act.wait_ge(p_ps, it * G + j + 1)
                    nc.scalar.copy(h[:, it * G + j, :], b_o[j][:, D:D + E * R]).then_inc(h_ok, 1)
            act.wait_ge(d_ok, 1)
            nc.scalar.activation(prob[:], logit[:], ACT.Exp).then_inc(e_ok, 1)
            high_parts(PIECES[NG], len(pieces) - 2)
            for it in range(NG):
                if it == T_TURN:
                    norm.scalar_hi(act, NG)
                act.wait_ge(h_ps, it + 1)
                if it >= 2:
                    act.wait_ge(o_ps, (it - 1) * G)
                nc.scalar.copy(hT[0][:, it % 2], b_h[it % 2][:, :]).then_inc(h_hi, 1)
                if it < 2:
                    high_parts(len(pieces) - 2 + it, len(pieces) - 1 + it)

        @block.vector
        def _(dve):
            def keep(it):
                for j in range(G):
                    dve.wait_ge(h_ok, it * G + j + 1)
                    nc.vector.tensor_tensor(x[:, it * G + j, :], b_o[j][:, 0:D], x[:, it * G + j, :], ALU.add)
                    nc.vector.tensor_copy(logit[:, bass.ds(it * G + j, 1), :],
                                          b_o[j][:, D + E * R:W].unsqueeze(1)).then_inc(main_ok, 1)

            dve.sem_inc(main_ok, G)
            dve.sem_inc(x_ok, G)
            with dve.Fori(0, NG - 1) as it:
                norm.vector_norm(dve, it + 1)
                keep(it)
                norm.vector_lo(dve, it + 1)
            keep(NG - 1)
            dve.wait_ge(main_ok, G + NB)
            chain = Chain(dve, chain_s, 0, 21)
            per_e = lambda t: t.unsqueeze(2).to_broadcast([P, NB, E])
            chain.done(nc.vector.tensor_reduce(stat[:, 0, :], logit[:], AX, ALU.max))
            nc.vector.tensor_tensor(logit[:], logit[:], per_e(stat[:, 0, :]), ALU.subtract).then_inc(d_ok, 1)
            dve.wait_ge(e_ok, 1)
            chain.done(nc.vector.tensor_reduce(stat[:, 1, :], prob[:], AX, ALU.add))
            chain.done(nc.vector.reciprocal(stat[:, 2, :], stat[:, 1, :]))
            nc.vector.tensor_tensor(left[:], prob[:], per_e(stat[:, 2, :]), ALU.mult)
            chain.done(nc.vector.tensor_tensor(prob[:], prob[:], per_e(stat[:, 2, :]), ALU.mult))
            for best in range(TOP):
                chain.done(nc.vector.tensor_reduce(stat[:, 0, :], left[:], AX, ALU.max))
                chain.done(nc.vector.tensor_tensor(is_best[:], left[:], per_e(stat[:, 0, :]), ALU.is_equal))
                chain.done(nc.vector.tensor_tensor(is_best[:], is_best[:], order, ALU.mult))
                chain.done(nc.vector.tensor_reduce(stat[:, 0, :], is_best[:], AX, ALU.max))
                chain.done(nc.vector.tensor_tensor(is_best[:], is_best[:], per_e(stat[:, 0, :]), ALU.is_equal))
                chain.done(nc.vector.scalar_tensor_tensor(left[:], is_best[:], -2.0, left[:], ALU.mult, ALU.add))
            chain.done(nc.vector.scalar_tensor_tensor(rank[:], left[:], 0.0, prob[:], ALU.is_lt, ALU.mult))
            chain.done(nc.vector.tensor_reduce(stat[:, 3, :], rank[:], AX, ALU.add))
            chain.done(nc.vector.reciprocal(stat[:, 3, :], stat[:, 3, :]))
            chain.done(nc.vector.tensor_scalar(stat[:, 3, :], stat[:, 3, :], ALPHA, None, ALU.mult))
            chain.done(nc.vector.tensor_tensor(rank[:], rank[:], per_e(stat[:, 3, :]), ALU.mult))
            chain.close()

            def weigh(it):
                nc.vector.tensor_tensor(
                    hw[:].rearrange("p j (e r) -> p (j e) r", e=E),
                    h[:, bass.ds(it * G, G), :].rearrange("p j (e r) -> p (j e) r", e=E),
                    rank[:, bass.ds(it * G, G), :].rearrange("p j e -> p (j e)").unsqueeze(2)
                    .to_broadcast([P, G * E, R]), ALU.mult).then_inc(hw_ok, 1)

            def low(it):
                dve.wait_ge(h_hi, it + 1)
                nc.vector.tensor_tensor(hT[1][:, it % 2], b_h[it % 2][:, :], hT[0][:, it % 2].bitcast(F32),
                                        ALU.subtract).then_inc(h_lo, 1)

            weigh(0)
            dve.wait_ge(h_ps, 1)
            weigh(1)
            low(0)
            for it in range(NG):
                if it + 2 < NG:
                    dve.wait_ge(h_ps, it + 2)
                    weigh(it + 2)
                if it + 1 < NG:
                    low(it + 1)
                if it == T_TURN:
                    norm.vector_lo(dve, NG)
                for j in range(G):
                    dve.wait_ge(o_ps, it * G + j + 1)
                    nc.vector.tensor_tensor(x[:, it * G + j, :], b_o[j][:, 0:D], x[:, it * G + j, :],
                                            ALU.add).then_inc(x_ok, 1)
                if it == 0:
                    dve.wait_ge(x_ok, G + G)
                    norm.vector_stats(dve, NG)
                if it == 1:
                    norm.vector_apply(dve, NG)


WIDE_COLS = 4096
WIDE_CHUNK = 1024


def stage_wide_attention(pr):
    nc, io, x, banks = pr.nc, pr.io, pr.x, pr.banks
    H, HD = 16, 128
    VH = 4
    SCALE = HD ** -0.5
    b_p, b_s, b_t, b_z, b_o = banks[0:2], banks[2:4], banks[4], banks[5], banks[6:8]
    with ExitStack() as ctx:
        sb = lambda n, shape, dt=F32: ctx.enter_context(nc.sbuf_tensor(f"wa_{n}", shape, dt))
        sem = lambda n: pr.sem(f"wa_{n}")
        norm = pr.norm
        norm.enter_stage(3, 2, b_p)
        xT = norm.xT
        wq, wk, wv = [tuple(t[:].rearrange("p (c n) -> p c n", c=DC) for t in pr.wide[n]) for n in range(3)]
        wo = tuple(t[:].rearrange("p (h n) -> p h n", h=H) for t in pr.wide[3])
        causal = sb("causal", [P, P])
        q = sb("q", [P, 2, GT])
        k = sb("k", [P, 2, GT])
        v = sb("v", [P, 2, G, VH * HD])
        negmax = sb("negmax", [P, 2, G])
        sums = sb("sums", [P, 2, G])
        rsum = sb("rsum", [P, 2, G])
        prob = sb("prob", [P, 2, G, P])
        probT = sb("probT", [P, 2, G, P])
        z = [t[:].rearrange("p (n t) -> p n t", n=2) for t in pr.le_w_or_z]

        loaded = sem("masks_loaded")
        q_ps, q_ok, k_ps, k_ok = sem("q_in_psum"), sem("q_ready"), sem("k_in_psum"), sem("k_ready")
        v_ps, v_ok = sem("v_in_psum"), sem("v_ready")
        s_ps, masked_ok = sem("scores_in_psum"), sem("scores_masked")
        max_ok, exp_ok = sem("negmax_ready"), sem("exps_ready")
        r_ok, prob_ok = sem("rsum_ready"), sem("probs_ready")
        t_ps, t_ok = sem("probsT_in_psum"), sem("probsT_ready")
        z_ps, z_hi, z_lo = sem("z_in_psum"), sem("z_hi_ready"), sem("z_ready")
        o_ps, x_ok = sem("out_in_psum"), sem("x_updated")
        chain_s = sem("vector_chain")
        block = ctx.enter_context(nc.Block())

        V_UNITS = {t: [t + G] for t in range(H - G)}
        V_UNITS |= {H - 2: [H, H + 1], H - 1: [H + 2, H + 3]}
        T_STATS, T_APPLY, T_TURN = 4, 5, H - 3

        def in_range(h, last):
            return h < H or not last

        def v_units(t, last):
            units = V_UNITS.get(t, []) if t < H - 2 or not last else []
            return units[:1], units[1:]

        @block.sync
        def _(sp):
            sp.dma_start(causal[:], io["causal"]).then_inc(loaded, 16)
            sp.dma_start(pr.h_or_fold[:], io["li_fold"]).then_inc(pr.fold_loaded, 16)

        @block.gpsimd
        def _(pool):
            def normalise(n, s):
                pool.wait_ge(r_ok, BASE + n + 1)
                nc.gpsimd.tensor_tensor(prob[:, s], prob[:, s], rsum[:, s, :].unsqueeze(2).to_broadcast([P, G, P]),
                                        ALU.mult).then_inc(prob_ok, 1)

            def group(it, last):
                for t in range(H):
                    if in_range(t + 1, last):
                        normalise(it * H + t + 1, (t + 1) % 2)
                    if t == T_STATS:
                        norm.pool_rstd(pool, it + 1)

            pool.sem_inc(prob_ok, BASE)
            normalise(0, 0)
            with pool.Fori(0, NG - 1) as it:
                group(it, False)
            group(NG - 1, True)

        @block.tensor
        def _(pe):
            def scores(n, s):
                pe.wait_ge(q_ok, BASE + n + 1)
                pe.wait_ge(k_ok, BASE + n + 1)
                pe.wait_ge(masked_ok, BASE + n - 1)
                for j in range(G):
                    t = slice(j * P, (j + 1) * P)
                    last = nc.tensor.matmul(b_s[s][:, t], q[:, s, t], k[:, s, t], start=True, stop=True)
                last.then_inc(s_ps, 1)

            def project_q(n, h, v_before):
                cols = slice(h * HD, (h + 1) * HD)
                pe.wait_ge(q_ok, BASE + n)
                pe.wait_ge(v_ok, BASE + v_before)
                for c in range(DC):
                    last = product(nc, b_p[0][:, :], pair(wq, slice(None), c, cols), pair(xT, slice(None), c),
                                   c == 0, c == DC - 1)
                last.then_inc(q_ps, 1)

            def project_k(n, h):
                cols = slice(h * HD, (h + 1) * HD)
                pe.wait_ge(k_ok, BASE + n)
                for c in range(DC):
                    last = product(nc, b_p[1][:, :], pair(wk, slice(None), c, cols), pair(xT, slice(None), c),
                                   c == 0, c == DC - 1)
                last.then_inc(k_ps, 1)

            def qk(n, h, v_before):
                project_q(n, h, v_before)
                project_k(n, h)

            def values(n, unit, q_before):
                g, j = divmod(unit, G)
                pe.wait_ge(q_ok, BASE + q_before)
                pe.wait_ge(v_ok, BASE + n)
                for c in range(DC):
                    last = product(nc, b_p[0][:, :], pair(xT, slice(None), c, slice(j * P, (j + 1) * P)),
                                   pair(wv, slice(None), c, slice(g * VH * HD, (g + 1) * VH * HD)),
                                   c == 0, c == DC - 1)
                last.then_inc(v_ps, 1)

            def turn(n, s):
                pe.wait_ge(prob_ok, BASE + n + 1)
                pe.wait_ge(t_ok, BASE + n)
                for j in range(G):
                    last = nc.tensor.transpose(b_t[:, j * P:(j + 1) * P], prob[:, s, j, :], pr.ident[:])
                last.then_inc(t_ps, 1)

            def weigh(it, h):
                n = it * H + h
                g, m = divmod(h, VH)
                pe.wait_ge(t_ok, BASE + n + 1)
                pe.wait_ge(v_ok, BASE + it * H + G * (g + 1))
                pe.wait_ge(z_lo, BASE + n)
                for j in range(G):
                    last = nc.tensor.matmul(b_z[:, j * P:(j + 1) * P], v[:, g % 2, j, m * HD:(m + 1) * HD],
                                            probT[:, h % 2, j, :], start=True, stop=True)
                last.then_inc(z_ps, 1)

            def project(it, h):
                pe.wait_ge(z_lo, BASE + it * H + h + 1)
                if h == 0:
                    pe.wait_ge(x_ok, ONE + it * G)
                for j in range(G):
                    last = product(nc, b_o[j // 2][:, (j % 2) * D:(j % 2) * D + D],
                                   pair(z, slice(None), h % 2, slice(j * P, (j + 1) * P)),
                                   pair(wo, slice(None), h), h == 0 and j % 2 == 0, h == H - 1)
                last.then_inc(o_ps, 1)

            def group(it, last):
                n_v = G
                for t in range(H):
                    n = it * H + t
                    early, late = v_units(t, last)
                    turning = t == H - 2 and not last
                    if in_range(t + 1, last):
                        scores(n + 1, (t + 1) % 2)
                    if in_range(t + 2, last) and t < H - 2:
                        qk(n + 2, (t + 2) % H, it * H + n_v)
                    if t >= 1 and early and t < H - 2:
                        project(it, t - 1)
                    turn(n, t % 2)
                    if t >= 1 and not (early and t < H - 2):
                        project(it, t - 1)
                    if turning:
                        pe.wait_ge(norm.s_lo, DC * norm.split(it + 1))
                        qk(n + 2, 0, it * H + n_v)
                    for unit in early:
                        values(it * H + n_v, unit % H, it * H + min(t + 3, H + 1))
                        n_v += 1
                    if t == T_TURN:
                        pe.wait_ge(q_ok, BASE + it * H + H)
                        pe.wait_ge(v_ok, BASE + it * H + H)
                        pe.wait_ge(k_ok, BASE + it * H + H)
                        norm.tensor_transpose(pe, it + 1)
                    weigh(it, t)
                    for unit in late:
                        values(it * H + n_v, unit % H, it * H + H + 1)
                        n_v += 1
                    if t == H - 1:
                        if not last:
                            project_k(n + 2, 1)
                            project_q(n + 2, 1, it * H + n_v)
                        project(it, t)

            for event in (s_ps, t_ps, z_ps, o_ps):
                pe.sem_inc(event, BASE)
            pe.wait_ge(norm.s_lo, DC * norm.split(0))
            qk(0, 0, 0)
            values(0, 0, 1)
            project_k(1, 1)
            values(1, 1, 1)
            scores(0, 0)
            project_q(1, 1, 2)
            values(2, 2, 2)
            values(3, 3, 2)
            with pe.Fori(0, NG - 1) as it:
                group(it, False)
            group(NG - 1, True)

        @block.scalar
        def _(act):
            def exps(n, s):
                act.wait_ge(max_ok, BASE + n + 1)
                for j in range(G):
                    last = nc.scalar.activation(prob[:, s, j, :], prob[:, s, j, :], ACT.Exp,
                                                bias=negmax[:, s, j:j + 1], scale=SCALE,
                                                accum_out=sums[:, s, j:j + 1])
                last.then_inc(exp_ok, 1)

            def keep_q(n, s):
                act.wait_ge(q_ps, n + 1)
                act.wait_ge(s_ps, BASE + n - 1)
                nc.scalar.copy(q[:, s, :], b_p[0][:, :]).then_inc(q_ok, 1)

            def keep_v(it, unit):
                g, j = divmod(unit, G)
                act.wait_ge(v_ps, it * H + unit + 1)
                if g >= 2:
                    act.wait_ge(z_ps, BASE + it * H + VH * (g - 1))
                nc.scalar.copy(v[:, g % 2, j, :], b_p[0][:, :]).then_inc(v_ok, 1)

            def group(it, last):
                for t in range(H):
                    n = it * H + t
                    early, late = v_units(t, last)
                    if in_range(t + 2, last) and t < H - 2:
                        keep_q(n + 2, t % 2)
                    if in_range(t + 1, last):
                        exps(n + 1, (t + 1) % 2)
                    if t == H - 2 and not last:
                        keep_q(n + 2, t % 2)
                    for unit in early:
                        keep_v(it, unit)
                    if t == T_TURN:
                        norm.scalar_hi(act, it + 1)
                    act.wait_ge(z_ps, BASE + n + 1)
                    act.wait_ge(o_ps, BASE + n - 1)
                    nc.scalar.copy(z[0][:, t % 2, :], b_z[:, :]).then_inc(z_hi, 1)
                    for unit in late:
                        keep_v(it, unit)
                    if t == H - 1 and not last:
                        keep_q(n + 2, t % 2)

            for event in (exp_ok, q_ok, v_ok):
                act.sem_inc(event, BASE)
            keep_q(0, 0)
            keep_v(0, 0)
            keep_v(0, 1)
            keep_q(1, 1)
            keep_v(0, 2)
            keep_v(0, 3)
            exps(0, 0)
            with act.Fori(0, NG - 1) as it:
                group(it, False)
            group(NG - 1, True)

        @block.vector
        def _(dve):
            def row_max(n, s, chain):
                dve.wait_ge(s_ps, BASE + n + 1)
                dve.wait_ge(t_ps, BASE + n - 1)
                nc.vector.tensor_tensor(prob[:, s], b_s[s][:, :].rearrange("p (j k) -> p j k", j=G),
                                        causal[:].unsqueeze(1).to_broadcast([P, G, P]), ALU.add)\
                    .then_inc(masked_ok, 1)
                dve.wait_ge(masked_ok, BASE + n + 1)
                chain.done(nc.vector.tensor_reduce(negmax[:, s, :], prob[:, s], AX, ALU.max))
                nc.vector.tensor_scalar(negmax[:, s, :], negmax[:, s, :], -SCALE, None, ALU.mult)\
                    .then_inc(max_ok, 1)

            def keep_k(n, s):
                dve.wait_ge(k_ps, n + 1)
                dve.wait_ge(s_ps, BASE + n - 1)
                nc.vector.tensor_copy(k[:, s, :], b_p[1][:, :]).then_inc(k_ok, 1)

            def inverse_sums(n, s):
                dve.wait_ge(exp_ok, BASE + n + 1)
                dve.wait_ge(prob_ok, BASE + n - 1)
                nc.vector.reciprocal(rsum[:, s, :], sums[:, s, :]).then_inc(r_ok, 1)

            def group(it, last):
                chain = Chain(dve, chain_s, it, H)
                chain.n = 1
                for t in range(H):
                    n = it * H + t
                    if in_range(t + 1, last):
                        row_max(n + 1, (t + 1) % 2, chain)
                    if in_range(t + 2, last) and t < H - 1:
                        keep_k(n + 2, t % 2)
                    dve.wait_ge(t_ps, BASE + n + 1)
                    dve.wait_ge(z_ps, BASE + n - 1)
                    nc.vector.tensor_copy(probT[:, t % 2], b_t[:, :].rearrange("p (j k) -> p j k", j=G))\
                        .then_inc(t_ok, 1)
                    if in_range(t + 1, last):
                        inverse_sums(n + 1, (t + 1) % 2)
                    if t == T_STATS:
                        if last:
                            dve.wait_ge(x_ok, ONE + G)
                        norm.vector_stats(dve, it + 1)
                    if t == T_APPLY:
                        norm.vector_apply(dve, it + 1)
                    if t == T_TURN:
                        norm.vector_lo(dve, it + 1)
                    dve.wait_ge(z_hi, n + 1)
                    nc.vector.tensor_tensor(z[1][:, t % 2, :], b_z[:, :], z[0][:, t % 2, :].bitcast(F32),
                                            ALU.subtract).then_inc(z_lo, 1)
                    if t == H - 1 and not last:
                        keep_k(n + 2, t % 2)
                dve.wait_ge(o_ps, BASE + it * H + H)
                for j in range(G):
                    nc.vector.tensor_tensor(x[:, it * G + j, :], b_o[j // 2][:, (j % 2) * D:(j % 2) * D + D],
                                            x[:, it * G + j, :], ALU.add).then_inc(x_ok, 1)
                if not last:
                    chain.n -= 1
                chain.close()

            for event in (masked_ok, max_ok, k_ok, r_ok, t_ok, z_lo):
                dve.sem_inc(event, BASE)
            dve.sem_inc(x_ok, ONE)
            keep_k(0, 0)
            keep_k(1, 1)
            first = Chain(dve, chain_s, 0, 1)
            dve.wait_ge(loaded, 16)
            row_max(0, 0, first)
            inverse_sums(0, 0)
            with dve.Fori(0, NG - 1) as it:
                group(it, False)
            group(NG - 1, True)


def first_layer_and_wide_attention(pr):
    nc = pr.nc
    W = D + P + 8
    with ExitStack() as ctx:
        sb = lambda c, n, shape, dt=F32: c.enter_context(nc.sbuf_tensor(n, shape, dt))
        pr.le_w_or_z = (sb(ctx, "le_w_or_z_hi", [P, 2 * GT], F32R), sb(ctx, "le_w_or_z_lo", [P, 2 * GT], F32R))
        pr.le_w = [t[:, 0:DC * W].rearrange("p (c n) -> p c n", c=DC) for t in pr.le_w_or_z]
        pr.le_u = (sb(ctx, "le_u_hi", [P, D], F32R), sb(ctx, "le_u_lo", [P, D], F32R))
        pr.le_order = sb(ctx, "le_order", [P, 8])
        with ExitStack() as conv:
            pr.toep = sb(conv, "lc_toep", [P, CONV_H, 2 * P])
            pr.skip = sb(conv, "lc_skip", [P, CONV_H])
            pr.anti = sb(conv, "lc_anti", [P, P])
            pr.kt = sb(conv, "lc_kt", [P, 2, NB * CONV_H, CONV_C])
            pr.shared = sb(conv, "v_or_conv", [P, 2 * (G * 16 * P + P)])
            pr.kk = pr.shared[:, 0:2 * GH * NPAIR].rearrange("p (a bh n) -> p a bh n", a=2, n=NPAIR)
            stage_lora_attention(pr)
            pr.release_semaphores()
            pr.le_w32 = sb(conv, "le_w32", [P, DC, W])
            pr.le_u32 = sb(conv, "le_u32", [P, D])
            stage_long_conv(pr)
            pr.release_semaphores()
        pr.wide = [tuple(sb(ctx, f"wide{n}_{part}", [P, WIDE_COLS], F32R) for part in ("hi", "lo"))
                   for n in range(4)]
        stage_lora_experts(pr)
        pr.release_semaphores()
        stage_wide_attention(pr)


def keep_mix_input(pr, act, it, g, done):
    for c in range(DC):
        act.wait_ge(pr.norm.s_tr, DC * (pr.norm.done(it) - 1) + c + 1)
        for j in range(G):
            last = pr.nc.scalar.activation(pr.em_xT[:, c, g * G + j, :], pr.norm.banks[c][:, j * P:(j + 1) * P],
                                           ACT.Identity, accum_out=pr.em_rep[:, c, g * G + j:g * G + j + 1])
        last.then_inc(done, 1)


def stage_linear_attention(pr):
    nc, io, x, banks = pr.nc, pr.io, pr.x, pr.banks
    H, HD, F = 16, 16, 64
    T = H // 2
    HF = H * F
    VW = HD + 1
    HH = H // DC
    HC = HH * F
    b_p = banks[0:2]
    b_k, b_kv, b_qkv, b_v = banks[2:4], banks[4], banks[5], banks[6]
    b_o, b_ot = banks[7][:, 0:D], banks[7][:, D:2 * D]
    with ExitStack() as ctx:
        sb = lambda n, shape, dt=F32: ctx.enter_context(nc.sbuf_tensor(f"li_{n}", shape, dt))
        both = lambda n, shape: (sb(f"{n}_hi", shape, F32R), sb(f"{n}_lo", shape, F32R))
        sem = lambda n: pr.sem(f"li_{n}")
        norm = pr.norm
        norm.enter_stage(4, 3, b_p)
        wqk = pr.h_or_fold[:, 0:2 * DC * D].rearrange("p (w c d) -> p w c d", w=2, c=DC)
        wf = pr.h_or_fold[:, 2 * DC * D:].rearrange("p (w n) -> p w n", w=2)
        bqk = sb("bqk", [P, 2, DC])
        vo32 = sb("vo32", [P, 2, DC, D])
        vo = both("vo", [P, 2, DC, D])
        v_bias = sb("v_bias", [P, D])
        k_bias = sb("k_bias", [P, HF])
        out_bias = sb("out_bias", [P, D])
        mqk = both("mqk", [P, 2, DC, HF])
        q_bias = sb("q_bias", [P, T])
        mask = sb("mask", [P, NB])
        kt32 = sb("kt32", [P, DC, NB, P])
        kt = both("kt", [P, 2, DC, P])
        qp = sb("qp", [P, T, GT])
        kp = sb("kp", [P, 2, HF])
        va = sb("va", [P, 2, H, VW])
        kv = sb("kv", [P, 2, T, 2 * VW])
        rden = sb("rden", [P, 2, H])
        o = sb("o", [P, 2, D])
        oT = both("oT", [P, 2, DC, P])

        loaded, late_loaded, kt_loaded = sem("loaded"), sem("late_loaded"), sem("kt_loaded")
        fold_ps, fold_hi, fold_lo = sem("folded_in_psum"), sem("folded_hi"), sem("folded_ready")
        w_hi, w_lo, clear = sem("vo_hi"), sem("vo_ready"), sem("cleared")
        kt_hi, kt_lo = sem("kt_hi"), sem("kt_ready")
        q_ps, q_ok = sem("q_in_psum"), sem("q_ready")
        k_ps, k_sum, k_ok = sem("k_in_psum"), sem("k_biased"), sem("k_ready")
        v_ps, v_ok = sem("v_in_psum"), sem("v_ready")
        kv_ps, kv_ok = sem("kv_in_psum"), sem("kv_ready")
        n_ps, n_ok = sem("qkv_in_psum"), sem("o_ready")
        ot_ps, ot_hi, ot_lo = sem("oT_in_psum"), sem("oT_hi_ready"), sem("oT_ready")
        o_ps, xb_ok, x_ok = sem("out_in_psum"), sem("x_biased"), sem("x_updated")
        chain_s = sem("vector_chain")
        em_ok = sem("mix_input_kept")
        block = ctx.enter_context(nc.Block())
        NLOAD, NLATE = 1, 5
        FOLDS = [("k", c, half) for c in range(DC) for half in range(2)] + [("k_row", 0, half) for half in range(2)]
        NK = len(FOLDS)
        FOLDS += [("q", c, half) for c in range(DC) for half in range(2)]

        T_STATS, T_APPLY, T_TURN = 0, 1, 2
        def query_steps(it, j):
            return (it + j // 2, 1 - j // 2, range(T // 2 * (j % 2), T // 2 * (j % 2) + T // 2))

        @block.sync
        def _(sp):
            sp.dma_start(bqk[:], io["li_bqk"]).then_inc(loaded, 16)
            sp.dma_start(kt32[:, :, 0:G], io["ctx_rev"][:, :, 0:G]).then_inc(late_loaded, 16)
            sp.wait_ge(late_loaded, 16 * NLATE)
            sp.dma_start(kt32[:, :, G:NB], io["ctx_rev"][:, :, G:NB]).then_inc(kt_loaded, 16)
            sp.dma_start(pr.em_w[:], io["em_w"]).then_inc(pr.em_loaded, 16)

        @block.gpsimd
        def _(pool):
            nc.gpsimd.memset(va[:], 1.0).then_inc(clear, 1)
            nc.gpsimd.memset(kv[:], 0.0).then_inc(clear, 1)
            pool.wait_ge(late_loaded, 16 * NLATE)

            def add_bias(it):
                pool.wait_ge(norm.s_xn, norm.done(it))
                nc.gpsimd.tensor_tensor(x[:, bass.ds(it * G, G), :], x[:, bass.ds(it * G, G), :],
                                        out_bias[:].unsqueeze(1).to_broadcast([P, G, D]), ALU.add).then_inc(xb_ok, 1)

            add_bias(0)
            with pool.Fori(1, NG) as it:
                norm.pool_rstd(pool, it)
                add_bias(it)
            for n in range(3):
                norm.pool_rstd(pool, NG + n)

        @block.tensor
        def _(pe):
            def keys(n, s):
                pe.wait_ge(kt_lo, n + 1)
                for half in range(2):
                    cols = slice(half * HC, (half + 1) * HC)
                    pe.wait_ge(k_sum, BASE + 2 * n + half - 1)
                    for c in range(DC):
                        last = product(nc, b_k[half][:, :], pair(kt, slice(None), s, c),
                                       pair(mqk, slice(None), 1, c, cols), c == 0, c == DC - 1)
                    last.then_inc(k_ps, 1)
                pe.wait_ge(v_ok, ONE + n)
                for c in range(DC):
                    last = product(nc, b_v[:, 0:D], pair(kt, slice(None), s, c), pair(vo, slice(None), 0, c),
                                   c == 0, c == DC - 1)
                last.then_inc(v_ps, 1)

            def key_values(n, s):
                pe.wait_ge(k_ok, 2 * n + 2)
                pe.wait_ge(v_ok, ONE + n + 1)
                pe.wait_ge(kv_ok, ONE + n)
                for t in range(T):
                    last = nc.tensor.matmul(b_kv[:, t * 2 * VW:(t + 1) * 2 * VW], kp[:, s, t * P:(t + 1) * P],
                                            va[:, s, 2 * t:2 * t + 2, :], start=True, stop=True)
                last.then_inc(kv_ps, 1)

            def queries(it, p, heads):
                pe.wait_ge(norm.s_lo, DC * norm.split(it))
                for t in heads:
                    pe.wait_ge(q_ok, BASE + it * 2 * T + p * T + t - 1)
                    tokens = slice(2 * P * p, 2 * P * (p + 1))
                    for c in range(DC):
                        last = product(nc, b_p[t % 2][:, 0:2 * P],
                                       pair(mqk, slice(None), 0, c, slice(t * P, (t + 1) * P)),
                                       pair(norm.xT, slice(None), c, tokens), c == 0, c == DC - 1)
                    last.then_inc(q_ps, 1)

            def numerators(it, j):
                n = it * G + j
                pe.wait_ge(kv_ok, ONE + n + 1)
                pe.wait_ge(q_ok, BASE + it * 2 * T + (j // 2 + 1) * T)
                pe.wait_ge(n_ok, ONE + n)
                for t in range(T):
                    last = nc.tensor.matmul(b_qkv[:, t * 2 * VW:(t + 1) * 2 * VW], qp[:, t, j * P:(j + 1) * P],
                                            kv[:, j % 2, t, :], start=True, stop=True)
                last.then_inc(n_ps, 1)

            def turn_o(n, s):
                pe.wait_ge(n_ok, ONE + n + 1)
                pe.wait_ge(ot_lo, ONE + n)
                for c in range(DC):
                    last = nc.tensor.transpose(b_ot[:, c * P:(c + 1) * P], o[:, s, c * P:(c + 1) * P], pr.ident[:])
                last.then_inc(ot_ps, 1)

            def project(n, s):
                pe.wait_ge(ot_lo, ONE + n + 1)
                pe.wait_ge(x_ok, ONE + n)
                for c in range(DC):
                    last = product(nc, b_o, pair(oT, slice(None), s, c), pair(vo, slice(None), 1, c),
                                   c == 0, c == DC - 1)
                last.then_inc(o_ps, 1)

            def group(it, last):
                for j in range(G):
                    n = it * G + j
                    more = not last or j + 1 < G
                    if j == T_TURN:
                        pe.wait_ge(q_ok, BASE + (it + 1) * 2 * T)
                        norm.tensor_transpose(pe, it + 1)
                    if j == T_TURN + 1 and last:
                        pe.wait_ge(em_ok, DC)
                        norm.tensor_transpose(pe, it + 2)
                    if more:
                        keys(n + 1, (j + 1) % 2)
                    numerators(it, j)
                    if not last or j < 2:
                        queries(*query_steps(it, j))
                    turn_o(n, j % 2)
                    if more:
                        key_values(n + 1, (j + 1) % 2)
                    project(n, j % 2)

            for event in (kv_ps, n_ps, ot_ps, o_ps):
                pe.sem_inc(event, BASE)
            pe.wait_ge(pr.fold_loaded, 16)
            for n, (what, c, half) in enumerate(FOLDS):
                if what == "k_row" and half == 0:
                    pe.wait_ge(loaded, 16 * NLOAD)
                if n >= 8:
                    pe.wait_ge(fold_lo, n - 7)
                w = 0 if what == "q" else 1
                if what == "k_row":
                    nc.tensor.matmul(banks[n][:, :], bqk[:, 1, half:half + 1].to_broadcast([P, P]), wf[:, 1, :],
                                     start=True, stop=True).then_inc(fold_ps, 1)
                else:
                    nc.tensor.matmul(banks[n % 8][:, :], wqk[:, w, half, c * P:(c + 1) * P], wf[:, w, :],
                                     start=True, stop=True).then_inc(fold_ps, 1)
            pe.wait_ge(fold_lo, NK - 1)
            for t in range(T):
                half, m = divmod(t, T // 2)
                last = nc.tensor.matmul(b_kv[:, t:t + 1], wf[:, 0, m * P:(m + 1) * P], bqk[:, 0, half:half + 1],
                                        start=True, stop=True)
            last.then_inc(fold_ps, 1)
            pe.wait_ge(fold_lo, NK + 1)
            pe.wait_ge(w_lo, 1)
            keys(0, 0)
            pe.wait_ge(fold_lo, len(FOLDS) + 1)
            queries(0, 0, range(T))
            key_values(0, 0)
            with pe.Fori(0, NG - 1) as it:
                group(it, False)
            group(NG - 1, True)

        @block.scalar
        def _(act):
            for t, src in ((vo32[:], io["li_vo"]), (v_bias[:], io["li_v_bias"]),
                           (mask[:], io["li_mask"]), (out_bias[:], io["li_o_bias"])):
                act.dma_start(t, src).then_inc(late_loaded, 16)

            def keep_kt(n, s):
                nc.scalar.copy(kt[0][:, s], kt32[:, :, bass.ds(n, 1), :].rearrange("p c b t -> p c (b t)"))\
                    .then_inc(kt_hi, 1)

            def keep_kv(n, s):
                act.wait_ge(kv_ps, BASE + n + 1)
                act.wait_ge(n_ps, BASE + n - 1)
                src = b_kv[:, 0:T * 2 * VW].rearrange("p (t n) -> p t n", t=T)
                nc.scalar.copy(kv[0:F, s, :, 0:VW], src[0:F, :, 0:VW])
                nc.scalar.copy(kv[F:2 * F, s, :, VW:2 * VW], src[F:2 * F, :, VW:2 * VW]).then_inc(kv_ok, 1)

            def keep_q(it, p, heads):
                act.wait_ge(n_ps, BASE + it * G + 2 * p - 2)
                for t in heads:
                    act.wait_ge(q_ps, it * 2 * T + p * T + t + 1)
                    nc.scalar.activation(qp[:, t, 2 * P * p:2 * P * (p + 1)], b_p[t % 2][:, 0:2 * P], ACT.Relu,
                                         bias=q_bias[:, t:t + 1]).then_inc(q_ok, 1)

            def group(it, last):
                for j in range(G):
                    n = it * G + j
                    if j == T_TURN and not last:
                        norm.scalar_hi(act, it + 1)
                    if j >= T_TURN and last:
                        keep_mix_input(pr, act, NG + j - T_TURN, j - T_TURN, em_ok)
                    if not last or j + 2 < G:
                        keep_kt(n + 2, j % 2)
                    if not last or j < 2:
                        keep_q(*query_steps(it, j))
                    act.wait_ge(ot_ps, BASE + n + 1)
                    act.wait_ge(o_ps, BASE + n - 1)
                    nc.scalar.copy(oT[0][:, j % 2, :, :], b_ot.rearrange("p (c t) -> p c t", c=DC))\
                        .then_inc(ot_hi, 1)
                    if not last or j + 1 < G:
                        keep_kv(n + 1, (j + 1) % 2)

            act.sem_inc(q_ok, BASE)
            act.sem_inc(kv_ok, ONE)
            for n, (what, c, half) in enumerate(FOLDS):
                act.wait_ge(fold_ps, n + 1)
                cols = slice(half * HC, (half + 1) * HC)
                if what != "k_row":
                    w = 0 if what == "q" else 1
                    nc.scalar.copy(mqk[0][:, w, c, cols], banks[n % 8][:, :]).then_inc(fold_hi, 1)
                if n == NK:
                    act.wait_ge(late_loaded, 16 * NLATE)
                    nc.scalar.copy(vo[0][:], vo32[:]).then_inc(w_hi, 1)
                    keep_kt(0, 0)
            keep_kt(1, 1)
            act.wait_ge(fold_lo, len(FOLDS) + 1)
            act.wait_ge(clear, 2)
            for t in range(T):
                act.wait_ge(q_ps, t + 1)
                nc.scalar.activation(qp[:, t, 0:2 * P], b_p[t % 2][:, 0:2 * P], ACT.Relu,
                                     bias=q_bias[:, t:t + 1]).then_inc(q_ok, 1)
            keep_kv(0, 0)
            act.wait_ge(kt_loaded, 16)
            with act.Fori(0, NG - 1) as it:
                group(it, False)
            group(NG - 1, True)

        @block.vector
        def _(dve):
            def kt_rest(n, s):
                dve.wait_ge(kt_hi, n + 1)
                nc.vector.tensor_tensor(kt[1][:, s], kt32[:, :, bass.ds(n, 1), :].rearrange("p c b t -> p c (b t)"),
                                        kt[0][:, s].bitcast(F32), ALU.subtract).then_inc(kt_lo, 1)

            def keep_keys(n, s):
                dve.wait_ge(kv_ps, BASE + n - 1)
                halves = [(half, kp[:, s, half * HC:(half + 1) * HC]) for half in range(2)]
                for half, out in halves:
                    dve.wait_ge(k_ps, 2 * n + half + 1)
                    nc.vector.tensor_tensor(out, b_k[half][:, :], k_bias[:, half * HC:(half + 1) * HC], ALU.add)\
                        .then_inc(k_sum, 1)
                dve.wait_ge(v_ps, n + 1)
                nc.vector.tensor_tensor(va[:, s, :, 0:HD], b_v[:, 0:D].rearrange("p (h d) -> p h d", h=H),
                                        v_bias[:].rearrange("p (h d) -> p h d", h=H), ALU.add).then_inc(v_ok, 1)
                for half, out in halves:
                    dve.wait_ge(k_sum, BASE + 2 * n + half + 1)
                    nc.vector.tensor_scalar(out, out, 0.0, mask[:, bass.ds(n, 1)], ALU.max, ALU.mult)\
                        .then_inc(k_ok, 1)

            def group(it, last):
                chain = Chain(dve, chain_s, it, 2 * G)
                for j in range(G):
                    n, s = it * G + j, j % 2
                    if j == T_TURN and not last:
                        norm.vector_lo(dve, it + 1)
                    if not last or j + 2 < G:
                        kt_rest(n + 2, s)
                    if not last or j + 1 < G:
                        keep_keys(n + 1, 1 - s)
                    dve.wait_ge(n_ps, BASE + n + 1)
                    src = b_qkv[:, 0:H * VW].rearrange("p (h n) -> p h n", h=H)
                    chain.done(nc.vector.tensor_scalar(rden[:, s, :], src[:, :, HD], 1e-8, None, ALU.add))
                    chain.done(nc.vector.reciprocal(rden[:, s, :], rden[:, s, :]))
                    dve.wait_ge(ot_ps, BASE + n - 1)
                    nc.vector.tensor_tensor(o[:, s, :].rearrange("p (h d) -> p h d", h=H), src[:, :, 0:HD],
                                            rden[:, s, :].unsqueeze(2).to_broadcast([P, H, HD]), ALU.mult)\
                        .then_inc(n_ok, 1)
                    if j == T_STATS:
                        if last:
                            dve.wait_ge(x_ok, ONE + G)
                        norm.vector_stats(dve, it + 1)
                    if j == T_APPLY:
                        norm.vector_apply(dve, it + 1)
                    if j > T_APPLY and last:
                        dve.wait_ge(norm.s_tr, DC * norm.done(NG + j - T_TURN))
                        norm.vector_apply(dve, NG + j - T_APPLY)
                    dve.wait_ge(ot_hi, n + 1)
                    nc.vector.tensor_tensor(oT[1][:, s, :, :], b_ot.rearrange("p (c t) -> p c t", c=DC),
                                            oT[0][:, s, :, :].bitcast(F32), ALU.subtract).then_inc(ot_lo, 1)
                    if j == 0:
                        dve.wait_ge(xb_ok, it + 1)
                    dve.wait_ge(o_ps, BASE + n + 1)
                    nc.vector.tensor_tensor(x[:, n, :], b_o, x[:, n, :], ALU.add).then_inc(x_ok, 1)
                    if j in (T_APPLY, T_TURN) and last:
                        dve.wait_ge(x_ok, ONE + (j + 1) * G)
                        norm.vector_stats(dve, NG + j)
                chain.close()

            dve.sem_inc(k_sum, BASE)
            for event in (v_ok, n_ok, ot_lo, x_ok):
                dve.sem_inc(event, ONE)
            for n, (what, c, half) in enumerate(FOLDS):
                cols = slice(half * HC, (half + 1) * HC)
                if what == "k_row":
                    dve.wait_ge(fold_ps, n + 1)
                    nc.vector.tensor_copy(k_bias[:, cols], banks[n][:, :]).then_inc(fold_lo, 1)
                else:
                    w = 0 if what == "q" else 1
                    dve.wait_ge(fold_hi, n + 1 if w else n - 1)
                    nc.vector.tensor_tensor(mqk[1][:, w, c, cols], banks[n % 8][:, :],
                                            mqk[0][:, w, c, cols].bitcast(F32), ALU.subtract).then_inc(fold_lo, 1)
                if n == NK:
                    dve.wait_ge(w_hi, 1)
                    nc.vector.tensor_tensor(vo[1][:], vo32[:], vo[0][:].bitcast(F32), ALU.subtract).then_inc(w_lo, 1)
                    kt_rest(0, 0)
            dve.wait_ge(fold_ps, len(FOLDS) + 1)
            nc.vector.tensor_copy(q_bias[:], b_kv[:, 0:T]).then_inc(fold_lo, 1)
            kt_rest(1, 1)
            dve.wait_ge(clear, 2)
            keep_keys(0, 0)
            with dve.Fori(0, NG - 1) as it:
                group(it, False)
            group(NG - 1, True)


def stage_expert_mix(pr):
    nc, io, x, banks = pr.nc, pr.io, pr.x, pr.banks
    E, H, K = 32, 64, 16
    RG = P // E
    HQ = H // RG
    WC = HQ * D
    MC = 512
    NMIX = 2 * WC // MC
    NP = NB // 2
    BIG = 3e38
    w = pr.em_w
    b_m = banks[2:8]
    with ExitStack() as ctx:
        sb = lambda n, shape, dt=F32: ctx.enter_context(nc.sbuf_tensor(f"em_{n}", shape, dt))
        sem = lambda n: pr.sem(f"em_{n}")
        norm = pr.norm
        norm.enter_stage(5, 4, banks[0:2])
        simT = sb("simT", [E, D])
        simT2 = sb("simT2", [E, D])
        sim_len = sb("sim_len", [E, 1])
        sim = sb("sim", [P, DC, E])
        gates = sb("gates", [NB, E])
        before = sb("before", [NB, E, E])
        row_group = sb("row_group", [P, RG])
        xT, rep = pr.em_xT, pr.em_rep
        rep2 = sb("rep2", [P, DC, NB])
        ones = sb("ones", [P, NB])
        repn = sb("repn", [NB, 1])
        logit = sb("logit", [NB, E])
        gated = sb("gated", [NB, E])
        act_mask = sb("act_mask", [NB, E])
        small = sb("small", [NB, 8])
        more = sb("more", [NB, E, E])
        tied = sb("tied", [NB, E, E])
        rank = sb("rank", [NB, E])
        sig = sb("sig", [NB, E])
        route = sb("route", [NB, 2, RG, E])
        routeT = sb("routeT", [P, 2, RG, NB])
        mixed = sb("mixed", [P, 2, NP, D])
        wvT = sb("wvT", [P, DC, NP, P])
        hT = sb("hT", [P, NP, P])
        scratch = nc.dram_tensor("em_scratch", (RG, NB, 2, WC), F32, kind="Internal").ap()

        loaded, xT_ok, rep_ok = sem("loaded"), sem("xT_kept"), sem("rep_ready")
        const_ok, aff_ps, rn_in, rn_ok = sem("consts"), sem("affinity_in_psum"), sem("norms_in"), sem("rnorms_ready")
        simn_ok, simT_ps, sim_ok = sem("sim_of_length_one"), sem("sim_in_psum"), sem("sim_ready")
        exp_in, exp_ok, r_ok, rT_ps, rT_ok = (sem("exp_in"), sem("exp_ready"), sem("routing_ready"),
                                              sem("routingT_in_psum"), sem("routingT_ready"))
        mix_ps = sem("mix_in_psum")
        mix_ok = [sem("mix_kept_even"), sem("mix_kept_odd")]
        spilled = [sem("mix_v_in_dram"), sem("mix_o_in_dram")]
        mixed_in = [sem("mix_v_loaded"), sem("mix_o_loaded")]
        wt_ps = sem("wvT_in_psum")
        wt_ok = [sem("wvT_ready_act"), sem("wvT_ready_vec")]
        h_ps, h_ok, o_ps, x_ok = sem("hT_in_psum"), sem("hT_ready"), sem("out_in_psum"), sem("x_updated")
        chain_s, sig_ok, stored = sem("vector_chain"), sem("gate_exps"), sem("stored")
        block = ctx.enter_context(nc.Block())

        def reload(eng, kind, groups):
            eng.wait_ge(spilled[kind], 16 * 2)
            for g in groups:
                for odd in range(2):
                    first = odd * H + g * HQ
                    eng.dma_start(mixed[first:first + HQ, kind],
                                  scratch[g, odd::2, kind].rearrange("b (h c) -> h b c", c=D))\
                        .then_inc(mixed_in[kind], 16)

        @block.sync
        def _(sp):
            sp.dma_start(simT[:], io["em_simT"]).then_inc(loaded, 16)
            sp.dma_start(gates[:], io["em_gates"]).then_inc(loaded, 16)
            sp.dma_start(before[:], io["before32"]).then_inc(loaded, 16)
            sp.dma_start(row_group[:], io["em_row_group"]).then_inc(loaded, 16)
            for n in range(4):
                for parity in range(2):
                    sp.wait_ge(mix_ok[parity], (n + 1) * NMIX // 8)
                kind, half = divmod(n, 2)
                sp.dma_start(scratch[:, :, kind, half * WC // 2:(half + 1) * WC // 2],
                             w[0:RG * NB, kind, half * WC // 2:(half + 1) * WC // 2]).then_inc(spilled[kind], 16)
                if half:
                    reload(sp, kind, range(RG))
            for b in range(NP):
                sp.wait_ge(x_ok, b + 1)
                sp.dma_start(io["out"][2 * b:2 * b + 2].rearrange("b t d -> t b d"),
                             x[:, 2 * b:2 * b + 2, :]).then_inc(stored, 16)
            sp.wait_ge(stored, 16 * NP)

        @block.gpsimd
        def _(pool):
            nc.gpsimd.memset(ones[:], 1.0).then_inc(const_ok, 1)
            norm.pool_rstd(pool, 3)
            pool.wait_ge(rn_in, 1)
            nc.gpsimd.tensor_tensor(sim_len[:], sim_len[:], pr.minus_half[0:E, 0:1], ALU.pow).then_inc(rn_ok, 1)
            pool.wait_ge(rn_in, 2)
            nc.gpsimd.tensor_tensor(repn[:], repn[:], pr.minus_half[0:NB, 0:1], ALU.pow).then_inc(rn_ok, 1)

        @block.tensor
        def _(pe):
            norm.tensor_transpose(pe, 2)
            pe.wait_ge(xT_ok, DC)
            norm.tensor_transpose(pe, 3)
            pe.wait_ge(simn_ok, 1)
            for c in range(DC):
                last = nc.tensor.transpose(banks[5][:, c * E:(c + 1) * E], simT[:, c * P:(c + 1) * P],
                                           pr.ident[0:E, 0:E])
            last.then_inc(simT_ps, 1)
            pe.wait_ge(const_ok, 1)
            pe.wait_ge(sim_ok, 1)
            pe.wait_ge(rep_ok, 1)
            aff, r2 = banks[2][0:NB, 0:E], banks[4][0:NB, 0:1]
            for c in range(DC):
                nc.tensor.matmul(r2, rep2[:, c, :], ones[:, 0:1], start=(c == 0), stop=(c == DC - 1))
            for c in range(DC):
                last = nc.tensor.matmul(aff, rep[:, c, :], sim[:, c, :], start=(c == 0), stop=(c == DC - 1))
            last.then_inc(aff_ps, 1)
            pe.wait_ge(r_ok, 1)
            for kind in range(2):
                last = nc.tensor.transpose(banks[1][:, kind * NB:(kind + 1) * NB],
                                           route[:, kind].rearrange("p r e -> p (r e)"), pr.ident[0:NB, 0:NB])
            last.then_inc(rT_ps, 1)
            pe.wait_ge(pr.em_loaded, 16)
            pe.wait_ge(rT_ok, 1)
            for n in range(NMIX):
                kind, m = divmod(n, NMIX // 2)
                if n >= len(b_m):
                    before_n = n - len(b_m)
                    pe.wait_ge(mix_ok[before_n % 2], before_n // 2 + 1)
                nc.tensor.matmul(b_m[n % len(b_m)][0:RG * NB, :], routeT[:, kind].rearrange("p g b -> p (g b)"),
                                 w[:, kind, m * MC:(m + 1) * MC], start=True, stop=True).then_inc(mix_ps, 1)
            pe.wait_ge(mixed_in[0], 16 * 2 * RG)
            for parity in range(2):
                pe.wait_ge(mix_ok[parity], NMIX // 2)
            for n in range(4):
                c, half = n % 2, n // 2
                for b in range(4):
                    last = nc.tensor.transpose(banks[4 + n][:, b * P:(b + 1) * P],
                                               mixed[:, 0, 4 * half + b, c * P:(c + 1) * P], pr.ident[:])
                last.then_inc(wt_ps, 1)

            def hidden(b):
                if b >= 4:
                    pe.wait_ge(h_ok, b - 3)
                for c in range(DC):
                    last = nc.tensor.matmul(banks[b % 4][:, 0:2 * P], wvT[:, c, b, :],
                                            xT[:, c, 2 * b:2 * b + 2, :].rearrange("p b t -> p (b t)"),
                                            start=(c == 0), stop=(c == DC - 1))
                last.then_inc(h_ps, 1)

            def outputs(b):
                pe.wait_ge(h_ok, b + 1)
                if b >= 2:
                    pe.wait_ge(x_ok, b - 1)
                for odd in range(2):
                    rows = slice(H * odd, H * odd + H)
                    last = nc.tensor.matmul(banks[4 + 2 * (b % 2) + odd][:, 0:D], hT[rows, b, :],
                                            mixed[rows, 1, b, :], start=True, stop=True)
                last.then_inc(o_ps, 1)

            pe.wait_ge(xT_ok, 2 * DC)
            for part in wt_ok:
                pe.wait_ge(part, 2)
            for b in range(NP):
                hidden(b)
            pe.wait_ge(mixed_in[1], 16 * 2 * RG)
            for b in range(NP):
                outputs(b)

        @block.scalar
        def _(act):
            for g in (2, 3):
                keep_mix_input(pr, act, g, g, xT_ok)
            act.wait_ge(simT_ps, 1)
            nc.scalar.copy(sim[:], banks[5][:, 0:DC * E].rearrange("p (c e) -> p c e", c=DC)).then_inc(sim_ok, 1)
            act.wait_ge(loaded, 64)
            nc.scalar.activation(sig[:], gates[:], ACT.Exp, scale=-1.0).then_inc(sig_ok, 1)
            act.wait_ge(exp_in, 1)
            nc.scalar.activation(gated[:], gated[:], ACT.Exp, bias=small[:, 2:3],
                                 accum_out=small[:, 3:4]).then_inc(exp_ok, 1)
            for n in range(0, NMIX, 2):
                kind, m = divmod(n, NMIX // 2)
                act.wait_ge(mix_ps, n + 1)
                nc.scalar.copy(w[0:RG * NB, kind, m * MC:(m + 1) * MC], b_m[n % len(b_m)][0:RG * NB, :])\
                    .then_inc(mix_ok[0], 1)
            for n in (0, 2):
                act.wait_ge(wt_ps, n + 1)
                nc.scalar.copy(wvT[:, 0, 2 * n:2 * n + 4, :], banks[4 + n][:, :]
                               .rearrange("p (b h) -> p b h", b=4)).then_inc(wt_ok[0], 1)
            for b in range(NP):
                act.wait_ge(h_ps, b + 1)
                nc.scalar.copy(hT[0:H, b, :], banks[b % 4][0:H, 0:P])
                nc.scalar.copy(hT[H:P, b, :], banks[b % 4][H:P, P:2 * P]).then_inc(h_ok, 1)

        @block.vector
        def _(dve):
            norm.vector_stats(dve, 3)
            dve.wait_ge(norm.s_tr, DC * norm.done(2))
            norm.vector_apply(dve, 3)
            dve.wait_ge(loaded, 64)
            chain = Chain(dve, chain_s, 0, 21)
            chain.done(nc.vector.tensor_tensor(simT2[:], simT[:], simT[:], ALU.mult))
            nc.vector.tensor_reduce(sim_len[:], simT2[:], AX, ALU.add).then_inc(rn_in, 1)
            dve.wait_ge(rn_ok, 1)
            nc.vector.tensor_scalar(simT[:], simT[:], sim_len[:, 0:1], None, ALU.mult).then_inc(simn_ok, 1)
            dve.wait_ge(sig_ok, 1)
            chain.done(nc.vector.tensor_scalar(sig[:], sig[:], 1.0, None, ALU.add))
            chain.done(nc.vector.reciprocal(sig[:], sig[:]))
            dve.wait_ge(xT_ok, 2 * DC)
            chain.done(nc.vector.tensor_scalar(rep[:], rep[:], 1.0 / P, None, ALU.mult))
            nc.vector.tensor_tensor(rep2[:], rep[:], rep[:], ALU.mult).then_inc(rep_ok, 1)
            dve.wait_ge(aff_ps, 1)
            nc.vector.tensor_copy(repn[:], banks[4][0:NB, 0:1]).then_inc(rn_in, 1)
            dve.wait_ge(rn_ok, 2)
            chain.done(nc.vector.tensor_scalar(logit[:], banks[2][0:NB, 0:E], repn[:, 0:1], None, ALU.mult))
            chain.done(nc.vector.tensor_tensor(logit[:], logit[:], sig[:], ALU.subtract))
            chain.done(nc.vector.tensor_scalar(gated[:], logit[:], 0.0, None, ALU.max))
            chain.done(nc.vector.tensor_scalar(act_mask[:], gated[:], 0.0, None, ALU.is_gt))
            chain.done(nc.vector.tensor_reduce(small[:, 0:1], act_mask[:], AX, ALU.add))
            chain.done(nc.vector.tensor_scalar(small[:, 1:2], small[:, 0:1], 0.0, None, ALU.is_equal))
            ahead = logit[:].unsqueeze(1).to_broadcast([NB, E, E])
            self_ = logit[:].unsqueeze(2).to_broadcast([NB, E, E])
            nc.vector.tensor_tensor(more[:], ahead, self_, ALU.is_gt)
            chain.done(nc.vector.tensor_tensor(tied[:], ahead, self_, ALU.is_equal))
            chain.done(nc.vector.tensor_tensor(tied[:], tied[:], before[:], ALU.mult))
            chain.done(nc.vector.tensor_tensor(more[:], more[:], tied[:], ALU.add))
            chain.done(nc.vector.tensor_reduce(rank[:], more[:], AX, ALU.add))
            chain.done(nc.vector.tensor_scalar(rank[:], rank[:], K - 0.5, small[:, 1:2], ALU.is_lt, ALU.mult))
            chain.done(nc.vector.tensor_tensor(act_mask[:], act_mask[:], rank[:], ALU.max))
            chain.done(nc.vector.tensor_tensor(gated[:], gated[:], act_mask[:], ALU.mult))
            chain.done(nc.vector.tensor_scalar(rank[:], act_mask[:], 1.0, BIG, ALU.subtract, ALU.mult))
            chain.done(nc.vector.tensor_tensor(gated[:], gated[:], rank[:], ALU.add))
            chain.done(nc.vector.tensor_reduce(small[:, 1:2], gated[:], AX, ALU.max))
            nc.vector.tensor_scalar(small[:, 2:3], small[:, 1:2], -1.0, None, ALU.mult).then_inc(exp_in, 1)
            dve.wait_ge(exp_ok, 1)
            nc.vector.reciprocal(small[:, 4:5], small[:, 3:4]).then_inc(chain_s, 1)
            dve.wait_ge(chain_s, chain.n + 1)
            nc.vector.tensor_scalar(route[:, 1], gated[:].unsqueeze(1).to_broadcast([NB, RG, E]), small[:, 4:5],
                                    None, ALU.mult).then_inc(chain_s, 1)
            dve.wait_ge(chain_s, chain.n + 2)
            nc.vector.tensor_tensor(route[:, 0], route[:, 1], act_mask[:].unsqueeze(1).to_broadcast([NB, RG, E]),
                                    ALU.mult).then_inc(r_ok, 1)
            dve.wait_ge(rT_ps, 1)
            for kind in range(2):
                last = nc.vector.tensor_tensor(
                    routeT[:, kind], banks[1][:, kind * NB:(kind + 1) * NB].unsqueeze(1).to_broadcast([P, RG, NB]),
                    row_group[:].unsqueeze(2).to_broadcast([P, RG, NB]), ALU.mult)
            last.then_inc(rT_ok, 1)
            for n in range(1, NMIX, 2):
                kind, m = divmod(n, NMIX // 2)
                dve.wait_ge(mix_ps, n + 1)
                nc.vector.tensor_copy(w[0:RG * NB, kind, m * MC:(m + 1) * MC], b_m[n % len(b_m)][0:RG * NB, :])\
                    .then_inc(mix_ok[1], 1)
            for n in (1, 3):
                dve.wait_ge(wt_ps, n + 1)
                nc.vector.tensor_copy(wvT[:, 1, 2 * (n - 1):2 * (n - 1) + 4, :], banks[4 + n][:, :]
                                      .rearrange("p (b h) -> p b h", b=4)).then_inc(wt_ok[1], 1)
            for b in range(NP):
                dve.wait_ge(o_ps, b + 1)
                for odd in range(2):
                    last = nc.vector.tensor_tensor(x[:, 2 * b + odd, :], banks[4 + 2 * (b % 2) + odd][:, 0:D],
                                                   x[:, 2 * b + odd, :], ALU.add)
                last.then_inc(x_ok, 1)


def stage_linear_attention_and_expert_mix(pr):
    nc = pr.nc
    with ExitStack() as ctx:
        pr.em_w = ctx.enter_context(nc.sbuf_tensor("em_w", [P, 2, 4096], F32))
        pr.em_xT = ctx.enter_context(nc.sbuf_tensor("em_xT", [P, DC, NB, P], F32))
        pr.em_rep = ctx.enter_context(nc.sbuf_tensor("em_rep", [P, DC, NB], F32))
        stage_linear_attention(pr)
        pr.release_semaphores()
        stage_expert_mix(pr)


def store_output(pr):
    nc, io = pr.nc, pr.io
    stored = pr.sem("stored")
    with nc.Block() as block:
        @block.sync
        def _(sp):
            sp.dma_start(io["out"].rearrange("b t d -> t b d"), pr.x[:]).then_inc(stored, 16)
            sp.wait_ge(stored, 16)


def build(nc, io, stages):
    pr = Program(nc, io)
    with ExitStack() as ctx:
        pr.x = ctx.enter_context(nc.sbuf_tensor("x", [P, NB, D], F32))
        pr.ident = ctx.enter_context(nc.sbuf_tensor("ident", [P, P], F32))
        pr.wait_slot = ctx.enter_context(nc.sbuf_tensor("wait_slot", [1, 1], F32))
        pr.minus_half = ctx.enter_context(nc.sbuf_tensor("minus_half", [P, G], F32))
        pr.banks = [ctx.enter_context(nc.psum_tensor(f"bank{n}", [P, 512], F32)) for n in range(8)]
        pr.norm = Norm(pr, ctx)
        pr.h_or_fold = ctx.enter_context(nc.sbuf_tensor("h_or_fold", [P, 2 * DC * D + 2 * 512], F32))
        pr.x_loaded = [pr.sem(f"x_loaded{t}") for t in range(NG)]
        pr.const_ok = pr.sem("consts_ready")
        pr.conv_loaded = nc.alloc_semaphore(name="conv_consts_loaded")
        pr.le_loaded = nc.alloc_semaphore(name="le_weights_loaded")
        pr.le_hi = nc.alloc_semaphore(name="le_weights_hi")
        pr.fold_loaded = nc.alloc_semaphore(name="li_fold_loaded")
        pr.em_loaded = nc.alloc_semaphore(name="em_w_loaded")
        for stage in STAGES[:stages]:
            stage(pr)
            if stage is not STAGES[-1]:
                pr.release_semaphores()
        if stages < len(STAGES):
            store_output(pr)


STAGES = [first_layer_and_wide_attention, stage_linear_attention_and_expert_mix]


def kernel(**inputs):
    import numpy as np
    import concourse.bacc as bacc
    from concourse.bass_utils import run_bass_kernel_spmd

    a = {n: np.asarray(v) for n, v in inputs.items()}

    def chunks(w):
        return w.reshape(DC, P, -1).transpose(1, 0, 2)

    r = {}
    r["x"] = a["x"]
    r["ident"] = np.eye(P, dtype=np.float32)
    odd = (np.arange(P) // 16) % 2
    r["parity"] = np.stack([1 - odd, odd], axis=1).astype(np.float32)
    qkvo = "qkvo"
    r["l0_w"] = np.stack([chunks(a[f"L0_attn_W{n}"].T) for n in qkvo], axis=1)
    r["l0_a"] = np.stack([a[f"L0_attn_A{n}"].T for n in qkvo], axis=1)
    r["l0_b"] = np.stack([a[f"L0_attn_B{n}"] for n in qkvo], axis=1)
    r["l0_qk_bias"] = np.stack([a["L0_attn_bq"].reshape(DC, P).T, a["L0_attn_bk"].reshape(DC, P).T], axis=1)
    r["l0_v_bias"] = a["L0_attn_bv"].reshape(DC, P).T
    r["l0_o_bias"] = np.broadcast_to(a["L0_attn_bo"], (P, D))

    r["ctx_rev"] = a["ctx_2048"].transpose(2, 0, 1).reshape(DC, P, NB, P)[:, ::-1].transpose(1, 0, 2, 3)
    kpad = np.concatenate([np.zeros((16, P - 1), np.float32), a["L0_xattn_ssm_kernel"]], axis=1)
    r["toeplitz"] = np.lib.stride_tricks.sliding_window_view(kpad, 2 * P, axis=1).transpose(1, 0, 2)
    r["conv_d"] = np.broadcast_to(a["L0_xattn_D"], (P, 16))
    r["anti"] = np.eye(P, dtype=np.float32)[::-1]
    r["le_w"] = np.concatenate([chunks(a["L0_ffn_W"].T), chunks(a["L0_ffn_A"].reshape(P, D).T),
                                chunks(a["L0_ffn_gate_w"].T)], axis=2)
    r["le_u"] = a["L0_ffn_B"].transpose(0, 2, 1).reshape(P, D)
    r["le_order"] = np.broadcast_to(np.arange(8, 0, -1, dtype=np.float32), (P, 8))
    wide = [chunks(a[f"L1_attn_W_{n}"].reshape(-1, D).T).reshape(P, -1) for n in "QKV"]
    wide.append(a["L1_attn_W_O"].T.reshape(16, P, D).transpose(1, 0, 2).reshape(P, -1))
    r["wide_w"] = np.stack(wide)
    r["causal"] = np.triu(np.full((P, P), -1e30, np.float32), 1)

    reverse = lambda t: t.reshape(DC, P, -1)[:, ::-1].transpose(1, 0, 2)
    wk = a["L1_xattn_Wk"].reshape(D, DC, P)[:, :, ::-1].reshape(D, D)
    wqk = np.stack([chunks(a["L1_xattn_Wq"]), chunks(wk)], axis=1)
    wf = np.zeros((8, 16, 2, 8, 64), np.float32)
    for n, name in enumerate("qk"):
        for h in range(8):
            wf[h, :, n, h] = a[f"L1_xattn_W{name}f"].T
    r["li_fold"] = np.concatenate([wqk.reshape(P, -1), wf.reshape(P, -1)], axis=1)
    r["li_bqk"] = np.stack([a[f"L1_xattn_b{n}"].reshape(DC, P).T for n in "qk"], axis=1)
    r["li_vo"] = np.stack([reverse(a["L1_xattn_Wv"].T), chunks(a["L1_xattn_Wo"].T)], axis=1)
    r["li_v_bias"] = np.broadcast_to(a["L1_xattn_bv"], (P, D))
    r["li_o_bias"] = np.broadcast_to(a["L1_xattn_bo"], (P, D))
    r["li_mask"] = a["mask_BxS2_ff1"].T
    by_quarter = lambda w: w.reshape(32, 4, -1).transpose(1, 0, 2).reshape(P, -1)
    r["em_w"] = np.stack([by_quarter(a["L1_ffn_w_v"]), by_quarter(a["L1_ffn_o_weights"])], axis=1)
    r["em_row_group"] = np.repeat(np.eye(4, dtype=np.float32), 32, axis=0)
    r["em_simT"] = a["L1_ffn_sim_matrix"].T
    r["em_gates"] = np.broadcast_to(a["L1_ffn_gates"], (NB, 32))
    r["before32"] = np.broadcast_to(np.tril(np.ones((32, 32), np.float32), -1), (NB, 32, 32))

    nc = bacc.Bacc("TRN2", target_bir_lowering=False, num_devices=1)
    arrays, io = {}, {}
    for name, v in r.items():
        v = np.ascontiguousarray(v)
        arrays[f"in_{name}"] = v
        io[name] = nc.dram_tensor(f"in_{name}", v.shape, mybir.dt.from_np(v.dtype), kind="ExternalInput").ap()
    io["out"] = nc.dram_tensor("out_x", (NB, P, D), F32, kind="ExternalOutput").ap()
    build(nc, io, len(STAGES))
    got = run_bass_kernel_spmd(nc, [arrays], core_ids=[0])
    return got.results[0]["out_x"]
```
